# Optimizing a Trainium2 kernel written in Bass

```python
import numpy as np
import jax
import jax.numpy as jnp

def _softmax(x, axis=-1):
    return jax.nn.softmax(x, axis=axis)

def _gelu(x):
    return jax.nn.gelu(x, approximate=True)

def _silu(x):
    return jax.nn.silu(x)

def _sigmoid(x):
    return jax.nn.sigmoid(x)

def _layernorm(x, axis=-1, eps=1e-05):
    m = jnp.mean(x, axis=axis, keepdims=True)
    v = jnp.var(x, axis=axis, keepdims=True)
    return (x - m) / jnp.sqrt(v + eps)

def _scatter_add(tgt, idx, src, axis=0):
    return tgt.at[idx].add(src)

def _segment_sum(src, seg, n):
    return jax.ops.segment_sum(src, seg, n)
kernel_name = 'mk_gps_d1_gnn_r16_01db31'

def setup_inputs(seed: int=0):
    np.random.seed(seed)
    _w = jnp.asarray

    def _rec_inputs():
        import jax
        import jax.numpy as jnp
        _gk = jax.random.key(seed)
        x = -0.0003713 + 1 * jax.random.normal(jax.random.fold_in(_gk, 1), (3125, 256), jnp.float32)
        _s = jax.random.randint(jax.random.fold_in(_gk, 2), (25000,), 0, 3125, jnp.int32)
        _d = jax.random.randint(jax.random.fold_in(_gk, 3), (25000,), 0, 3125, jnp.int32)
        _loop = jnp.arange(3125, dtype=jnp.int32)
        src = jnp.concatenate([_s, _d, _loop])
        dst = jnp.concatenate([_d, _s, _loop])
        _o = jnp.argsort(dst, stable=True)
        src = src[_o]
        dst = dst[_o]
        edge_weight = jax.random.uniform(jax.random.fold_in(_gk, 12), (53125,), jnp.float32, 0.0, 0.999999)
        return (x, src, dst, edge_weight)
    x, src, dst, edge_weight = _rec_inputs()

    def _L0_gnn_setup():
        import jax, jax.numpy as jnp
        import numpy as np
        N_NODES = 3125
        key = jax.random.key(seed)
        k1, k2, k3, k4, k5 = jax.random.split(key, 5)
        x = jax.random.normal(k1, (N_NODES, 256), dtype=jnp.float32)
        edge_row = jax.random.randint(k2, (50000,), 0, N_NODES, dtype=jnp.int32)
        edge_col = jax.random.randint(k3, (50000,), 0, N_NODES, dtype=jnp.int32)
        edge_val = jax.random.uniform(k4, (50000,), dtype=jnp.float32)
        W = jax.random.normal(k5, (256, 256), dtype=jnp.float32) * 0.0625
        b = jnp.zeros((256,), dtype=jnp.float32)
        return {'x': x, 'edge_row': edge_row, 'edge_col': edge_col, 'edge_val': edge_val, 'W': W, 'b': b}
    _L0_gnn_all = _L0_gnn_setup()
    _L0_gnn_in = {k: v for k, v in _L0_gnn_all.items() if k in ('W', 'b')}
    del _L0_gnn_all

    def _L0_mix_setup():
        import jax, jax.numpy as jnp
        import numpy as np
        NHEAD = 8
        ATT_EPS = 1e-06
        LN_EPS = 1e-05

        def _layernorm(x, g, b):
            mu = jnp.mean(x, axis=-1, keepdims=True)
            var = jnp.mean(jnp.square(x - mu), axis=-1, keepdims=True)
            return (x - mu) * jax.lax.rsqrt(var + LN_EPS) * g + b
        key = jax.random.key(seed)
        ks = jax.random.split(key, 7)
        N, L, C = (4, 1024, 256)
        s = 1.0 / np.sqrt(C)
        return {'x': jax.random.normal(ks[0], (N, L, C), jnp.float32), 'Wq': jax.random.normal(ks[1], (C, C), jnp.float32) * s, 'Wk': jax.random.normal(ks[2], (C, C), jnp.float32) * s, 'Wv': jax.random.normal(ks[3], (C, C), jnp.float32) * s, 'Wm': jax.random.normal(ks[4], (C, C), jnp.float32) * s, 'W1': jax.random.normal(ks[5], (2 * C, 2 * C), jnp.float32) * (1.0 / np.sqrt(2 * C)), 'W2': jax.random.normal(ks[6], (2 * C, C), jnp.float32) * (1.0 / np.sqrt(2 * C)), 'g1': jnp.ones((C,), jnp.float32), 'b1': jnp.zeros((C,), jnp.float32), 'g2': jnp.ones((C,), jnp.float32), 'b2': jnp.zeros((C,), jnp.float32)}
    _L0_mix_all = _L0_mix_setup()
    _L0_mix_in = {k: v for k, v in _L0_mix_all.items() if k in ('Wq', 'Wk', 'Wv', 'Wm', 'W1', 'W2', 'g1', 'b1', 'g2', 'b2')}
    del _L0_mix_all

    def _L0_ffn_setup():
        import jax, jax.numpy as jnp
        import numpy as np
        D_MODEL = 256
        N_EXPERTS = 16
        HIDDEN = 512
        SCALE = 0.02
        key = jax.random.key(seed)
        ks = jax.random.split(key, 5)
        x = jax.random.normal(ks[0], (4, 512, D_MODEL), dtype=jnp.float32)
        gate_w = jax.random.normal(ks[1], (D_MODEL, N_EXPERTS), dtype=jnp.float32) * SCALE
        gate_b = jnp.zeros((N_EXPERTS,), dtype=jnp.float32)
        w1 = jax.random.normal(ks[2], (N_EXPERTS, D_MODEL, HIDDEN), dtype=jnp.float32) * SCALE
        w2 = jax.random.normal(ks[3], (N_EXPERTS, D_MODEL, HIDDEN), dtype=jnp.float32) * SCALE
        w3 = jax.random.normal(ks[4], (N_EXPERTS, HIDDEN, D_MODEL), dtype=jnp.float32) * SCALE
        return {'x': x, 'gate_w': gate_w, 'gate_b': gate_b, 'w1': w1, 'w2': w2, 'w3': w3}
    _L0_ffn_all = _L0_ffn_setup()
    _L0_ffn_in = {k: v for k, v in _L0_ffn_all.items() if k in ('gate_w', 'gate_b', 'w1', 'w2', 'w3')}
    del _L0_ffn_all
    return {'x': x, 'src': src, 'dst': dst, 'edge_weight': edge_weight, 'L0_gnn_W': _L0_gnn_in['W'], 'L0_gnn_b': _L0_gnn_in['b'], 'L0_mix_Wq': _L0_mix_in['Wq'], 'L0_mix_Wk': _L0_mix_in['Wk'], 'L0_mix_Wv': _L0_mix_in['Wv'], 'L0_mix_Wm': _L0_mix_in['Wm'], 'L0_mix_W1': _L0_mix_in['W1'], 'L0_mix_W2': _L0_mix_in['W2'], 'L0_mix_g1': _L0_mix_in['g1'], 'L0_mix_b1': _L0_mix_in['b1'], 'L0_mix_g2': _L0_mix_in['g2'], 'L0_mix_b2': _L0_mix_in['b2'], 'L0_ffn_gate_w': _L0_ffn_in['gate_w'], 'L0_ffn_gate_b': _L0_ffn_in['gate_b'], 'L0_ffn_w1': _L0_ffn_in['w1'], 'L0_ffn_w2': _L0_ffn_in['w2'], 'L0_ffn_w3': _L0_ffn_in['w3']}

def reference(x, src, dst, edge_weight, L0_gnn_W, L0_gnn_b, L0_mix_Wq, L0_mix_Wk, L0_mix_Wv, L0_mix_Wm, L0_mix_W1, L0_mix_W2, L0_mix_g1, L0_mix_b1, L0_mix_g2, L0_mix_b2, L0_ffn_gate_w, L0_ffn_gate_b, L0_ffn_w1, L0_ffn_w2, L0_ffn_w3):
    import jax
    import jax.numpy as jnp

    def _L0_gnn_ref(x, edge_row, edge_col, edge_val, W, b):
        import jax, jax.numpy as jnp
        import numpy as np
        N_NODES = 3125
        msgs = edge_val[:, None] * x[edge_col]
        agg = jax.ops.segment_sum(msgs, edge_row, num_segments=N_NODES)
        return jnp.einsum('nf,of->no', agg, W) + b

    def _L0_mix_ref(x, Wq, Wk, Wv, Wm, W1, W2, g1, b1, g2, b2):
        import jax, jax.numpy as jnp
        import numpy as np
        NHEAD = 8
        ATT_EPS = 1e-06
        LN_EPS = 1e-05

        def _layernorm(x, g, b):
            mu = jnp.mean(x, axis=-1, keepdims=True)
            var = jnp.mean(jnp.square(x - mu), axis=-1, keepdims=True)
            return (x - mu) * jax.lax.rsqrt(var + LN_EPS) * g + b
        N, L, C = x.shape
        H = NHEAD
        D = C // H
        q = (x @ Wq).reshape(N, L, H, D)
        k = (x @ Wk).reshape(N, L, H, D)
        v = (x @ Wv).reshape(N, L, H, D)
        Q = jax.nn.elu(q) + 1.0
        K = jax.nn.elu(k) + 1.0
        v = v / L
        KV = jnp.einsum('nshd,nshv->nhdv', K, v)
        Z = 1.0 / (jnp.einsum('nlhd,nhd->nlh', Q, K.sum(axis=1)) + ATT_EPS)
        msg = jnp.einsum('nlhd,nhdv,nlh->nlhv', Q, KV, Z) * L
        msg = msg.reshape(N, L, C) @ Wm
        msg = _layernorm(msg, g1, b1)
        h = jnp.concatenate([x, msg], axis=-1) @ W1
        h = jax.nn.relu(h) @ W2
        msg = _layernorm(h, g2, b2)
        return x + msg

    def _L0_ffn_ref(x, gate_w, gate_b, w1, w2, w3):
        import jax, jax.numpy as jnp
        import numpy as np
        D_MODEL = 256
        N_EXPERTS = 16
        HIDDEN = 512
        SCALE = 0.02
        n_experts = w1.shape[0]
        logits = jnp.einsum('bsd,de->bse', x, gate_w) + gate_b
        probs = jax.nn.softmax(logits, axis=-1)
        top_probs, top_idx = jax.lax.top_k(probs, 2)
        top_probs = top_probs / jnp.sum(top_probs, axis=-1, keepdims=True)
        dispatch = jnp.sum(jax.nn.one_hot(top_idx, n_experts, dtype=x.dtype) * top_probs[..., None], axis=-2)
        h1 = jnp.einsum('bsd,edh->bseh', x, w1)
        h2 = jnp.einsum('bsd,edh->bseh', x, w2)
        hidden = jax.nn.silu(h1) * h2
        expert_out = jnp.einsum('bseh,eho->bseo', hidden, w3)
        return jnp.einsum('bseo,bse->bso', expert_out, dispatch)
    xn = _layernorm(x, axis=-1)
    x = x + _L0_gnn_ref(xn, src, dst, edge_weight, L0_gnn_W, L0_gnn_b) + _L0_mix_ref(xn[None], L0_mix_Wq, L0_mix_Wk, L0_mix_Wv, L0_mix_Wm, L0_mix_W1, L0_mix_W2, L0_mix_g1, L0_mix_b1, L0_mix_g2, L0_mix_b2)[0]
    x = x + _L0_ffn_ref(_layernorm(x, axis=-1)[None], L0_ffn_gate_w, L0_ffn_gate_b, L0_ffn_w1, L0_ffn_w2, L0_ffn_w3)[0]
    return x

_drawn_inputs = setup_inputs


def setup_inputs(seed=0):
    import zlib

    import numpy as np

    out = dict(_drawn_inputs(seed))
    spreads = {'L0_gnn_b': (0.0, 0.1),
     'L0_mix_g1': (1.0, 0.2),
     'L0_mix_b1': (0.0, 0.382),
     'L0_mix_g2': (1.0, 0.2),
     'L0_mix_b2': (0.0, 0.1),
     'L0_ffn_gate_b': (0.0, 0.8)}
    factors = {'L0_ffn_gate_w': 8.0, 'L0_ffn_w1': 8.0, 'L0_ffn_w2': 8.0, 'L0_ffn_w3': 8.0}
    for name, (base, spread) in spreads.items():
        noise = np.random.default_rng([zlib.crc32(name.encode()), seed]).standard_normal(out[name].shape)
        drawn = base * np.exp(spread * noise) if base else spread * noise
        out[name] = jnp.asarray(drawn.astype(out[name].dtype))
    for name, factor in factors.items():
        out[name] = (out[name] * factor).astype(out[name].dtype)
    return out
```

```python
from contextlib import ExitStack

import concourse.bass as bass
from concourse import mybir

ALU = mybir.AluOpType
ACT = mybir.ActivationFunctionType
F32 = mybir.dt.float32
BF16 = mybir.dt.bfloat16
I32 = mybir.dt.int32
AX = mybir.AxisListType.X
DVE = (mybir.EngineType.DVE,)
PE = (mybir.EngineType.PE,)
SP = (mybir.EngineType.SP,)

P = 128
U = 5
LN_EPS = 1e-5
ATT_EPS = 1e-6
HEADS = 8


def gps_layer(nc, x, src, dst, edge_weight, gnn_W, gnn_b, Wq, Wk, Wv, Wm, W1, W2, g1, b1, g2, b2,
              gate_w, gate_b, ew1, ew2, ew3, out):
    N, C = x.shape
    KC = C // P
    NT = -(-N // P)
    LAST = N - (NT - 1) * P
    TURNS = NT // U
    E = src.shape[0]
    GE = 25
    EP = N // GE
    NG = E // (EP * GE)
    GT = -(-(EP * GE) // P)
    BINS = NT
    STEPS = GT + BINS - 1
    SU = 7
    PIECES = 7
    HID = W1.shape[1]
    HC = HID // P
    NE = gate_w.shape[1]
    EH = ew1.shape[2]
    EHC = EH // P
    ETILES = (2 * N + NE * (P - 1)) // P
    HD = C // HEADS
    HPC = P // HD
    DT = 3
    assert NT == U * TURNS and EP * GE * NG == E and STEPS % SU == 0 and ETILES % 2 == 0
    assert NG % 2 == 1 and (NT - 1) % DT == 0

    xn_rows = nc.dram_tensor("xn_rows", [N, C], F32).ap()
    slot_rows = nc.dram_tensor("slot_rows", [ETILES * P, C], F32).ap()
    expert_rows = nc.dram_tensor("expert_rows", [ETILES * P, C], F32).ap()

    with ExitStack() as ctx:
        def sb(name, shape, dt=F32):
            return ctx.enter_context(nc.sbuf_tensor(name, shape, dt))

        def sem(name):
            return ctx.enter_context(nc.semaphore(name))

        xn = sb("xn", [P, NT, C])
        xnT = sb("xnT", [P, KC, NT * P])
        agg = sb("agg", [P, NT, C])
        arena = sb("arena", [P, 2 * NT * C])
        rows = [arena[:, h * NT * C:h * NT * C + GT * C].rearrange("p (t c) -> p t c", c=C) for h in range(2)]
        ident = sb("ident", [P, P])
        iota_bins = sb("iota_bins", [P, NT * P], mybir.dt.int16)
        iota = sb("iota", [P, P])
        before = sb("before", [P, P])
        ones = sb("ones", [P, P])
        valid = sb("valid", [P, NT])
        wq = sb("wq", [P, KC, C])
        wkv = sb("wkv", [P, KC, 2 * C])
        wm = sb("wm", [P, KC, C])
        gnn_raw = xnT[:, 0, 0:KC * C].rearrange("p (k c) -> p k c", k=KC)
        gnnT = sb("gnnT", [P, KC, C])
        w1 = sb("w1", [P, 2 * KC, HID])
        w2 = sb("w2", [P, HC, C])
        gw = sb("gw", [P, KC, NE])
        g1c = sb("g1c", [P, KC])
        b1c = sb("b1c", [P, KC])
        g2r = sb("g2r", [P, C])
        bias_row = sb("bias_row", [P, 2, C])
        gate_row = sb("gate_row", [P, NE])
        KV = sb("KV", [P, KC, P + 1])
        KVd = sb("KVd", [P, KC, P + HPC])
        logits = sb("logits", [P, NT, NE])
        slots = sb("slots", [P, 2, NT], I32)
        gates = sb("gates", [P, 2, NT])
        owner = sb("owner", [1, ETILES], I32)
        tiny = sb("tiny", [P, 8, 32])
        epsc = sb("epsc", [P, 1])
        s_at = sb("s_at", [P, DT, 2], I32)
        edge_i = sb("edge_i", [EP, 3, NG * GE], I32)
        src_i, dst_i, part_i = edge_i[:, 0, :], edge_i[:, 1, :], edge_i[:, 2, :]
        wgt = sb("wgt", [EP, NG * GE])
        bin_f = sb("bin_f", [EP, NG * GE])
        piece = sb("piece", [EP, PIECES, NG * GE], BF16)
        in_bin = sb("in_bin", [EP, BINS, GE])
        count = sb("count", [EP, 1 + BINS * GE])
        in_tile = sb("in_tile", [EP, GE, GT], BF16)
        in_slot = sb("in_slot", [EP, GE, P], BF16)
        record = sb("record", [EP, GE, PIECES, GT], BF16)
        ordered = sb("ordered", [P, PIECES, GT])
        place_i = sb("place_i", [EP, 3, GE], I32)
        place_f = sb("place_f", [EP, 2, GE])
        ends_i = sb("ends_i", [1, BINS], I32)
        meets = edge_i[0:1, :, :].rearrange("p a b -> p (a b)")[:, 0:STEPS * BINS].bitcast(F32).rearrange("p (a b) -> p a b", b=BINS)
        pair_f = sb("pair_f", [1, STEPS, 2])
        pairs = [sb(f"pairs{h}", [1, STEPS, 2], I32) for h in range(2)]
        gather_i = [sb(f"gather_i{h}", [P, GT], I32) for h in range(2)]
        node = [sb(f"node{h}", [P, GT]) for h in range(2)]
        weight = [sb(f"weight{h}", [P, GT]) for h in range(2)]
        zero = sb("zero", [P, P])
        hot = xn[:, :, :].rearrange("p t c -> p (t c)")[:, 0:STEPS * P].rearrange("p (s k c) -> p s k c", k=SU, c=P)

        at = [NT * C]

        def ring(width, slots_=U, start=None):
            if start is not None:
                at[0] = start
            a = arena[:, at[0]:at[0] + slots_ * width].rearrange("p (s c) -> p s c", c=width)
            at[0] += slots_ * width
            return a

        tok = ring(C)
        feat = ring(C)
        neg = ring(C)
        wide = ring(2 * C)
        assert at[0] <= 2 * NT * C
        e_w1 = ring(KC * EH, 2, 0)
        e_w2 = ring(KC * EH, 2)
        e_w3 = ring(EHC * C, 2)
        e_x = ring(C, 2)
        e_xT = ring(C, 2)
        e_act = ring(EH, 2)
        e_hid = ring(EH, 2)
        e_y = ring(C, 2)
        assert at[0] <= 2 * NT * C
        x_again = ring(C, U, 0)
        nbr = ring(C)
        xn_again = ring(C)
        c_y1 = ring(C, DT, 0)
        c_y2 = ring(C, DT)
        c_out = ring(C, DT)
        s_x = ring(C, DT)
        squares = arena[:, 0:NT * C].rearrange("p (t c) -> p t c", c=C)
        r_at = [0]

        def routing(*shape, dt=F32):
            n = 1
            for s in shape:
                n *= s
            a = arena[:, r_at[0]:r_at[0] + n]
            r_at[0] += n
            if len(shape) == 2:
                a = a.rearrange("p (a b) -> p a b", b=shape[1])
            return a if dt == F32 else a.bitcast(dt)

        psum = ctx.enter_context(nc.psum_tensor("psum", [P, 8 * 512], F32))
        bank = [psum[:, i * 512:(i + 1) * 512] for i in range(8)]
        sums = psum[:, 0:BINS * P].rearrange("p (b c) -> p b c", c=P)
        BPB = 512 // P
        BANKS = -(-BINS // BPB)

        x_loaded, edges_loaded, weights_loaded, zero_pad = sem("x_loaded"), sem("edges_loaded"), sem("weights_loaded"), sem("zero_pad")
        consts_ready, var_ready, std_ready, xn_ready, xn_stored = sem("consts_ready"), sem("var_ready"), sem("std_ready"), sem("xn_ready"), sem("xn_stored")
        gnn_turned, gnnT_ready = sem("gnn_turned"), sem("gnnT_ready")
        ring_tok, ring_turned, ring_feat, ring_kept = sem("ring_tok"), sem("ring_turned"), sem("ring_feat"), sem("ring_kept")
        ring_kv, ring_kv_sb, ring_kneg, ring_kexp, ring_k = sem("ring_kv"), sem("ring_kv_sb"), sem("ring_kneg"), sem("ring_kexp"), sem("ring_k")
        kv_part, kv_added, kvd_ready = sem("kv_part"), sem("kv_added"), sem("kvd_ready")
        counts_ready, prefix_ready, record_ready, ordered_ready, list_ready = sem("counts_ready"), sem("prefix_ready"), sem("record_ready"), sem("ordered_ready"), sem("list_ready")
        hot_ready, met, flushed, group_added = sem("hot_ready"), sem("met"), sem("flushed"), sem("group_added")
        gathered = [sem("gathered0"), sem("gathered1")]
        ordered_read = sem("ordered_read")
        x_back, x_base = sem("x_back"), sem("x_base")
        ring_q, ring_q_sb, ring_qneg, ring_qexp, ring_qelu = sem("ring_q"), sem("ring_q_sb"), sem("ring_qneg"), sem("ring_qexp"), sem("ring_qelu")
        ring_att, ring_msg, ring_msgT, ring_msgT_sb = sem("ring_att"), sem("ring_msg"), sem("ring_msgT"), sem("ring_msgT_sb")
        ring_mm, ring_mm_sb, ring_n1, ring_n1T, ring_n1T_sb = sem("ring_mm"), sem("ring_mm_sb"), sem("ring_n1"), sem("ring_n1T"), sem("ring_n1T_sb")
        ring_h, ring_h_sb, ring_h2, ring_h2_sb, ring_n2 = sem("ring_h"), sem("ring_h_sb"), sem("ring_h2"), sem("ring_h2_sb"), sem("ring_n2")
        ring_nbr, ring_nbrT, ring_nbrT_sb, ring_gnn, ring_x1, ring_x1_kept = sem("ring_nbr"), sem("ring_nbrT"), sem("ring_nbrT_sb"), sem("ring_gnn"), sem("ring_x1"), sem("ring_x1_kept")
        ring_n3, ring_n3_kept, ring_n3T, ring_n3T_sb, ring_gate, ring_logit = sem("ring_n3"), sem("ring_n3_kept"), sem("ring_n3T"), sem("ring_n3T_sb"), sem("ring_gate"), sem("ring_logit")
        mean_ready = [sem(f"mean{n}_ready") for n in range(3)]
        dev_ready = [sem(f"deviation{n}_ready") for n in range(3)]
        logits_neg, exp_ready, choice_counts, choice_prefix, slots_ready = sem("logits_neg"), sem("exp_ready"), sem("choice_counts"), sem("choice_prefix"), sem("slots_ready")
        slots_zeroed = sem("slots_zeroed")
        s_copied, scattered = sem("s_copied"), [sem(f"scattered{n}") for n in range(DT)]
        e_weights = [sem("e_weights0"), sem("e_weights1")]
        e_rows = [sem("e_rows0"), sem("e_rows1")]
        e_turned, e_feat, e_h1, e_h2, e_silu, e_hidden, e_out, e_out_sb = (
            sem("e_turned"), sem("e_feat"), sem("e_h1"), sem("e_h2"), sem("e_silu"), sem("e_hidden"), sem("e_out"), sem("e_out_sb"))
        e_stored = [sem("e_stored0"), sem("e_stored1")]
        y_gathered, y_summed, y_stored = [sem(f"y_gathered{n}") for n in range(DT)], sem("y_summed"), [sem(f"y_stored{n}") for n in range(DT)]

        def ready(t):
            return t + 1 + U

        def free(t):
            return t + 1

        def tile_of(a, i, j):
            return a[:].rearrange("p (a b) c -> p a b c", b=U)[:, bass.ds(i, 1), j, :].rearrange("p a c -> p (a c)")

        def xnT_of(k, i, j):
            return xnT[:, k, :].rearrange("p (a b c) -> p a b c", b=U, c=P)[:, bass.ds(i, 1), j, :].rearrange("p a c -> p (a c)")

        def edges_of(a, g):
            return a.rearrange("p (g c) -> p g c", c=GE)[:, bass.ds(g, 1), :].rearrange("p g c -> p (g c)")

        x_tiles = x[0:(NT - 1) * P, :].rearrange("(t p) c -> p t c", p=P)
        block = ctx.enter_context(nc.Block())

        @block.sync
        def _(sp):
            sp.dma_start(xn[:, 0:NT - 1, :], x_tiles).then_inc(x_loaded, 16)
            sp.wait_ge(zero_pad, 1)
            sp.dma_start(xn[0:LAST, NT - 1, :], x[(NT - 1) * P:N, :]).then_inc(x_loaded, 16)
            for a, b in ((src_i, src), (dst_i, dst), (wgt[:, :], edge_weight)):
                sp.dma_start(a, b.rearrange("(p c) -> p c", p=EP)).then_inc(edges_loaded, 16)
            chunks = "(k p) n -> p k n"
            loads = [(wkv[:, :, 0:C], Wk.rearrange(chunks, p=P)), (wkv[:, :, C:2 * C], Wv.rearrange(chunks, p=P)),
                     (wq[:, :, :], Wq.rearrange(chunks, p=P)), (wm[:, :, :], Wm.rearrange(chunks, p=P)),
                     (gnn_raw[:, :, :], gnn_W.rearrange(chunks, p=P)), (w1[:, :, :], W1.rearrange(chunks, p=P)),
                     (w2[:, :, :], W2.rearrange(chunks, p=P)), (gw[:, :, :], gate_w.rearrange(chunks, p=P)),
                     (g2r[:, :], g2.rearrange("(a c) -> a c", a=1).to_broadcast([P, C])),
                     (bias_row[:, 0, :], b2.rearrange("(a c) -> a c", a=1).to_broadcast([P, C])),
                     (bias_row[:, 1, :], gnn_b.rearrange("(a c) -> a c", a=1).to_broadcast([P, C])),
                     (gate_row[:, :], gate_b.rearrange("(a c) -> a c", a=1).to_broadcast([P, NE]))]
            for a, b in loads:
                sp.dma_start(a, b).then_inc(weights_loaded, 16)
            with nc.allow_non_contiguous_dma(reason="two short columns"):
                for k in range(KC):
                    sp.dma_start(g1c[:, k:k + 1], g1[k * P:(k + 1) * P].rearrange("(p a) -> p a", a=1)).then_inc(weights_loaded, 16)
                    sp.dma_start(b1c[:, k:k + 1], b1[k * P:(k + 1) * P].rearrange("(p a) -> p a", a=1)).then_inc(weights_loaded, 16)
            sp.wait_ge(consts_ready, 1)
            sp.dma_start(slot_rows.rearrange("(p t) c -> p t c", p=P),
                         agg[:, 0, :].unsqueeze(1).to_broadcast([P, ETILES, C])).then_inc(slots_zeroed, 16)
            sp.wait_ge(xn_ready, 1)
            sp.dma_start(xn_rows[0:(NT - 1) * P, :].rearrange("(t p) c -> p t c", p=P), xn[:, 0:NT - 1, :]).then_inc(xn_stored, 16)
            sp.dma_start(xn_rows[(NT - 1) * P:N, :], xn[0:LAST, NT - 1, :]).then_inc(xn_stored, 16)
            sp.wait_ge(group_added, NG)
            xn_tiles = xn_rows[0:(NT - 1) * P, :].rearrange("(t p) c -> p t c", p=P)
            for i in range(TURNS):
                if i >= 1:
                    sp.wait_ge(ring_x1, ready(i * U - 1))
                for a, tiles, rest in ((x_again, x_tiles, x), (xn_again, xn_tiles, xn_rows)):
                    sp.dma_start(a[:, 0:U - 1, :], tiles[:, i * U:i * U + U - 1, :]).then_inc(x_back, 16)
                    if i < TURNS - 1:
                        sp.dma_start(a[:, U - 1, :], tiles[:, i * U + U - 1, :]).then_inc(x_back, 16)
                    else:
                        sp.dma_start(a[0:LAST, U - 1, :], rest[(NT - 1) * P:N, :]).then_inc(x_back, 16)
            sp.wait_ge(slots_ready, 1)
            for n in range(DT):
                sp.wait_ge(scattered[n], 32 * (NT - 1) // DT + (32 if n == 0 else 0))
            with sp.Fori(0, ETILES // 2) as i:
                for h in range(2):
                    e = nc.values_load(owner[0:1, :].rearrange("p (a b) -> p a b", b=2)[:, bass.ds(i, 1), h], engines=SP,
                                       min_val=0, max_val=NE - 1,
                                       skip_runtime_bounds_check_because="it is a minimum with NE - 1 of a count")
                    sp.wait_ge(e_hidden, 2 * i + h + 1)
                    sp.wait_ge(e_out, 2 * i + h + 1)
                    sp.nop(nofuse=True)
                    sp.dma_start(e_x[:, h, :], slot_rows.rearrange("(a b p) c -> a b p c", b=2, p=P)[bass.ds(i, 1), h, :, :]
                                 .rearrange("a p c -> (a p) c")).then_inc(e_rows[h], 16)
                    for w, b, k in ((e_w1, ew1, KC), (e_w2, ew2, KC), (e_w3, ew3, EHC)):
                        sp.dma_start(w[:, h, :].rearrange("p (k n) -> p k n", k=k),
                                     b.rearrange("e (k p) n -> e p k n", p=P)[bass.ds(e, 1), :, :, :].rearrange("e p k n -> (e p) k n"))\
                            .then_inc(e_weights[h], 16)
            for n in range(DT):
                sp.wait_ge(y_stored[n], 16 + 16 * (NT - 1) // DT + (16 if n == 0 else 0))

        @block.scalar
        def _(act):
            for s in (ring_tok, ring_kv_sb, ring_kexp, ring_q_sb, ring_qexp, ring_msgT_sb, ring_mm_sb, ring_n1T_sb,
                      ring_h_sb, ring_h2_sb, ring_nbr, ring_nbrT_sb, ring_x1_kept, ring_n3T_sb):
                act.sem_inc(s, U)
            for s in (e_silu, e_out_sb):
                act.sem_inc(s, 2)
            for n in range(DT):
                act.sem_inc(y_stored[n], 16)
            act.wait_ge(consts_ready, 1)
            act.wait_ge(var_ready, 1)
            act.activation(tiny[:, 2, 0:NT], tiny[:, 1, 0:NT], ACT.Sqrt, scale=1.0 / C, bias=epsc[:, 0:1]).then_inc(std_ready, 1)
            act.wait_ge(gnn_turned, 1)
            act.activation(gnnT[:, :, :], bank[7][:, :].rearrange("p (k n) -> p k n", k=KC), ACT.Copy).then_inc(gnnT_ready, 1)

            act.wait_ge(xn_ready, 1)
            with act.Fori(0, TURNS) as i:
                for j in range(U):
                    t = i * U + j
                    act.wait_ge(ring_turned, free(t))
                    act.nop(nofuse=True)
                    act.activation(tok[:, j, :], tile_of(xn, i, j), ACT.Copy).then_inc(ring_tok, 1)
                for j in range(U):
                    t = i * U + j
                    act.wait_ge(ring_kv, ready(t))
                    act.wait_ge(kv_part, i + 1)
                    act.nop(nofuse=True)
                    act.activation(wide[:, j, :], bank[j][:, :], ACT.Copy).then_inc(ring_kv_sb, 1)
                for j in range(U):
                    t = i * U + j
                    act.wait_ge(ring_kneg, ready(t))
                    act.nop(nofuse=True)
                    act.activation(neg[:, j, :], neg[:, j, :], ACT.Exp).then_inc(ring_kexp, 1)

            def deviations(n, i):
                act.wait_ge(mean_ready[n], i + 1)
                act.nop(nofuse=True)
                for j in range(U):
                    act.activation(neg[:, j, :], tok[:, j, :], ACT.Square, bias=tiny[:, 4, j:j + 1],
                                   accum_out=tiny[:, 5, j:j + 1])
                act.drain()
                act.activation(tiny[:, 6, 0:U], tiny[:, 5, 0:U], ACT.Sqrt, scale=1.0 / C, bias=epsc[:, 0:1]).then_inc(dev_ready[n], 1)

            act.wait_ge(weights_loaded, 16 * 16)
            act.wait_ge(group_added, NG)
            with act.Fori(0, TURNS) as i:
                for j in range(U):
                    act.wait_ge(ring_q, ready(i * U + j))
                    act.nop(nofuse=True)
                    act.activation(wide[:, j, 0:C], bank[j][:, 0:C], ACT.Copy).then_inc(ring_q_sb, 1)
                for j in range(U):
                    act.wait_ge(ring_qneg, ready(i * U + j))
                    act.nop(nofuse=True)
                    act.activation(neg[:, j, :], neg[:, j, :], ACT.Exp).then_inc(ring_qexp, 1)
                for j in range(U):
                    act.wait_ge(ring_msgT, ready(i * U + j))
                    act.nop(nofuse=True)
                    act.activation(feat[:, j, :], bank[j][:, 0:C], ACT.Copy).then_inc(ring_msgT_sb, 1)
                for j in range(U):
                    act.wait_ge(ring_mm, ready(i * U + j))
                    act.nop(nofuse=True)
                    act.activation(tok[:, j, :], bank[j][:, 0:C], ACT.Copy, accum_out=tiny[:, 3, j:j + 1]).then_inc(ring_mm_sb, 1)
                deviations(0, i)
                for j in range(U):
                    act.wait_ge(ring_n1T, ready(i * U + j))
                    act.nop(nofuse=True)
                    for k in range(KC):
                        last = act.activation(feat[:, j, k * P:(k + 1) * P], bank[j][:, k * P:(k + 1) * P], ACT.Identity,
                                              scale=g1c[:, k:k + 1], bias=b1c[:, k:k + 1])
                    last.then_inc(ring_n1T_sb, 1)
                for j in range(U):
                    act.wait_ge(ring_h, ready(i * U + j))
                    act.nop(nofuse=True)
                    act.activation(wide[:, j, :], bank[j][:, :], ACT.Relu).then_inc(ring_h_sb, 1)
                for j in range(U):
                    act.wait_ge(ring_h2, ready(i * U + j))
                    act.nop(nofuse=True)
                    act.activation(tok[:, j, :], bank[j][:, 0:C], ACT.Copy, accum_out=tiny[:, 3, j:j + 1]).then_inc(ring_h2_sb, 1)
                for j in range(U):
                    act.activation(nbr[:, j, :], tile_of(agg, i, j), ACT.Copy).then_inc(ring_nbr, 1)
                deviations(1, i)
                for j in range(U):
                    act.wait_ge(ring_nbrT, ready(i * U + j))
                    act.nop(nofuse=True)
                    act.activation(feat[:, j, :], bank[j][:, 0:C], ACT.Copy).then_inc(ring_nbrT_sb, 1)
                for j in range(U):
                    act.wait_ge(ring_x1, ready(i * U + j))
                    act.nop(nofuse=True)
                    act.activation(tile_of(xn, i, j), tok[:, j, :], ACT.Copy, accum_out=tiny[:, 3, j:j + 1]).then_inc(ring_x1_kept, 1)
                deviations(2, i)
                for j in range(U):
                    act.wait_ge(ring_n3T, ready(i * U + j))
                    act.nop(nofuse=True)
                    act.activation(feat[:, j, :], bank[j][:, 0:C], ACT.Copy).then_inc(ring_n3T_sb, 1)

            act.wait_ge(logits_neg, 1)
            act.activation(logits[:, :, :], logits[:, :, :], ACT.Exp).then_inc(exp_ready, 1)

            with act.Fori(0, ETILES // 2) as i:
                for h in range(2):
                    n = 2 * i + h
                    act.wait_ge(e_h1, n + 3)
                    act.wait_ge(e_hidden, n + 1)
                    act.nop(nofuse=True)
                    act.activation(e_act[:, h, :], bank[h][:, :], ACT.Silu).then_inc(e_silu, 1)
                    act.wait_ge(e_out, n + 3)
                    act.wait_ge(e_stored[h], 16 * i + 16)
                    act.nop(nofuse=True)
                    act.activation(e_y[:, h, :], bank[6 + h][:, 0:C], ACT.Copy).then_inc(e_out_sb, 1)
                    act.wait_ge(e_out_sb, n + 3)
                    act.nop(nofuse=True)
                    act.dma_start(expert_rows.rearrange("(a b p) c -> a b p c", b=2, p=P)[bass.ds(i, 1), h, :, :]
                                  .rearrange("a p c -> (a p) c"), e_y[:, h, :]).then_inc(e_stored[h], 16)

            with act.Fori(0, (NT - 1) // DT) as i:
                for n in range(DT):
                    act.wait_ge(y_summed, i * DT + n + 1)
                    act.nop(nofuse=True)
                    act.dma_start(out[0:(NT - 1) * P, :].rearrange("(a b p) c -> a b p c", b=DT, p=P)[bass.ds(i, 1), n, :, :]
                                  .rearrange("a p c -> (a p) c"), c_out[:, n, :]).then_inc(y_stored[n], 16)
            act.wait_ge(y_summed, NT)
            act.dma_start(out[(NT - 1) * P:N, :], c_out[0:LAST, 0, :]).then_inc(y_stored[0], 16)

        @block.gpsimd
        def _(pool):
            for s in (ring_kept, ring_n3_kept):
                pool.sem_inc(s, U)
            for h in range(2):
                pool.sem_inc(e_stored[h], 16)
            pool.memset(xn[:, NT - 1, :], 0.0)
            pool.drain().then_inc(zero_pad, 1)
            pool.memset(epsc[:, :], LN_EPS)
            pool.memset(ones[:, :], 1.0)
            pool.memset(zero[:, :], 0.0)
            pool.memset(ident[:, :], 0.0)
            pool.memset(before[:, :], 1.0)
            pool.memset(valid[:, :], 1.0)
            pool.memset(KV[:, :, :], 0.0)
            pool.memset(KVd[:, :, :], 0.0)
            pool.memset(agg[:, :, :], 0.0)
            pool.memset(count[:, 0:1], 0.0)
            pool.drain()
            pool.affine_select(out=ident[:, :], in_=ident[:, :], compare_op=ALU.not_equal, fill=1.0, base=0,
                               pattern=[[-1, P]], channel_multiplier=1)
            pool.affine_select(out=before[:, :], in_=before[:, :], compare_op=ALU.is_gt, fill=0.0, base=0,
                               pattern=[[1, P]], channel_multiplier=-1)
            pool.affine_select(out=valid[:, NT - 1:NT], in_=valid[:, NT - 1:NT], compare_op=ALU.is_gt, fill=0.0, base=LAST,
                               pattern=[[0, 1]], channel_multiplier=-1)
            pool.iota(iota_bins[:, :], [[1, NT * P]], base=0, channel_multiplier=0)
            pool.iota(iota[:, :], [[1, P]], base=0, channel_multiplier=0, allow_small_or_imprecise_dtypes=True)
            pool.drain().then_inc(consts_ready, 1)

            with pool.Fori(0, TURNS) as i:
                for j in range(U):
                    pool.wait_ge(ring_feat, ready(i * U + j))
                    pool.nop(nofuse=True)
                    for k in range(KC):
                        last = pool.tensor_copy(xnT_of(k, i, j), feat[:, j, k * P:(k + 1) * P])
                    last.then_inc(ring_kept, 1)

            def gather(g, h, first):
                pool.wait_ge(list_ready, g + 1)
                if not first:
                    pool.wait_ge(group_added, g - 1)
                pool.nop(nofuse=True)
                for t in range(GT):
                    pool.indirect_dma_start(rows[h][:, t, :], None, xn_rows,
                                            bass.IndirectOffsetOnAxis(ap=gather_i[h][:, t:t + 1], axis=0)).then_inc(gathered[h], 16)

            pool.wait_ge(xn_stored, 32)
            pool.drain()
            pool.wait_ge(kvd_ready, 1)
            gather(0, 0, True)
            gather(1, 1, True)
            with pool.Fori(0, (NG - 3) // 2) as i:
                for h in range(2):
                    gather(2 * i + h + 2, h, False)
            gather(NG - 1, 0, False)

            pool.wait_ge(weights_loaded, 16 * 16)
            pool.tensor_tensor(bias_row[:, 0, :], bias_row[:, 0, :], bias_row[:, 1, :], ALU.add)
            pool.drain()
            with pool.Fori(0, TURNS) as i:
                pool.wait_ge(x_back, 64 * i + 64)
                pool.nop(nofuse=True)
                for j in range(U):
                    pool.tensor_tensor(x_again[:, j, :], x_again[:, j, :], bias_row[:, 0, :], ALU.add)
                pool.drain()
                for j in range(U):
                    pool.tensor_tensor(x_again[:, j, :], x_again[:, j, :], xn_again[:, j, :], ALU.add).then_inc(x_base, 1)
                for j in range(U):
                    pool.wait_ge(ring_n3, ready(i * U + j))
                    pool.wait_ge(ring_nbr, ready(i * U + j))
                    pool.nop(nofuse=True)
                    pool.tensor_copy(tile_of(agg, i, j), tok[:, j, :]).then_inc(ring_n3_kept, 1)

            pool.wait_ge(slots_ready, 1)
            pool.wait_ge(slots_zeroed, 16)

            def scatter(n, rows_n):
                for c in range(2):
                    pool.indirect_dma_start(slot_rows, bass.IndirectOffsetOnAxis(ap=s_at[0:rows_n, n, c:c + 1], axis=0),
                                            s_x[0:rows_n, n, :], None).then_inc(scattered[n], 16)

            with pool.Fori(0, (NT - 1) // DT) as i:
                for n in range(DT):
                    pool.wait_ge(s_copied, i * DT + n + 1)
                    pool.nop(nofuse=True)
                    scatter(n, P)
            pool.wait_ge(s_copied, NT)
            scatter(0, LAST)

            def collect(n, rows_n):
                for c, y in ((0, c_y1), (1, c_y2)):
                    pool.indirect_dma_start(y[0:rows_n, n, :], None, expert_rows,
                                            bass.IndirectOffsetOnAxis(ap=s_at[0:rows_n, n, c:c + 1], axis=0)).then_inc(y_gathered[n], 16)

            for h in range(2):
                pool.wait_ge(e_stored[h], 16 * (ETILES // 2 + 1))
            with pool.Fori(0, (NT - 1) // DT) as i:
                for n in range(DT):
                    pool.wait_ge(s_copied, NT + i * DT + n + 1)
                    pool.nop(nofuse=True)
                    collect(n, P)
            pool.wait_ge(s_copied, 2 * NT)
            collect(0, LAST)

        @block.tensor
        def _(pe):
            for s in (ring_turned, ring_kv, ring_q, ring_att, ring_msgT, ring_mm, ring_n1T, ring_h, ring_h2,
                      ring_nbrT, ring_gnn, ring_n3T, ring_gate):
                pe.sem_inc(s, U)
            pe.sem_inc(kv_part, 1)
            for s in (e_turned, e_h1, e_h2, e_out):
                pe.sem_inc(s, 2)

            def turn(j, a):
                for k in range(KC):
                    last = pe.transpose(bank[j][:, k * P:(k + 1) * P], a[:, j, k * P:(k + 1) * P], ident[:, :])
                return last

            def project(j, w, n):
                for k in range(KC):
                    last = pe.matmul(bank[j][:, 0:n], feat[:, j, k * P:(k + 1) * P], w[:, k, 0:n],
                                     start=(k == 0), stop=(k == KC - 1))
                return last

            pe.wait_ge(consts_ready, 1)
            pe.wait_ge(weights_loaded, 16 * 16)
            for m in range(KC):
                for k in range(KC):
                    last = pe.transpose(bank[7][:, k * C + m * P:k * C + (m + 1) * P], gnn_raw[:, m, k * P:(k + 1) * P], ident[:, :])
            last.then_inc(gnn_turned, 1)

            with pe.Fori(0, TURNS) as i:
                for j in range(U):
                    pe.wait_ge(ring_tok, ready(i * U + j))
                    pe.wait_ge(ring_kv_sb, free(i * U + j))
                    pe.nop(nofuse=True)
                    turn(j, tok).then_inc(ring_turned, 1)
                for j in range(U):
                    pe.wait_ge(ring_feat, ready(i * U + j))
                    pe.nop(nofuse=True)
                    project(j, wkv, 2 * C).then_inc(ring_kv, 1)
                pe.wait_ge(kv_added, i + 1)
                for j in range(U):
                    pe.wait_ge(ring_k, ready(i * U + j))
                    pe.nop(nofuse=True)
                    for m in range(KC):
                        k_m = wide[:, j, m * P:(m + 1) * P]
                        pe.matmul(bank[5 + m][:, 0:P], k_m, wide[:, j, C + m * P:C + (m + 1) * P],
                                  start=(j == 0), stop=(j == U - 1), skip_group_check=True)
                        mask = valid[:, :].rearrange("p (a b) -> p a b", b=U)[:, bass.ds(i, 1), j]
                        last = pe.matmul(bank[5 + m][:, P:P + 1], k_m, mask,
                                         start=False, stop=(j == U - 1), skip_group_check=True)
                last.then_inc(kv_part, 1)

            def prefix(g):
                pe.wait_ge(counts_ready, g + 1)
                pe.nop(nofuse=True)
                pe.matmul(bank[7][:, 0:BINS], before[0:EP, :], tiny[0:EP, 0, 0:BINS], start=True, stop=True)
                pe.matmul(bank[7][:, 32:32 + BINS], ones[0:EP, :], tiny[0:EP, 0, 0:BINS], start=True, stop=True)\
                    .then_inc(prefix_ready, 1)

            def reorder(g):
                pe.wait_ge(record_ready, g + 1)
                pe.nop(nofuse=True)
                for c in range(GE):
                    last = pe.matmul(bank[7][:, 64:64 + PIECES * GT], in_slot[:, c, :], record[:, c, :, :].rearrange("p a b -> p (a b)"),
                                     start=(c == 0), stop=(c == GE - 1))
                last.then_inc(ordered_ready, 1)

            def add_up(g, g_half, h, ordering):
                pe.wait_ge(list_ready, g + 1)
                pe.wait_ge(gathered[h], 16 * GT * (g_half + 1))
                pe.nop(nofuse=True)
                for c in range(KC):
                    for s in range(STEPS // SU):
                        _, pair = nc.values_load_multi_w_load_instructions(
                            pairs[h][0:1, s * SU:(s + 1) * SU, :].rearrange("p a b -> p (a b)"),
                            engines=PE, min_val=0, max_val=BINS - 1,
                            skip_runtime_bounds_check_because="bins and tiles are clipped when the list is made")
                        for k in range(SU):
                            n = s * SU + k
                            if n % BPB == 0 and n // BPB < BANKS:
                                b = n // BPB
                                pe.wait_ge(flushed, (g * KC + c) * BANKS + b + 1)
                                pe.nop(nofuse=True)
                                pe.matmul(bank[b][:, 0:2], zero[:, :], ident[:, 0:2], start=True, stop=True)
                            if c == 0:
                                pe.wait_ge(hot_ready, g * STEPS + n + 1)
                                pe.nop(nofuse=True)
                            pe.matmul(sums[:, bass.ds(pair[2 * k + 1], 1), :].rearrange("p a c -> p (a c)"), hot[:, s, k, :],
                                      rows[h][:, bass.ds(pair[2 * k], 1), c * P:(c + 1) * P].rearrange("p a c -> p (a c)"),
                                      start=False, stop=True, skip_group_check=True).then_inc(met, 1)
                            if ordering and c == KC - 1 and n == SU + 3:
                                prefix(g + 2)
                if ordering:
                    reorder(g + 2)

            for g in range(2):
                prefix(g)
                reorder(g)
            with pe.Fori(0, (NG - 3) // 2) as i:
                for h in range(2):
                    add_up(2 * i + h, i, h, True)
            add_up(NG - 3, (NG - 3) // 2, 0, True)
            add_up(NG - 2, (NG - 3) // 2, 1, False)
            add_up(NG - 1, (NG - 1) // 2, 0, False)

            pe.wait_ge(group_added, NG)
            with pe.Fori(0, TURNS) as i:
                for j in range(U):
                    pe.wait_ge(ring_logit, free(i * U + j))
                    pe.wait_ge(ring_kept, ready(i * U + j))
                    pe.nop(nofuse=True)
                    for m in range(KC):
                        for k in range(KC):
                            last = pe.matmul(bank[j][:, m * P:(m + 1) * P], wq[:, k, m * P:(m + 1) * P], xnT_of(k, i, j),
                                             start=(k == 0), stop=(k == KC - 1))
                    last.then_inc(ring_q, 1)
                for j in range(U):
                    pe.wait_ge(ring_qelu, ready(i * U + j))
                    pe.nop(nofuse=True)
                    for m in range(KC):
                        last = pe.matmul(bank[j][:, m * (P + HPC):(m + 1) * (P + HPC)], wide[:, j, m * P:(m + 1) * P], KVd[:, m, :],
                                         start=True, stop=True)
                    last.then_inc(ring_att, 1)
                for j in range(U):
                    pe.wait_ge(ring_msg, ready(i * U + j))
                    pe.nop(nofuse=True)
                    turn(j, tok).then_inc(ring_msgT, 1)
                for j in range(U):
                    pe.wait_ge(ring_msgT_sb, ready(i * U + j))
                    pe.nop(nofuse=True)
                    project(j, wm, C).then_inc(ring_mm, 1)
                for j in range(U):
                    pe.wait_ge(ring_n1, ready(i * U + j))
                    pe.nop(nofuse=True)
                    turn(j, tok).then_inc(ring_n1T, 1)
                for j in range(U):
                    pe.wait_ge(ring_n1T_sb, ready(i * U + j))
                    pe.nop(nofuse=True)
                    for m in range(HC):
                        for k in range(2 * KC):
                            operand = xnT_of(k, i, j) if k < KC else feat[:, j, (k - KC) * P:(k - KC + 1) * P]
                            last = pe.matmul(bank[j][:, m * P:(m + 1) * P], w1[:, k, m * P:(m + 1) * P], operand,
                                             start=(k == 0), stop=(k == 2 * KC - 1))
                    last.then_inc(ring_h, 1)
                for j in range(U):
                    pe.wait_ge(ring_h_sb, ready(i * U + j))
                    pe.nop(nofuse=True)
                    for k in range(HC):
                        last = pe.matmul(bank[j][:, 0:C], wide[:, j, k * P:(k + 1) * P], w2[:, k, :],
                                         start=(k == 0), stop=(k == HC - 1))
                    last.then_inc(ring_h2, 1)
                for j in range(U):
                    pe.wait_ge(ring_h2_sb, ready(i * U + j))
                    pe.wait_ge(ring_nbr, ready(i * U + j))
                    pe.nop(nofuse=True)
                    turn(j, nbr).then_inc(ring_nbrT, 1)
                for j in range(U):
                    pe.wait_ge(ring_nbrT_sb, ready(i * U + j))
                    pe.nop(nofuse=True)
                    project(j, gnnT, C).then_inc(ring_gnn, 1)
                for j in range(U):
                    pe.wait_ge(ring_n3, ready(i * U + j))
                    pe.nop(nofuse=True)
                    turn(j, tok).then_inc(ring_n3T, 1)
                for j in range(U):
                    pe.wait_ge(ring_n3T_sb, ready(i * U + j))
                    pe.nop(nofuse=True)
                    project(j, gw, NE).then_inc(ring_gate, 1)

            pe.wait_ge(choice_counts, 1)
            pe.matmul(bank[7][:, 0:NE], before[:, :], tiny[:, 0, 0:NE], start=True, stop=True)
            pe.matmul(bank[7][:, 32:32 + NE], ones[:, :], tiny[:, 0, 0:NE], start=True, stop=True).then_inc(choice_prefix, 1)

            with pe.Fori(0, ETILES // 2) as i:
                for h in range(2):
                    n = 2 * i + h
                    pe.wait_ge(e_rows[h], 16 * i + 16)
                    pe.wait_ge(e_feat, n + 1)
                    pe.nop(nofuse=True)
                    for k in range(KC):
                        last = pe.transpose(bank[4 + h][:, k * P:(k + 1) * P], e_x[:, h, k * P:(k + 1) * P], ident[:, :])
                    last.then_inc(e_turned, 1)
                    pe.wait_ge(e_feat, n + 3)
                    pe.wait_ge(e_weights[h], 48 * i + 48)
                    pe.wait_ge(e_silu, n + 1)
                    pe.wait_ge(e_hidden, n + 1)
                    pe.nop(nofuse=True)
                    for b, w, done in ((h, e_w1, e_h1), (2 + h, e_w2, e_h2)):
                        for m in range(EHC):
                            for k in range(KC):
                                last = pe.matmul(bank[b][:, m * P:(m + 1) * P], w[:, h, k * EH + m * P:k * EH + (m + 1) * P],
                                                 e_xT[:, h, k * P:(k + 1) * P], start=(k == 0), stop=(k == KC - 1))
                        last.then_inc(done, 1)
                    pe.wait_ge(e_hidden, n + 3)
                    pe.wait_ge(e_out_sb, n + 1)
                    pe.nop(nofuse=True)
                    for k in range(EHC):
                        last = pe.matmul(bank[6 + h][:, 0:C], e_hid[:, h, k * P:(k + 1) * P], e_w3[:, h, k * C:(k + 1) * C],
                                         start=(k == 0), stop=(k == EHC - 1))
                    last.then_inc(e_out, 1)

        @block.vector
        def _(dve):
            for s in (ring_feat, ring_kneg, ring_k, ring_qneg, ring_qelu, ring_msg, ring_n1, ring_n2, ring_x1, ring_n3, ring_logit):
                dve.sem_inc(s, U)
            dve.sem_inc(kv_added, 1)
            dve.sem_inc(flushed, BANKS)
            for s in (e_feat, e_hidden):
                dve.sem_inc(s, 2)

            dve.wait_ge(x_loaded, 32)
            dve.tensor_reduce(tiny[:, 0, 0:NT], xn[:, :, :], AX, ALU.add)
            dve.drain()
            dve.tensor_scalar(tiny[:, 3, 0:NT], tiny[:, 0, 0:NT], -1.0 / C, None, ALU.mult)
            dve.drain()
            dve.tensor_tensor(xn[:, :, :], xn[:, :, :], tiny[:, 3, 0:NT].unsqueeze(2).to_broadcast([P, NT, C]), ALU.add)
            dve.drain()
            dve.tensor_tensor(squares, xn[:, :, :], xn[:, :, :], ALU.mult)
            dve.drain()
            dve.tensor_reduce(tiny[:, 1, 0:NT], squares, AX, ALU.add).then_inc(var_ready, 1)
            dve.wait_ge(std_ready, 1)
            dve.reciprocal(tiny[:, 3, 0:NT], tiny[:, 2, 0:NT])
            dve.drain()
            dve.tensor_tensor(xn[:, :, :], xn[:, :, :], tiny[:, 3, 0:NT].unsqueeze(2).to_broadcast([P, NT, C]), ALU.mult)\
                .then_inc(xn_ready, 1)

            dve.wait_ge(edges_loaded, 48)
            for n, (a, op, by) in enumerate(((src_i, ALU.arith_shift_right, 7), (src_i, ALU.bitwise_and, P - 1),
                                             (dst_i, ALU.arith_shift_right, 7), (dst_i, ALU.bitwise_and, P - 1))):
                dve.tensor_scalar(part_i, a, by, None, op)
                dve.drain()
                dve.tensor_copy(piece[:, n, :], part_i)
                if n == 0:
                    dve.tensor_copy(bin_f[:, :], part_i)
                dve.drain()
            for n in range(4, PIECES):
                dve.drain()
                dve.tensor_copy(piece[:, n, :], wgt[:, :])
                if n < PIECES - 1:
                    dve.drain()
                    dve.tensor_tensor(wgt[:, :], wgt[:, :], piece[:, n, :], ALU.subtract)
            dve.wait_ge(consts_ready, 1)

            with dve.Fori(0, TURNS) as i:
                for j in range(U):
                    t = i * U + j
                    dve.wait_ge(ring_turned, ready(t))
                    dve.wait_ge(ring_kv, free(t))
                    dve.wait_ge(ring_kept, free(t))
                    dve.nop(nofuse=True)
                    dve.tensor_copy(feat[:, j, :], bank[j][:, 0:C]).then_inc(ring_feat, 1)
                for j in range(U):
                    dve.wait_ge(ring_kv_sb, ready(i * U + j))
                    dve.nop(nofuse=True)
                    dve.tensor_scalar(neg[:, j, :], wide[:, j, 0:C], 0.0, None, ALU.min).then_inc(ring_kneg, 1)
                for j in range(U):
                    dve.wait_ge(ring_kexp, ready(i * U + j))
                    dve.nop(nofuse=True)
                    dve.scalar_tensor_tensor(wide[:, j, 0:C], wide[:, j, 0:C], 0.0, neg[:, j, :], ALU.max, ALU.add).then_inc(ring_k, 1)
                dve.wait_ge(kv_part, i + 2)
                dve.nop(nofuse=True)
                for m in range(KC):
                    last = dve.tensor_tensor(KV[:, m, :], bank[5 + m][:, 0:P + 1], KV[:, m, :], ALU.add)
                last.then_inc(kv_added, 1)
            dve.drain()
            dve.tensor_scalar(KV[:, :, 0:P], KV[:, :, 0:P], 1.0 / N, None, ALU.mult)
            dve.drain()
            for a in range(HPC):
                own = slice(a * HD, (a + 1) * HD)
                dve.tensor_copy(KVd[own, :, a * HD:(a + 1) * HD], KV[own, :, a * HD:(a + 1) * HD])
                dve.tensor_copy(KVd[own, :, P + a:P + a + 1], KV[own, :, P:P + 1])
            dve.drain().then_inc(kvd_ready, 1)

            iota_b = iota[:, 0:BINS]

            def count_bins(g):
                dve.tensor_tensor(in_bin[:, :, :], edges_of(bin_f[:, :], g).unsqueeze(1).to_broadcast([EP, BINS, GE]),
                                  iota_b[0:EP, :].unsqueeze(2).to_broadcast([EP, BINS, GE]), ALU.is_equal)
                dve.drain()
                flat = in_bin[:, :, :].rearrange("p b c -> p (b c)")
                dve.tensor_tensor_scan(count[:, 1:1 + BINS * GE], flat, flat, 0.0, ALU.add, ALU.max)
                dve.drain()
                begin = count[:, 0:BINS * GE].rearrange("p (b c) -> p b c", c=GE)[:, :, 0]
                end = count[:, 1:1 + BINS * GE].rearrange("p (b c) -> p b c", c=GE)[:, :, GE - 1]
                dve.tensor_tensor(tiny[0:EP, 0, 0:BINS], end, begin, ALU.subtract).then_inc(counts_ready, 1)

            def make_records(g):
                begin = count[:, 0:BINS * GE].rearrange("p (b c) -> p b c", c=GE)[:, :, 0]
                dve.wait_ge(prefix_ready, g + 1)
                dve.nop(nofuse=True)
                dve.tensor_copy(tiny[:, 1, 0:BINS], bank[7][:, 32:32 + BINS])
                dve.drain()
                dve.tensor_tensor_scan(tiny[:, 2, 0:BINS], tiny[:, 1, 0:BINS], tiny[:, 1, 0:BINS], 0.0, ALU.add, ALU.max)
                dve.drain()
                dve.tensor_tensor(tiny[:, 3, 0:BINS], tiny[:, 2, 0:BINS], tiny[:, 1, 0:BINS], ALU.subtract)
                dve.drain()
                dve.tensor_tensor(tiny[:, 3, 0:BINS], bank[7][:, 0:BINS], tiny[:, 3, 0:BINS], ALU.add)
                dve.drain()
                dve.scalar_tensor_tensor(tiny[0:EP, 3, 0:BINS], tiny[0:EP, 3, 0:BINS], 1.0, begin, ALU.subtract, ALU.subtract)
                dve.drain()
                places = count[:, 1:1 + BINS * GE].rearrange("p (b c) -> p b c", c=GE)
                dve.tensor_tensor(places, places, tiny[0:EP, 3, 0:BINS].unsqueeze(2).to_broadcast([EP, BINS, GE]), ALU.add)
                dve.drain()
                dve.tensor_tensor(places, places, in_bin[:, :, :], ALU.mult)
                dve.drain()
                dve.tensor_reduce(place_f[:, 0, :], places.rearrange("p b c -> p c b"), AX, ALU.add)
                dve.drain()
                dve.tensor_copy(place_i[:, 0, :], place_f[:, 0, :])
                dve.drain()
                dve.tensor_scalar(place_i[:, 1, :], place_i[:, 0, :], 7, None, ALU.arith_shift_right)
                dve.tensor_scalar(place_i[:, 2, :], place_i[:, 0, :], P - 1, None, ALU.bitwise_and)
                dve.drain()
                dve.tensor_copy(place_f[:, :, :], place_i[:, 1:3, :])
                dve.drain()
                dve.tensor_tensor(in_tile[:, :, :], place_f[:, 0, :].unsqueeze(2).to_broadcast([EP, GE, GT]),
                                  iota_b[0:EP, 0:GT].unsqueeze(1).to_broadcast([EP, GE, GT]), ALU.is_equal)
                dve.tensor_tensor(in_slot[:, :, :], place_f[:, 1, :].unsqueeze(2).to_broadcast([EP, GE, P]),
                                  iota[0:EP, 0:P].unsqueeze(1).to_broadcast([EP, GE, P]), ALU.is_equal)
                dve.drain()
                for n in range(PIECES):
                    last = dve.tensor_tensor(record[:, :, n, :], in_tile[:, :, :],
                                             edges_of(piece[:, n, :], g).unsqueeze(2).to_broadcast([EP, GE, GT]), ALU.mult)
                last.then_inc(record_ready, 1)
                dve.tensor_copy(ends_i[:, :], tiny[0:1, 2, 0:BINS])
                dve.drain()
                dve.tensor_scalar(ends_i[:, :], ends_i[:, :], 7, None, ALU.arith_shift_right)
                dve.drain()
                dve.tensor_tensor(tiny[0:1, 4, 0:BINS], ends_i[:, :], iota_b[0:1, :], ALU.add)
                dve.drain()
                dve.tensor_tensor(meets[:, :, :], tiny[0:1, 4, 0:BINS].unsqueeze(1).to_broadcast([1, STEPS, BINS]),
                                  iota[0:1, 0:STEPS].unsqueeze(2).to_broadcast([1, STEPS, BINS]), ALU.is_lt)
                dve.drain()
                dve.tensor_reduce(pair_f[:, :, 1], meets[:, :, :], AX, ALU.add)
                dve.drain()
                dve.tensor_tensor(pair_f[:, :, 0], iota[0:1, 0:STEPS], pair_f[:, :, 1], ALU.subtract)
                dve.drain()
                dve.tensor_scalar(pair_f[:, :, 0], pair_f[:, :, 0], float(GT - 1), None, ALU.min)
                dve.tensor_scalar(pair_f[:, :, 1], pair_f[:, :, 1], float(BINS - 1), None, ALU.min)

            def make_list(g, h):
                dve.drain()
                dve.wait_ge(ordered_ready, g + 1)
                dve.nop(nofuse=True)
                dve.tensor_copy(pairs[h][:, :, :], pair_f[:, :, :])
                dve.tensor_copy(ordered[:, :, :], bank[7][:, 64:64 + PIECES * GT].rearrange("p (a b) -> p a b", b=GT))
                dve.drain()
                dve.scalar_tensor_tensor(node[h][:, :], ordered[:, 0, :], float(P), ordered[:, 1, :], ALU.mult, ALU.add)
                dve.scalar_tensor_tensor(gather_i[h][:, :], ordered[:, 2, :], float(P), ordered[:, 3, :], ALU.mult, ALU.add)
                dve.tensor_tensor(weight[h][:, :], ordered[:, 6, :], ordered[:, 5, :], ALU.add)
                dve.drain()
                dve.tensor_tensor(weight[h][:, :], weight[h][:, :], ordered[:, 4, :], ALU.add)
                dve.drain().then_inc(list_ready, 1)

            def make_hot(h):
                with dve.Fori(0, STEPS // SU) as s:
                    _, pair = nc.values_load_multi_w_load_instructions(
                        pairs[h][0:1, :, :].rearrange("p (a b) c -> p a (b c)", b=SU)[:, bass.ds(s, 1), :].rearrange("p a c -> p (a c)"),
                        engines=DVE, min_val=0, max_val=BINS - 1,
                        skip_runtime_bounds_check_because="bins and tiles are clipped when the list is made")
                    for k in range(SU):
                        dve.tensor_scalar(hot[:, bass.ds(s, 1), k, :].rearrange("p a c -> p (a c)"),
                                          iota_bins[:, :].rearrange("p (b c) -> p b c", c=P)[:, bass.ds(pair[2 * k + 1], 1), :]
                                          .rearrange("p a c -> p (a c)"),
                                          node[h][:, bass.ds(pair[2 * k], 1)], weight[h][:, bass.ds(pair[2 * k], 1)],
                                          ALU.is_equal, ALU.mult).then_inc(hot_ready, 1)

            def flush(g, c):
                for b in range(BANKS):
                    own = slice(b * BPB, min((b + 1) * BPB, BINS))
                    dve.wait_ge(met, (g * KC + c) * STEPS + min((b + 1) * BPB + GT - 1, STEPS))
                    dve.nop(nofuse=True)
                    dve.tensor_tensor(agg[:, own, c * P:(c + 1) * P], sums[:, own, :], agg[:, own, c * P:(c + 1) * P], ALU.add)\
                        .then_inc(flushed, 1)

            def add_up(g, h, ordering):
                make_hot(h)
                for c in range(KC):
                    if ordering and c == KC - 1:
                        count_bins(g + 2)
                        make_records(g + 2)
                    flush(g, c)
                dve.drain().then_inc(group_added, 1)
                if ordering:
                    make_list(g + 2, h)

            dve.wait_ge(slots_zeroed, 16)
            dve.wait_ge(xn_stored, 32)
            for g in range(2):
                count_bins(g)
                make_records(g)
                make_list(g, g)
            with dve.Fori(0, (NG - 3) // 2) as i:
                for h in range(2):
                    add_up(2 * i + h, h, True)
            add_up(NG - 3, 0, True)
            add_up(NG - 2, 1, False)
            add_up(NG - 1, 0, False)

            def means(n, i, wait):
                dve.wait_ge(wait, ready(i * U + U - 1))
                dve.nop(nofuse=True)
                dve.tensor_scalar(tiny[:, 4, 0:U], tiny[:, 3, 0:U], -1.0 / C, None, ALU.mult).then_inc(mean_ready[n], 1)

            def normalise(n, i, done):
                dve.wait_ge(dev_ready[n], i + 1)
                dve.nop(nofuse=True)
                dve.reciprocal(tiny[:, 7, 0:U], tiny[:, 6, 0:U])
                dve.drain()
                for j in range(U):
                    dve.tensor_scalar(tok[:, j, :], tok[:, j, :], tiny[:, 4, j:j + 1], tiny[:, 7, j:j + 1], ALU.add, ALU.mult)\
                        .then_inc(done, 1)

            with dve.Fori(0, TURNS) as i:
                for j in range(U):
                    dve.wait_ge(ring_q_sb, ready(i * U + j))
                    dve.nop(nofuse=True)
                    dve.tensor_scalar(neg[:, j, :], wide[:, j, 0:C], 0.0, None, ALU.min).then_inc(ring_qneg, 1)
                for j in range(U):
                    dve.wait_ge(ring_qexp, ready(i * U + j))
                    dve.nop(nofuse=True)
                    dve.scalar_tensor_tensor(wide[:, j, 0:C], wide[:, j, 0:C], 0.0, neg[:, j, :], ALU.max, ALU.add).then_inc(ring_qelu, 1)
                for j in range(U):
                    dve.wait_ge(ring_att, ready(i * U + j))
                    dve.wait_ge(ring_n3_kept, free(i * U + j))
                    dve.nop(nofuse=True)
                    both = bank[j][:, 0:KC * (P + HPC)].rearrange("p (m c) -> p m c", m=KC)
                    z = tiny[:, 0, 0:KC * HPC].rearrange("p (m a) -> p m a", m=KC)
                    dve.tensor_scalar(z, both[:, :, P:P + HPC], ATT_EPS, None, ALU.add)
                    dve.drain()
                    dve.reciprocal(tiny[:, 1, 0:KC * HPC], tiny[:, 0, 0:KC * HPC])
                    dve.drain()
                    for m in range(KC):
                        last = dve.scalar_tensor_tensor(
                            tok[:, j, m * P:(m + 1) * P].rearrange("p (a d) -> p a d", a=HPC),
                            both[:, m, 0:P].rearrange("p (a d) -> p a d", a=HPC), float(N),
                            tiny[:, 1, m * HPC:(m + 1) * HPC].unsqueeze(2).to_broadcast([P, HPC, HD]), ALU.mult, ALU.mult)
                    last.then_inc(ring_msg, 1)
                means(0, i, ring_mm_sb)
                normalise(0, i, ring_n1)
                means(1, i, ring_h2_sb)
                normalise(1, i, ring_n2)
                dve.drain()
                for j in range(U):
                    dve.tensor_tensor(tok[:, j, :], tok[:, j, :], g2r[:, :], ALU.mult)
                dve.drain()
                for j in range(U):
                    dve.wait_ge(x_base, i * U + j + 1)
                    dve.nop(nofuse=True)
                    dve.tensor_tensor(tok[:, j, :], tok[:, j, :], x_again[:, j, :], ALU.add)
                dve.drain()
                for j in range(U):
                    dve.wait_ge(ring_gnn, ready(i * U + j))
                    dve.nop(nofuse=True)
                    dve.tensor_tensor(tok[:, j, :], bank[j][:, 0:C], tok[:, j, :], ALU.add).then_inc(ring_x1, 1)
                means(2, i, ring_x1_kept)
                normalise(2, i, ring_n3)
                for j in range(U):
                    dve.wait_ge(ring_gate, ready(i * U + j))
                    dve.nop(nofuse=True)
                    dve.tensor_tensor(tile_of(logits, i, j), bank[j][:, 0:NE], gate_row[:, :], ALU.add).then_inc(ring_logit, 1)

            dve.drain()
            top = routing(NT)
            hot1, hot2 = routing(NT, NE), routing(NT, NE)
            cand = routing(NT, NE)
            pick, first, total = routing(NT), routing(NT), routing(NT)
            iota_e = iota[:, 0:NE].unsqueeze(1).to_broadcast([P, NT, NE])

            def wide_of(a):
                return a.unsqueeze(2).to_broadcast([P, NT, NE])

            dve.tensor_reduce(top, logits[:, :, :], AX, ALU.max)
            dve.drain()
            dve.tensor_tensor(logits[:, :, :], logits[:, :, :], wide_of(top), ALU.subtract).then_inc(logits_neg, 1)
            dve.wait_ge(exp_ready, 1)
            dve.tensor_reduce(total, logits[:, :, :], AX, ALU.add)
            dve.drain()
            dve.reciprocal(total, total)
            dve.drain()
            dve.tensor_tensor(logits[:, :, :], logits[:, :, :], wide_of(total), ALU.mult)
            dve.drain()
            for c, chosen in ((0, hot1), (1, hot2)):
                dve.tensor_reduce(gates[:, c, :], logits[:, :, :], AX, ALU.max)
                dve.drain()
                dve.tensor_tensor(cand, logits[:, :, :], wide_of(gates[:, c, :]), ALU.not_equal)
                dve.drain()
                dve.scalar_tensor_tensor(cand, cand, float(NE), iota_e, ALU.mult, ALU.add)
                dve.drain()
                dve.tensor_reduce(pick, cand, AX, ALU.min)
                dve.drain()
                dve.tensor_tensor(chosen, iota_e, wide_of(pick), ALU.is_equal)
                dve.drain()
                if c == 0:
                    dve.scalar_tensor_tensor(logits[:, :, :], hot1, -2.0, logits[:, :, :], ALU.mult, ALU.add)
                    dve.drain()
            dve.tensor_tensor(total, gates[:, 0, :], gates[:, 1, :], ALU.add)
            dve.drain()
            dve.reciprocal(total, total)
            dve.drain()
            for c in range(2):
                dve.tensor_tensor(gates[:, c, :], gates[:, c, :], total, ALU.mult)
            taken = routing(NE, NT)
            run = routing(1 + NE * NT)
            by_expert = "p t e -> p e t"
            dve.tensor_tensor(cand, hot1, hot2, ALU.add)
            dve.drain()
            dve.tensor_tensor(taken, cand.rearrange(by_expert), valid[:, :].unsqueeze(1).to_broadcast([P, NE, NT]), ALU.mult)
            dve.memset(run[:, 0:1], 0.0)
            dve.drain()
            flat = taken.rearrange("p e t -> p (e t)")
            dve.tensor_tensor_scan(run[:, 1:1 + NE * NT], flat, flat, 0.0, ALU.add, ALU.max)
            dve.drain()
            begin = run[:, 0:NE * NT].rearrange("p (e t) -> p e t", t=NT)[:, :, 0]
            end = run[:, 1:1 + NE * NT].rearrange("p (e t) -> p e t", t=NT)[:, :, NT - 1]
            dve.tensor_tensor(tiny[:, 0, 0:NE], end, begin, ALU.subtract).then_inc(choice_counts, 1)
            dve.wait_ge(choice_prefix, 1)
            tiles_i = routing(NE, dt=I32)
            dve.tensor_scalar(tiles_i, bank[7][:, 32:32 + NE], float(P - 1), None, ALU.add)
            dve.drain()
            dve.tensor_scalar(tiles_i, tiles_i, 7, None, ALU.arith_shift_right)
            dve.drain()
            dve.tensor_copy(tiny[:, 1, 0:NE], tiles_i)
            dve.drain()
            dve.tensor_tensor_scan(tiny[:, 2, 0:NE], tiny[:, 1, 0:NE], tiny[:, 1, 0:NE], 0.0, ALU.add, ALU.max)
            dve.drain()
            dve.tensor_tensor(tiny[:, 3, 0:NE], tiny[:, 2, 0:NE], tiny[:, 1, 0:NE], ALU.subtract)
            dve.drain()
            dve.scalar_tensor_tensor(tiny[:, 3, 0:NE], tiny[:, 3, 0:NE], float(P), begin, ALU.mult, ALU.subtract)
            dve.drain()
            dve.tensor_tensor(tiny[:, 3, 0:NE], bank[7][:, 0:NE], tiny[:, 3, 0:NE], ALU.add)
            dve.drain()
            spot = run[:, 0:NE * NT].rearrange("p (e t) -> p e t", t=NT)
            dve.tensor_tensor(spot, spot, tiny[:, 3, 0:NE].unsqueeze(2).to_broadcast([P, NE, NT]), ALU.add)
            dve.drain()
            for c, chosen in ((0, hot1), (1, hot2)):
                dve.tensor_tensor(taken, spot, chosen.rearrange(by_expert), ALU.mult)
                dve.drain()
                dve.tensor_reduce(first, taken.rearrange("p e t -> p t e"), AX, ALU.add)
                dve.drain()
                dve.tensor_copy(slots[:, c, :], first)
                dve.drain()
            over = routing(ETILES, NE)
            dve.tensor_tensor(over[0:1], tiny[0:1, 2, 0:NE].unsqueeze(1).to_broadcast([1, ETILES, NE]),
                              iota[0:1, 0:ETILES].unsqueeze(2).to_broadcast([1, ETILES, NE]), ALU.is_le)
            dve.drain()
            last_of = routing(ETILES)
            dve.tensor_reduce(last_of[0:1], over[0:1], AX, ALU.add)
            dve.drain()
            dve.tensor_scalar(last_of[0:1], last_of[0:1], float(NE - 1), None, ALU.min)
            dve.drain()
            dve.tensor_copy(owner[:, :], last_of[0:1])
            dve.drain().then_inc(slots_ready, 1)

            def slot_of(i, n):
                return slots[:, :, 0:NT - 1].rearrange("p c (a b) -> p c a b", b=DT)[:, :, bass.ds(i, 1), n].rearrange("p c a -> p (c a)")

            def dense_of(a, i, n):
                return a[:, 0:NT - 1, :].rearrange("p (a b) c -> p a b c", b=DT)[:, bass.ds(i, 1), n, :].rearrange("p a c -> p (a c)")

            dve.wait_ge(ring_n3_kept, ready(NT - 1))
            for n in range(DT):
                dve.tensor_copy(s_x[:, n, :], agg[:, n, :])
                dve.tensor_copy(s_at[:, n, :], slots[:, :, n])
                dve.drain().then_inc(s_copied, 1)
            with dve.Fori(1, (NT - 1) // DT) as i:
                for n in range(DT):
                    dve.wait_ge(scattered[n], 32 * i)
                    dve.nop(nofuse=True)
                    dve.tensor_copy(s_x[:, n, :], dense_of(agg, i, n))
                    dve.tensor_copy(s_at[:, n, :], slot_of(i, n))
                    dve.drain().then_inc(s_copied, 1)
            dve.wait_ge(scattered[0], 32 * (NT - 1) // DT)
            dve.tensor_copy(s_x[:, 0, :], agg[:, NT - 1, :])
            dve.tensor_copy(s_at[:, 0, :], slots[:, :, NT - 1])
            dve.drain().then_inc(s_copied, 1)

            with dve.Fori(0, ETILES // 2) as i:
                for h in range(2):
                    n = 2 * i + h
                    dve.wait_ge(e_turned, n + 3)
                    dve.wait_ge(e_h2, n + 1)
                    dve.nop(nofuse=True)
                    dve.tensor_copy(e_xT[:, h, :], bank[4 + h][:, 0:C]).then_inc(e_feat, 1)
                    dve.wait_ge(e_silu, n + 3)
                    dve.wait_ge(e_h2, n + 3)
                    dve.wait_ge(e_out, n + 1)
                    dve.nop(nofuse=True)
                    dve.tensor_tensor(e_hid[:, h, :], bank[2 + h][:, :], e_act[:, h, :], ALU.mult).then_inc(e_hidden, 1)

            def combine(n, rows_n, x1, g_1, g_2):
                dve.scalar_tensor_tensor(c_out[0:rows_n, n, :], c_y1[0:rows_n, n, :], g_1, x1, ALU.mult, ALU.add)
                dve.drain()
                dve.scalar_tensor_tensor(c_out[0:rows_n, n, :], c_y2[0:rows_n, n, :], g_2, c_out[0:rows_n, n, :], ALU.mult, ALU.add)\
                    .then_inc(y_summed, 1)

            def gate_of(c, i, n):
                return gates[:, c, 0:NT - 1].rearrange("p (a b) -> p a b", b=DT)[:, bass.ds(i, 1), n]

            for h in range(2):
                dve.wait_ge(e_stored[h], 16 * (ETILES // 2 + 1))
            with dve.Fori(0, (NT - 1) // DT) as i:
                for n in range(DT):
                    dve.tensor_copy(s_at[:, n, :], slot_of(i, n))
                    dve.drain().then_inc(s_copied, 1)
                for n in range(DT):
                    dve.wait_ge(y_gathered[n], 32 * i + 32)
                    dve.wait_ge(y_stored[n], 16 * i + 16)
                    dve.nop(nofuse=True)
                    combine(n, P, dense_of(xn, i, n), gate_of(0, i, n), gate_of(1, i, n))
            dve.tensor_copy(s_at[:, 0, :], slots[:, :, NT - 1])
            dve.drain().then_inc(s_copied, 1)
            dve.wait_ge(y_gathered[0], 32 * ((NT - 1) // DT) + 32)
            dve.wait_ge(y_stored[0], 16 * (NT - 1) // DT + 16)
            combine(0, LAST, xn[0:LAST, NT - 1, :], gates[0:LAST, 0, NT - 1:NT], gates[0:LAST, 1, NT - 1:NT])


_INS = ['x', 'src', 'dst', 'edge_weight', 'L0_gnn_W', 'L0_gnn_b', 'L0_mix_Wq', 'L0_mix_Wk', 'L0_mix_Wv', 'L0_mix_Wm',
        'L0_mix_W1', 'L0_mix_W2', 'L0_mix_g1', 'L0_mix_b1', 'L0_mix_g2', 'L0_mix_b2', 'L0_ffn_gate_w', 'L0_ffn_gate_b',
        'L0_ffn_w1', 'L0_ffn_w2', 'L0_ffn_w3']
_OUTS = [((3125, 256), 'float32')]


def kernel(**inputs):
    import numpy as _np
    import concourse.bacc as _bacc
    from concourse import mybir as _mybir
    from concourse.bass_utils import run_bass_kernel_spmd as _run

    nc = _bacc.Bacc("TRN2", target_bir_lowering=False, num_devices=1)
    arrays, args = {}, []
    for name in _INS:
        a = _np.ascontiguousarray(inputs[name])
        arrays[f"in_{name}_dram"] = a
        args.append(nc.dram_tensor(f"in_{name}_dram", a.shape, _mybir.dt.from_np(a.dtype), kind="ExternalInput").ap())
    for i, (shape, dtype) in enumerate(_OUTS):
        dt = _mybir.dt.from_np(_np.dtype(dtype))
        args.append(nc.dram_tensor(f"out_{i}_dram", shape, dt, kind="ExternalOutput").ap())
    gps_layer(nc, *args)
    r = _run(nc, [arrays], core_ids=[0])
    return r.results[0]["out_0_dram"]
```

```python
from contextlib import ExitStack

import concourse.bass as bass
from concourse import mybir

ALU = mybir.AluOpType
ACT = mybir.ActivationFunctionType
F32 = mybir.dt.float32
BF16 = mybir.dt.bfloat16
I32 = mybir.dt.int32
AX = mybir.AxisListType.X
DVE = (mybir.EngineType.DVE,)
PE = (mybir.EngineType.PE,)
SP = (mybir.EngineType.SP,)

P = 128
U = 5
LN_EPS = 1e-5
ATT_EPS = 1e-6
HEADS = 8


def gps_layer(nc, x, src, dst, edge_weight, gnn_W, gnn_b, Wq, Wk, Wv, Wm, W1, W2, g1, b1, g2, b2,
              gate_w, gate_b, ew1, ew2, ew3, out):
    N, C = x.shape
    KC = C // P
    NT = -(-N // P)
    LAST = N - (NT - 1) * P
    TURNS = NT // U
    E = src.shape[0]
    GE = 25
    EP = N // GE
    NG = E // (EP * GE)
    GT = -(-(EP * GE) // P)
    BINS = NT
    STEPS = GT + BINS - 1
    SU = 7
    PIECES = 6
    REC = STEPS + (PIECES - 1) * GT
    GC = 5
    HID = W1.shape[1]
    HC = HID // P
    NE = gate_w.shape[1]
    EH = ew1.shape[2]
    EHC = EH // P
    ETILES = (2 * N + NE * (P - 1)) // P
    HD = C // HEADS
    HPC = P // HD
    WS = 4
    DT = 6
    assert NT == U * TURNS and EP * GE * NG == E and STEPS % SU == 0 and ETILES % WS == 0
    assert NG % 2 == 1 and (NT - 1) % DT == 0

    xn_rows = nc.dram_tensor("xn_rows", [N, C], F32).ap()
    slot_rows = nc.dram_tensor("slot_rows", [ETILES * P, C], F32).ap()
    expert_rows = nc.dram_tensor("expert_rows", [ETILES * P, C], F32).ap()

    with ExitStack() as ctx:
        def sb(name, shape, dt=F32):
            return ctx.enter_context(nc.sbuf_tensor(name, shape, dt))

        def sem(name):
            return ctx.enter_context(nc.semaphore(name))

        xn = sb("xn", [P, NT, C])
        xnT = sb("xnT", [P, KC, NT * P])
        agg = sb("agg", [P, NT, C])
        arena = sb("arena", [P, 2 * NT * C])
        rows = [arena[:, h * NT * C:h * NT * C + GT * C].rearrange("p (t c) -> p t c", c=C) for h in range(2)]
        ident = sb("ident", [P, P])
        iota = sb("iota", [P, P])
        iota1 = sb("iota1", [P, P])
        before = sb("before", [P, P])
        after = sb("after", [P, P])
        ones = sb("ones", [P, P])
        valid = sb("valid", [P, NT])
        wq = sb("wq", [P, KC, C])
        wkv = sb("wkv", [P, KC, 2 * C])
        wm = sb("wm", [P, KC, C])
        gnn_raw = xnT[:, 0, 0:KC * C].rearrange("p (k c) -> p k c", k=KC)
        gnnT = sb("gnnT", [P, KC, C])
        w1 = sb("w1", [P, 2 * KC, HID])
        w2 = sb("w2", [P, HC, C])
        gw = sb("gw", [P, KC, NE])
        g1c = sb("g1c", [P, KC])
        b1c = sb("b1c", [P, KC])
        g2r = sb("g2r", [P, C])
        bias_row = sb("bias_row", [P, 2, C])
        gate_row = sb("gate_row", [P, NE])
        KV = sb("KV", [P, KC, P + 1])
        KVd = sb("KVd", [P, KC, P + HPC])
        logits = sb("logits", [P, NT, NE])
        slots = sb("slots", [P, 2, NT], I32)
        gates = sb("gates", [P, 2, NT])
        owner = sb("owner", [1, ETILES], I32)
        tiny = sb("tiny", [P, 8, 32])
        epsc = sb("epsc", [P, 1])
        stat = sb("stat", [P, 3, U, 10])
        s_at = sb("s_at", [P, DT, 2], I32)
        edge_i = sb("edge_i", [EP, 3, NG * GE], I32)
        src_i, dst_i, part_i = edge_i[:, 0, :], edge_i[:, 1, :], edge_i[:, 2, :]
        wgt = sb("wgt", [EP, NG * GE])
        bin_f = sb("bin_f", [EP, NG * GE])
        piece = sb("piece", [EP, PIECES, NG * GE], BF16)
        in_bin = sb("in_bin", [EP, BINS, GE])
        count = sb("count", [EP, 1 + BINS * GE])
        in_tile = sb("in_tile", [EP, GE, GT], BF16)
        in_slot = sb("in_slot", [EP, GE, P], BF16)
        in_step = sb("in_step", [EP, GE, STEPS], BF16)
        record = sb("record", [EP, GE, REC], BF16)
        ordered = sb("ordered", [P, PIECES - 1, GT])
        place_i = sb("place_i", [EP, 3, GE], I32)
        place_f = sb("place_f", [EP, 2, GE])
        ends = sb("ends", [BINS, 1])
        boundary = sb("boundary", [BINS, STEPS])
        meets = sb("meets", [BINS, STEPS])
        pair_f = sb("pair_f", [1, STEPS])
        pairs = [sb(f"pairs{h}", [1, 2, STEPS], I32) for h in range(2)]
        gather_i = [sb(f"gather_i{h}", [P, GT], I32) for h in range(2)]
        node = [sb(f"node{h}", [P, STEPS]) for h in range(2)]
        weight = [sb(f"weight{h}", [P, GT]) for h in range(2)]
        zero = sb("zero", [P, P])
        hot = xn[:, :, :].rearrange("p t c -> p (t c)")[:, 0:STEPS * P].rearrange("p (k c) -> p k c", c=P)

        at = [NT * C]

        def ring(width, slots_=U, start=None):
            if start is not None:
                at[0] = start
            a = arena[:, at[0]:at[0] + slots_ * width].rearrange("p (s c) -> p s c", c=width)
            at[0] += slots_ * width
            return a

        tok = ring(C)
        feat = ring(C)
        neg = ring(C)
        wide = ring(2 * C)
        assert at[0] <= 2 * NT * C
        e_xT = ring(C, 2, 0)
        e_act = ring(EH, 2)
        e_hid = ring(EH, 2)
        e_y = ring(C, 2)
        e_space = xnT[:, :, :].rearrange("p k n -> p (k n)")
        slot_size = 2 * KC * EH + EHC * C
        e_slots = [arena[:, at[0] + s * slot_size:at[0] + (s + 1) * slot_size] for s in range(WS - 1)] + [e_space[:, 0:slot_size]]
        e_w1, e_w2, e_w3 = ([a[:, b:b + n] for a in e_slots]
                            for b, n in ((0, KC * EH), (KC * EH, KC * EH), (2 * KC * EH, EHC * C)))
        assert at[0] + (WS - 1) * slot_size <= 2 * NT * C
        e_x = e_space[:, slot_size:slot_size + WS * C].rearrange("p (s c) -> p s c", c=C)
        s_x = e_space[:, slot_size + WS * C:slot_size + (WS + DT) * C].rearrange("p (s c) -> p s c", c=C)
        x_again = ring(C, U, 0)
        nbr = ring(C)
        xn_again = ring(C)
        n3 = ring(C)
        nbrT = ring(C, 2)
        n3T = ring(C, 2)
        assert at[0] <= NT * C
        c_y1 = ring(C, DT, 0)
        c_y2 = ring(C, DT)
        c_out = ring(C, DT)
        squares = arena[:, 0:NT * C].rearrange("p (t c) -> p t c", c=C)
        r_at = [0]

        def routing(*shape, dt=F32):
            n = 1
            for s in shape:
                n *= s
            a = arena[:, r_at[0]:r_at[0] + n]
            r_at[0] += n
            if len(shape) == 2:
                a = a.rearrange("p (a b) -> p a b", b=shape[1])
            return a if dt == F32 else a.bitcast(dt)

        psum = ctx.enter_context(nc.psum_tensor("psum", [P, 8 * 512], F32))
        bank = [psum[:, i * 512:(i + 1) * 512] for i in range(8)]
        sums = psum[:, 0:BINS * P].rearrange("p (b c) -> p b c", c=P)
        BPB = 512 // P
        BANKS = -(-BINS // BPB)
        HANDOVER = {0: (0, 1), 2 * BPB: (2, 3), 4 * BPB: tuple(range(4, BANKS))}

        x_loaded, edges_loaded, weights_loaded, zero_pad = sem("x_loaded"), sem("edges_loaded"), sem("weights_loaded"), sem("zero_pad")
        consts_ready, var_ready, std_ready, xn_ready, xn_stored = sem("consts_ready"), sem("var_ready"), sem("std_ready"), sem("xn_ready"), sem("xn_stored")
        gnn_turned, gnnT_ready = sem("gnn_turned"), sem("gnnT_ready")
        ring_tok, ring_turned, ring_feat, ring_kept = sem("ring_tok"), sem("ring_turned"), sem("ring_feat"), sem("ring_kept")
        ring_kv, ring_kv_sb, ring_kneg, ring_kexp, ring_k = sem("ring_kv"), sem("ring_kv_sb"), sem("ring_kneg"), sem("ring_kexp"), sem("ring_k")
        kv_part, kv_added, kvd_ready = sem("kv_part"), sem("kv_added"), sem("kvd_ready")
        counts_ready, prefix_ready, record_ready, ordered_ready, list_ready = sem("counts_ready"), sem("prefix_ready"), sem("record_ready"), sem("ordered_ready"), sem("list_ready")
        hot_ready, met, flushed, group_added = sem("hot_ready"), sem("met"), sem("flushed"), sem("group_added")
        gathered = [[sem(f"gathered{h}_{q}") for q in range(GT // GC)] for h in range(2)]
        scaled, places_ready, slot_hot_ready = sem("scaled"), sem("places_ready"), sem("slot_hot_ready")
        ordered_read = sem("ordered_read")
        x_back, x_base = sem("x_back"), sem("x_base")
        ring_q, ring_qneg, ring_qexp, ring_qelu = sem("ring_q"), sem("ring_qneg"), sem("ring_qexp"), sem("ring_qelu")
        ring_att, ring_msg, ring_msgT, ring_msgT_sb = sem("ring_att"), sem("ring_msg"), sem("ring_msgT"), sem("ring_msgT_sb")
        ring_mm, ring_n1, ring_n1T, ring_n1T_sb = sem("ring_mm"), sem("ring_n1"), sem("ring_n1T"), sem("ring_n1T_sb")
        ring_h, ring_h_sb, ring_h2, ring_h2_read = sem("ring_h"), sem("ring_h_sb"), sem("ring_h2"), sem("ring_h2_read")
        ring_nbr, ring_nbrT, ring_nbrT_sb, ring_gnn, ring_gnn_sb, ring_x1 = sem("ring_nbr"), sem("ring_nbrT"), sem("ring_nbrT_sb"), sem("ring_gnn"), sem("ring_gnn_sb"), sem("ring_x1")
        ring_n3, ring_n3_kept, ring_n3T, ring_n3T_sb, ring_gate, logits_made = sem("ring_n3"), sem("ring_n3_kept"), sem("ring_n3T"), sem("ring_n3T_sb"), sem("ring_gate"), sem("logits_made")
        ring_var = [sem(f"ring_var{n}") for n in range(3)]
        ring_std = [sem(f"ring_std{n}") for n in range(3)]
        logits_neg, exp_ready, choice_counts, choice_prefix, slots_ready = sem("logits_neg"), sem("exp_ready"), sem("choice_counts"), sem("choice_prefix"), sem("slots_ready")
        slots_zeroed = sem("slots_zeroed")
        s_copied, scattered = sem("s_copied"), [sem(f"scattered{n}") for n in range(DT)]
        e_weights = [sem(f"e_weights{s}") for s in range(WS)]
        e_rows = [sem(f"e_rows{s}") for s in range(WS)]
        e_turned, e_feat, e_h1, e_h2, e_silu, e_hidden, e_out, e_out_sb = (
            sem("e_turned"), sem("e_feat"), sem("e_h1"), sem("e_h2"), sem("e_silu"), sem("e_hidden"), sem("e_out"), sem("e_out_sb"))
        e_stored = [sem("e_stored0"), sem("e_stored1")]
        y_gathered, y_summed, y_stored = [sem(f"y_gathered{n}") for n in range(DT)], sem("y_summed"), [sem(f"y_stored{n}") for n in range(DT)]

        def ready(t):
            return t + 1 + U

        def free(t):
            return t + 1

        def tile_of(a, i, j):
            return a[:].rearrange("p (a b) c -> p a b c", b=U)[:, bass.ds(i, 1), j, :].rearrange("p a c -> p (a c)")

        def xnT_of(k, i, j):
            return xnT[:, k, :].rearrange("p (a b c) -> p a b c", b=U, c=P)[:, bass.ds(i, 1), j, :].rearrange("p a c -> p (a c)")

        def edges_of(a, g):
            return a.rearrange("p (g c) -> p g c", c=GE)[:, bass.ds(g, 1), :].rearrange("p g c -> p (g c)")

        count_begin = count[:, 0:BINS * GE].rearrange("p (b c) -> p b c", c=GE)[:, :, 0]
        count_end = count[:, 1:1 + BINS * GE].rearrange("p (b c) -> p b c", c=GE)[:, :, GE - 1]
        x_tiles = x[0:(NT - 1) * P, :].rearrange("(t p) c -> p t c", p=P)
        block = ctx.enter_context(nc.Block())

        @block.sync
        def _(sp):
            sp.dma_start(xn[:, 0:NT - 1, :], x_tiles).then_inc(x_loaded, 16)
            sp.wait_ge(zero_pad, 1)
            sp.dma_start(xn[0:LAST, NT - 1, :], x[(NT - 1) * P:N, :]).then_inc(x_loaded, 16)
            for a, b in ((src_i, src), (dst_i, dst), (wgt[:, :], edge_weight)):
                sp.dma_start(a, b.rearrange("(p c) -> p c", p=EP)).then_inc(edges_loaded, 16)
            chunks = "(k p) n -> p k n"
            loads = [(wkv[:, :, 0:C], Wk.rearrange(chunks, p=P)), (wkv[:, :, C:2 * C], Wv.rearrange(chunks, p=P)),
                     (wq[:, :, :], Wq.rearrange(chunks, p=P)), (wm[:, :, :], Wm.rearrange(chunks, p=P)),
                     (gnn_raw[:, :, :], gnn_W.rearrange(chunks, p=P)), (w1[:, :, :], W1.rearrange(chunks, p=P)),
                     (w2[:, :, :], W2.rearrange(chunks, p=P)), (gw[:, :, :], gate_w.rearrange(chunks, p=P)),
                     (g2r[:, :], g2.rearrange("(a c) -> a c", a=1).to_broadcast([P, C])),
                     (bias_row[:, 0, :], b2.rearrange("(a c) -> a c", a=1).to_broadcast([P, C])),
                     (bias_row[:, 1, :], gnn_b.rearrange("(a c) -> a c", a=1).to_broadcast([P, C])),
                     (gate_row[:, :], gate_b.rearrange("(a c) -> a c", a=1).to_broadcast([P, NE]))]
            for a, b in loads:
                sp.dma_start(a, b).then_inc(weights_loaded, 16)
            with nc.allow_non_contiguous_dma(reason="two short columns"):
                for k in range(KC):
                    sp.dma_start(g1c[:, k:k + 1], g1[k * P:(k + 1) * P].rearrange("(p a) -> p a", a=1)).then_inc(weights_loaded, 16)
                    sp.dma_start(b1c[:, k:k + 1], b1[k * P:(k + 1) * P].rearrange("(p a) -> p a", a=1)).then_inc(weights_loaded, 16)
            sp.wait_ge(consts_ready, 1)
            sp.dma_start(slot_rows.rearrange("(p t) c -> p t c", p=P),
                         agg[:, 0, :].unsqueeze(1).to_broadcast([P, ETILES, C])).then_inc(slots_zeroed, 16)
            sp.wait_ge(xn_ready, 1)
            sp.dma_start(xn_rows[0:(NT - 1) * P, :].rearrange("(t p) c -> p t c", p=P), xn[:, 0:NT - 1, :]).then_inc(xn_stored, 16)
            sp.dma_start(xn_rows[(NT - 1) * P:N, :], xn[0:LAST, NT - 1, :]).then_inc(xn_stored, 16)
            sp.wait_ge(group_added, NG)
            xn_tiles = xn_rows[0:(NT - 1) * P, :].rearrange("(t p) c -> p t c", p=P)
            for i in range(TURNS):
                if i >= 1:
                    sp.wait_ge(ring_x1, ready(i * U - 1))
                for a, tiles, rest in ((x_again, x_tiles, x), (xn_again, xn_tiles, xn_rows)):
                    sp.dma_start(a[:, 0:U - 1, :], tiles[:, i * U:i * U + U - 1, :]).then_inc(x_back, 16)
                    if i < TURNS - 1:
                        sp.dma_start(a[:, U - 1, :], tiles[:, i * U + U - 1, :]).then_inc(x_back, 16)
                    else:
                        sp.dma_start(a[0:LAST, U - 1, :], rest[(NT - 1) * P:N, :]).then_inc(x_back, 16)
            def e_owner(q, s):
                return nc.values_load(owner[0:1, :].rearrange("p (a b) -> p a b", b=WS)[:, bass.ds(q, 1), s], engines=SP,
                                   min_val=0, max_val=NE - 1,
                                   skip_runtime_bounds_check_because="it is a minimum with NE - 1 of a count")

            def e_load_rows(q, s):
                sp.dma_start(e_x[:, s, :], slot_rows.rearrange("(a b p) c -> a b p c", b=WS, p=P)[bass.ds(q, 1), s, :, :]
                             .rearrange("a p c -> (a p) c")).then_inc(e_rows[s], 16)

            def e_load_weights(e, s, kinds):
                for w, b, k in kinds:
                    sp.dma_start(w[s].rearrange("p (k n) -> p k n", k=k),
                                 b.rearrange("e (k p) n -> e p k n", p=P)[bass.ds(e, 1), :, :, :].rearrange("e p k n -> (e p) k n"))\
                        .then_inc(e_weights[s], 16)

            up, down = ((e_w1, ew1, KC), (e_w2, ew2, KC)), ((e_w3, ew3, EHC),)
            sp.wait_ge(slots_ready, 1)
            sp.wait_ge(ring_n3_kept, ready(NT - 1))
            for s in range(WS):
                e_load_weights(e_owner(0, s), s, up + down)
            for n in range(DT):
                sp.wait_ge(scattered[n], 32 * (NT - 1) // DT + (32 if n == 0 else 0))
            for s in range(WS):
                e_load_rows(0, s)
            with sp.Fori(1, ETILES // WS) as q:
                for s in range(WS):
                    n = q * WS + s
                    e = e_owner(q, s)
                    sp.wait_ge(e_h2, n - WS + 3)
                    sp.nop(nofuse=True)
                    e_load_rows(q, s)
                    e_load_weights(e, s, up)
                    sp.wait_ge(e_out, n - WS + 3)
                    sp.nop(nofuse=True)
                    e_load_weights(e, s, down)
            with sp.Fori(0, (NT - 1) // DT) as i:
                for n in range(DT):
                    sp.wait_ge(y_summed, i * DT + n + 1 + DT)
                    sp.nop(nofuse=True)
                    sp.dma_start(out[0:(NT - 1) * P, :].rearrange("(a b p) c -> a b p c", b=DT, p=P)[bass.ds(i, 1), n, :, :]
                                 .rearrange("a p c -> (a p) c"), c_out[:, n, :]).then_inc(y_stored[n], 16)
            sp.wait_ge(y_summed, NT + DT)
            sp.dma_start(out[(NT - 1) * P:N, :], c_out[0:LAST, 0, :]).then_inc(y_stored[0], 16)
            for n in range(DT):
                sp.wait_ge(y_stored[n], 16 + 16 * (NT - 1) // DT + (16 if n == 0 else 0))

        @block.scalar
        def _(act):
            for s in (ring_tok, ring_kv_sb, ring_kexp, ring_qexp, ring_msgT_sb, ring_n1T_sb,
                      ring_h_sb, ring_nbrT_sb, ring_gnn_sb, ring_n3T_sb, *ring_std):
                act.sem_inc(s, U)
            act.sem_inc(e_silu, 2)
            for n in range(DT):
                act.sem_inc(y_stored[n], 16)
            act.wait_ge(consts_ready, 1)
            act.wait_ge(var_ready, 1)
            act.activation(tiny[:, 2, 0:NT], tiny[:, 1, 0:NT], ACT.Sqrt, scale=1.0 / C, bias=epsc[:, 0:1]).then_inc(std_ready, 1)
            act.wait_ge(gnn_turned, 1)
            act.activation(gnnT[:, :, :], bank[7][:, :].rearrange("p (k n) -> p k n", k=KC), ACT.Copy).then_inc(gnnT_ready, 1)

            act.wait_ge(xn_ready, 1)
            with act.Fori(0, TURNS) as i:
                for j in range(U):
                    t = i * U + j
                    act.wait_ge(ring_turned, free(t))
                    act.nop(nofuse=True)
                    act.activation(tok[:, j, :], tile_of(xn, i, j), ACT.Copy).then_inc(ring_tok, 1)
                for j in range(U):
                    t = i * U + j
                    act.wait_ge(ring_kv, ready(t))
                    act.wait_ge(kv_part, i + 1)
                    act.nop(nofuse=True)
                    act.activation(wide[:, j, :], bank[j][:, :], ACT.Copy).then_inc(ring_kv_sb, 1)
                for j in range(U):
                    t = i * U + j
                    act.wait_ge(ring_kneg, ready(t))
                    act.nop(nofuse=True)
                    act.activation(neg[:, j, :], neg[:, j, :], ACT.Exp).then_inc(ring_kexp, 1)

            def slot_hot(g):
                act.wait_ge(places_ready, g + 1)
                if isinstance(g, int) and g == 0:
                    act.wait_ge(consts_ready, 1)
                act.nop(nofuse=True)
                for c in range(GE):
                    act.activation(in_slot[:, c, :], iota[0:EP, :], ACT.Abs, bias=place_f[:, 0, c:c + 1])
                act.drain()
                act.activation(in_slot[:, :, :], in_slot[:, :, :], ACT.Relu, scale=-1.0, bias=1.0).then_inc(slot_hot_ready, 1)

            def scale_rows(g_half, h, chunks):
                for q in chunks:
                    act.wait_ge(gathered[h][q], 16 * GC * (g_half + 1))
                    act.nop(nofuse=True)
                    for t in range(q * GC, (q + 1) * GC):
                        last = act.activation(rows[h][:, t, :], rows[h][:, t, :], ACT.Copy, scale=weight[h][:, t:t + 1])
                    last.then_inc(scaled, 1)

            early, late = range(0, 2), range(2, GT // GC)
            slot_hot(0)
            slot_hot(1)
            scale_rows(0, 0, early)
            scale_rows(0, 0, late)
            with act.Fori(0, (NG - 3) // 2) as i:
                scale_rows(i, 1, early)
                slot_hot(2 * i + 2)
                scale_rows(i, 1, late)
                scale_rows(i + 1, 0, early)
                slot_hot(2 * i + 3)
                scale_rows(i + 1, 0, late)
            scale_rows((NG - 3) // 2, 1, early)
            slot_hot(NG - 1)
            scale_rows((NG - 3) // 2, 1, late)
            scale_rows((NG - 1) // 2, 0, range(GT // GC))

            act.wait_ge(weights_loaded, 16 * 16)
            act.wait_ge(group_added, NG)
            def q_exp(i, j):
                act.wait_ge(ring_qneg, ready(i * U + j))
                act.nop(nofuse=True)
                act.activation(neg[:, j, :], neg[:, j, :], ACT.Exp).then_inc(ring_qexp, 1)

            def copy_out(i, j, produced, b, to, done):
                act.wait_ge(produced, ready(i * U + j))
                act.nop(nofuse=True)
                act.activation(to, bank[b][:, 0:C], ACT.Copy).then_inc(done, 1)

            def nbr_turned(i, j):
                copy_out(i, j, ring_nbrT, 5 + j % 2, nbrT[:, j % 2, :], ring_nbrT_sb)

            def nbr_projected(i, j):
                copy_out(i, j, ring_gnn, 7, nbr[:, j, :], ring_gnn_sb)

            def n3_turned(i, j):
                copy_out(i, j, ring_n3T, 5 + j % 2, n3T[:, j % 2, :], ring_n3T_sb)

            def std(n, i, j):
                act.wait_ge(ring_var[n], ready(i * U + j))
                act.nop(nofuse=True)
                act.activation(stat[:, n, j, 8:9], stat[:, n, j, 7:8], ACT.Sqrt, bias=epsc[:, 0:1]).then_inc(ring_std[n], 1)

            def n1_turned(i, j):
                act.wait_ge(ring_n1T, ready(i * U + j))
                act.nop(nofuse=True)
                for k in range(KC):
                    last = act.activation(feat[:, j, k * P:(k + 1) * P], bank[j][:, k * P:(k + 1) * P], ACT.Identity,
                                          scale=g1c[:, k:k + 1], bias=b1c[:, k:k + 1])
                last.then_inc(ring_n1T_sb, 1)

            def hidden(i, j):
                act.wait_ge(ring_h, ready(i * U + j))
                act.nop(nofuse=True)
                act.activation(wide[:, j, :], bank[j][:, :], ACT.Relu).then_inc(ring_h_sb, 1)

            def dense(i, before):
                act.preload_act_table(ACT.Exp)
                for step, j in ((q_exp, 0), (nbr_turned, 0), (q_exp, 1), (nbr_turned, 1), (q_exp, 2), (nbr_projected, 0),
                                (nbr_turned, 2), (q_exp, 3), (nbr_projected, 1), (nbr_turned, 3), (q_exp, 4),
                                (nbr_projected, 2), (nbr_turned, 4), (nbr_projected, 3), (nbr_projected, 4)):
                    step(i, j)
                act.preload_act_table(ACT.Sqrt)
                for j in range(U):
                    copy_out(i, j, ring_msgT, j, feat[:, j, :], ring_msgT_sb)
                for j in range(U):
                    std(0, i, j)
                    if 1 <= j < 3:
                        n1_turned(i, j - 1)
                for j in range(U):
                    hidden(i, j)
                    if j + 2 < U:
                        n1_turned(i, j + 2)
                    if before is not None:
                        for t in ((0, 1, 2), (3, 4), (), (), ())[j]:
                            std(2, before, t)
                        for t in ((), (0, 1), (2, 3), (4,), ())[j]:
                            n3_turned(before, t)
                for j in range(U):
                    std(1, i, j)

            dense(0, None)
            with act.Fori(1, TURNS) as i:
                dense(i, i - 1)
            for j in range(U + 1):
                if j < U:
                    std(2, TURNS - 1, j)
                if j >= 1:
                    n3_turned(TURNS - 1, j - 1)

            act.wait_ge(logits_neg, 1)
            act.activation(logits[:, :, :], logits[:, :, :], ACT.Exp).then_inc(exp_ready, 1)

            with act.Fori(0, ETILES // 2) as i:
                for h in range(2):
                    n = 2 * i + h
                    act.wait_ge(e_h1, n + 3)
                    act.wait_ge(e_hidden, n + 1)
                    act.nop(nofuse=True)
                    act.activation(e_act[:, h, :], bank[h][:, :], ACT.Silu).then_inc(e_silu, 1)

            def at_slots(n, tile):
                act.activation(s_at[:, n, :], tile, ACT.Copy).then_inc(s_copied, 1)

            for n in range(DT):
                at_slots(n, slots[:, :, n])
            with act.Fori(1, (NT - 1) // DT) as i:
                for n in range(DT):
                    act.wait_ge(y_gathered[n], 32 * i)
                    act.nop(nofuse=True)
                    at_slots(n, slots[:, :, 0:NT - 1].rearrange("p c (a b) -> p c a b", b=DT)[:, :, bass.ds(i, 1), n].rearrange("p c a -> p (c a)"))
            act.wait_ge(y_gathered[0], 32 * (NT - 1) // DT)
            at_slots(0, slots[:, :, NT - 1])

        @block.gpsimd
        def _(pool):
            for s in (ring_kept, ring_nbr, ring_n3_kept):
                pool.sem_inc(s, U)
            pool.memset(xn[:, NT - 1, :], 0.0)
            pool.drain().then_inc(zero_pad, 1)
            pool.memset(epsc[:, :], LN_EPS)
            pool.memset(ones[:, :], 1.0)
            pool.memset(zero[:, :], 0.0)
            pool.memset(ident[:, :], 0.0)
            pool.memset(before[:, :], 1.0)
            pool.memset(after[:, :], 1.0)
            pool.memset(valid[:, :], 1.0)
            pool.memset(KV[:, :, :], 0.0)
            pool.memset(KVd[:, :, :], 0.0)
            pool.memset(agg[:, :, :], 0.0)
            pool.memset(count[:, 0:1], 0.0)
            pool.drain()
            pool.affine_select(out=ident[:, :], in_=ident[:, :], compare_op=ALU.not_equal, fill=1.0, base=0,
                               pattern=[[-1, P]], channel_multiplier=1)
            pool.affine_select(out=before[:, :], in_=before[:, :], compare_op=ALU.is_gt, fill=0.0, base=0,
                               pattern=[[1, P]], channel_multiplier=-1)
            pool.affine_select(out=after[:, :], in_=after[:, :], compare_op=ALU.is_gt, fill=0.0, base=0,
                               pattern=[[-1, P]], channel_multiplier=1)
            pool.affine_select(out=valid[:, NT - 1:NT], in_=valid[:, NT - 1:NT], compare_op=ALU.is_gt, fill=0.0, base=LAST,
                               pattern=[[0, 1]], channel_multiplier=-1)
            pool.iota(iota1[:, :], [[1, P]], base=1, channel_multiplier=0, allow_small_or_imprecise_dtypes=True)
            pool.iota(iota[:, :], [[1, P]], base=0, channel_multiplier=0, allow_small_or_imprecise_dtypes=True)
            pool.iota(boundary[:, :], [[P, STEPS]], base=0, channel_multiplier=-P, allow_small_or_imprecise_dtypes=True)
            pool.drain().then_inc(consts_ready, 1)

            with pool.Fori(0, TURNS) as i:
                for j in range(U):
                    pool.wait_ge(ring_feat, ready(i * U + j))
                    pool.nop(nofuse=True)
                    for k in range(KC):
                        last = pool.tensor_copy(xnT_of(k, i, j), feat[:, j, k * P:(k + 1) * P])
                    last.then_inc(ring_kept, 1)

            def gather(g, h, first):
                pool.wait_ge(list_ready, g + 1)
                if not first:
                    pool.wait_ge(group_added, g - 1)
                pool.nop(nofuse=True)
                for t in range(GT):
                    pool.indirect_dma_start(rows[h][:, t, :], None, xn_rows,
                                            bass.IndirectOffsetOnAxis(ap=gather_i[h][:, t:t + 1], axis=0)).then_inc(gathered[h][t // GC], 16)

            pool.wait_ge(xn_stored, 32)
            pool.drain()
            pool.wait_ge(kvd_ready, 1)
            gather(0, 0, True)
            gather(1, 1, True)
            with pool.Fori(0, (NG - 3) // 2) as i:
                for h in range(2):
                    gather(2 * i + h + 2, h, False)
            gather(NG - 1, 0, False)

            pool.wait_ge(weights_loaded, 16 * 16)
            pool.tensor_tensor(bias_row[:, 0, :], bias_row[:, 0, :], bias_row[:, 1, :], ALU.add)
            pool.drain()
            def n3_copies(i):
                for j in range(U):
                    pool.wait_ge(ring_n3, ready(i * U + j))
                    pool.nop(nofuse=True)
                    pool.tensor_copy(tile_of(agg, i, j), n3[:, j, :]).then_inc(ring_n3_kept, 1)

            def base(i):
                for j in range(U):
                    pool.tensor_copy(nbr[:, j, :], tile_of(agg, i, j)).then_inc(ring_nbr, 1)
                pool.wait_ge(x_back, 64 * i + 64)
                pool.nop(nofuse=True)
                for j in range(U):
                    pool.tensor_tensor(x_again[:, j, :], x_again[:, j, :], bias_row[:, 0, :], ALU.add)
                pool.drain()
                for j in range(U):
                    pool.tensor_tensor(x_again[:, j, :], x_again[:, j, :], xn_again[:, j, :], ALU.add)
                pool.drain()
                for j in range(U):
                    pool.wait_ge(ring_gnn_sb, ready(i * U + j))
                    pool.nop(nofuse=True)
                    pool.tensor_tensor(x_again[:, j, :], x_again[:, j, :], nbr[:, j, :], ALU.add).then_inc(x_base, 1)
                pool.drain()

            pool.wait_ge(group_added, NG)
            base(0)
            with pool.Fori(1, TURNS) as i:
                base(i)
                n3_copies(i - 1)
            n3_copies(TURNS - 1)

            pool.wait_ge(slots_ready, 1)
            pool.wait_ge(slots_zeroed, 16)

            def scatter(n, rows_n):
                for c in range(2):
                    pool.indirect_dma_start(slot_rows, bass.IndirectOffsetOnAxis(ap=s_at[0:rows_n, n, c:c + 1], axis=0),
                                            s_x[0:rows_n, n, :], None).then_inc(scattered[n], 16)

            with pool.Fori(0, (NT - 1) // DT) as i:
                for n in range(DT):
                    pool.wait_ge(s_copied, i * DT + n + 1)
                    pool.nop(nofuse=True)
                    scatter(n, P)
            pool.wait_ge(s_copied, NT)
            scatter(0, LAST)

            def collect(n, rows_n):
                for c, y in ((0, c_y1), (1, c_y2)):
                    pool.indirect_dma_start(y[0:rows_n, n, :], None, expert_rows,
                                            bass.IndirectOffsetOnAxis(ap=s_at[0:rows_n, n, c:c + 1], axis=0)).then_inc(y_gathered[n], 16)

            with pool.Fori(0, ETILES // 2) as i:
                for h in range(2):
                    pool.wait_ge(e_out_sb, 2 * i + h + 3)
                    pool.nop(nofuse=True)
                    pool.dma_start(expert_rows.rearrange("(a b p) c -> a b p c", b=2, p=P)[bass.ds(i, 1), h, :, :]
                                   .rearrange("a p c -> (a p) c"), e_y[:, h, :]).then_inc(e_stored[h], 16)
            for h in range(2):
                pool.wait_ge(e_stored[h], 16 * ETILES // 2)
            with pool.Fori(0, (NT - 1) // DT) as i:
                for n in range(DT):
                    pool.wait_ge(s_copied, NT + i * DT + n + 1)
                    pool.wait_ge(y_summed, i * DT + n + 1)
                    pool.nop(nofuse=True)
                    collect(n, P)
            pool.wait_ge(s_copied, 2 * NT)
            pool.wait_ge(y_summed, NT)
            collect(0, LAST)

        @block.tensor
        def _(pe):
            for s in (ring_turned, ring_kv, ring_q, ring_att, ring_msgT, ring_mm, ring_n1T, ring_h, ring_h2,
                      ring_nbrT, ring_gnn, ring_n3T):
                pe.sem_inc(s, U)
            pe.sem_inc(kv_part, 1)
            for s in (e_turned, e_h1, e_h2, e_out):
                pe.sem_inc(s, 2)

            def turn(j, a, b=None):
                for k in range(KC):
                    last = pe.transpose(bank[j if b is None else b][:, k * P:(k + 1) * P], a[:, j, k * P:(k + 1) * P], ident[:, :])
                return last

            def project(j, w, n):
                for k in range(KC):
                    last = pe.matmul(bank[j][:, 0:n], feat[:, j, k * P:(k + 1) * P], w[:, k, 0:n],
                                     start=(k == 0), stop=(k == KC - 1))
                return last

            pe.wait_ge(consts_ready, 1)
            pe.wait_ge(weights_loaded, 16 * 16)
            for m in range(KC):
                for k in range(KC):
                    last = pe.transpose(bank[7][:, k * C + m * P:k * C + (m + 1) * P], gnn_raw[:, m, k * P:(k + 1) * P], ident[:, :])
            last.then_inc(gnn_turned, 1)

            with pe.Fori(0, TURNS) as i:
                for j in range(U):
                    pe.wait_ge(ring_tok, ready(i * U + j))
                    pe.wait_ge(ring_kv_sb, free(i * U + j))
                    pe.nop(nofuse=True)
                    turn(j, tok).then_inc(ring_turned, 1)
                for j in range(U):
                    pe.wait_ge(ring_feat, ready(i * U + j))
                    pe.nop(nofuse=True)
                    project(j, wkv, 2 * C).then_inc(ring_kv, 1)
                pe.wait_ge(kv_added, i + 1)
                for j in range(U):
                    pe.wait_ge(ring_k, ready(i * U + j))
                    pe.nop(nofuse=True)
                    for m in range(KC):
                        k_m = wide[:, j, m * P:(m + 1) * P]
                        pe.matmul(bank[5 + m][:, 0:P], k_m, wide[:, j, C + m * P:C + (m + 1) * P],
                                  start=(j == 0), stop=(j == U - 1), skip_group_check=True)
                        mask = valid[:, :].rearrange("p (a b) -> p a b", b=U)[:, bass.ds(i, 1), j]
                        last = pe.matmul(bank[5 + m][:, P:P + 1], k_m, mask,
                                         start=False, stop=(j == U - 1), skip_group_check=True)
                last.then_inc(kv_part, 1)

            def prefix(g):
                pe.wait_ge(counts_ready, g + 1)
                pe.nop(nofuse=True)
                pe.matmul(bank[7][0:EP, 0:BINS], before[0:EP, 0:EP], count_end, start=True, stop=False)
                pe.matmul(bank[7][0:EP, 0:BINS], after[0:EP, 0:EP], count_begin, start=False, stop=True)
                pe.matmul(bank[7][0:BINS, 32:33], count_end, ones[0:EP, 0:1], start=True, stop=True).then_inc(prefix_ready, 1)

            def reorder(g):
                pe.wait_ge(record_ready, g + 1)
                pe.wait_ge(slot_hot_ready, g + 1)
                pe.nop(nofuse=True)
                pe.matmul(bank[7][0:1, 64 + REC:64 + REC + STEPS], ones[0:BINS, 0:1], meets[:, :], start=True, stop=True)
                for c in range(GE):
                    last = pe.matmul(bank[7][:, 64:64 + REC], in_slot[:, c, :], record[:, c, :],
                                     start=(c == 0), stop=(c == GE - 1))
                last.then_inc(ordered_ready, 1)

            def add_up(g, h, ordering):
                pe.wait_ge(list_ready, g + 1)
                pe.nop(nofuse=True)
                for c in range(KC):
                    for s in range(STEPS // SU):
                        (_, row_at), (_, sum_at) = (
                            nc.values_load_multi_w_load_instructions(
                                pairs[h][0:1, a, s * SU:(s + 1) * SU], engines=PE, min_val=0, max_val=most,
                                skip_runtime_bounds_check_because="bins and tiles are clipped when the list is made")
                            for a, most in ((0, (GT - 1) * C), (1, (BINS - 1) * P)))
                        for k in range(SU):
                            n = s * SU + k
                            if n in HANDOVER:
                                banks = HANDOVER[n]
                                pe.wait_ge(flushed, (g * KC + c) * BANKS + banks[-1] + 1)
                                pe.nop(nofuse=True)
                                for b in banks:
                                    pe.matmul(bank[b][:, 0:2], zero[:, :], ident[:, 0:2], start=True, stop=True)
                            if c == 0 and n % GC == 0 and n < GT:
                                pe.wait_ge(scaled, g * (GT // GC) + n // GC + 1)
                                pe.nop(nofuse=True)
                            if c == 0 and k == 0:
                                pe.wait_ge(hot_ready, g * (STEPS // SU) + s + 1)
                                pe.nop(nofuse=True)
                            pe.matmul(psum[:, bass.ds(sum_at[k], P)], hot[:, n, :],
                                      rows[h][:, :, :].rearrange("p t c -> p (t c)")[:, c * P:][:, bass.ds(row_at[k], P)],
                                      start=False, stop=True, skip_group_check=True).then_inc(met, 1)
                            if ordering and c == 0 and n == 3 * SU:
                                prefix(g + 2)
                if ordering:
                    reorder(g + 2)

            for g in range(2):
                prefix(g)
                reorder(g)
            with pe.Fori(0, (NG - 3) // 2) as i:
                for h in range(2):
                    add_up(2 * i + h, h, True)
            add_up(NG - 3, 0, True)
            add_up(NG - 2, 1, False)
            add_up(NG - 1, 0, False)

            pe.wait_ge(group_added, NG)
            def query(i, j):
                pe.wait_ge(ring_h2_read, free(i * U + j))
                pe.wait_ge(ring_kept, ready(i * U + j))
                pe.nop(nofuse=True)
                for m in range(KC):
                    for k in range(KC):
                        last = pe.matmul(bank[j][:, m * P:(m + 1) * P], wq[:, k, m * P:(m + 1) * P], xnT_of(k, i, j),
                                         start=(k == 0), stop=(k == KC - 1))
                last.then_inc(ring_q, 1)

            def turn_nbr(i, j):
                pe.wait_ge(ring_nbr, ready(i * U + j))
                pe.nop(nofuse=True)
                turn(j, nbr, 5 + j % 2).then_inc(ring_nbrT, 1)

            def project_nbr(i, j):
                pe.wait_ge(ring_nbrT_sb, ready(i * U + j))
                pe.wait_ge(ring_gnn_sb, i * U + j + U)
                pe.nop(nofuse=True)
                for k in range(KC):
                    last = pe.matmul(bank[7][:, 0:C], nbrT[:, j % 2, k * P:(k + 1) * P], gnnT[:, k, :],
                                     start=(k == 0), stop=(k == KC - 1))
                last.then_inc(ring_gnn, 1)

            def attend(i, j):
                pe.wait_ge(ring_qelu, ready(i * U + j))
                pe.nop(nofuse=True)
                for m in range(KC):
                    last = pe.matmul(bank[j][:, m * (P + HPC):(m + 1) * (P + HPC)], wide[:, j, m * P:(m + 1) * P], KVd[:, m, :],
                                     start=True, stop=True)
                last.then_inc(ring_att, 1)

            def turn_msg(i, j):
                pe.wait_ge(ring_msg, ready(i * U + j))
                pe.nop(nofuse=True)
                turn(j, tok).then_inc(ring_msgT, 1)

            def merge(i, j):
                pe.wait_ge(ring_msgT_sb, ready(i * U + j))
                pe.nop(nofuse=True)
                project(j, wm, C).then_inc(ring_mm, 1)

            def turn_n1(i, j):
                pe.wait_ge(ring_n1, ready(i * U + j))
                pe.nop(nofuse=True)
                turn(j, tok).then_inc(ring_n1T, 1)

            def hidden(i, j):
                pe.wait_ge(ring_n1T_sb, ready(i * U + j))
                pe.nop(nofuse=True)
                for m in range(HC):
                    for k in range(2 * KC):
                        operand = xnT_of(k, i, j) if k < KC else feat[:, j, (k - KC) * P:(k - KC + 1) * P]
                        last = pe.matmul(bank[j][:, m * P:(m + 1) * P], w1[:, k, m * P:(m + 1) * P], operand,
                                         start=(k == 0), stop=(k == 2 * KC - 1))
                last.then_inc(ring_h, 1)

            def hidden_down(i, j):
                pe.wait_ge(ring_h_sb, ready(i * U + j))
                pe.nop(nofuse=True)
                for k in range(HC):
                    last = pe.matmul(bank[j][:, 0:C], wide[:, j, k * P:(k + 1) * P], w2[:, k, :],
                                     start=(k == 0), stop=(k == HC - 1))
                last.then_inc(ring_h2, 1)

            def turn_n3(i, j):
                pe.wait_ge(ring_n3, ready(i * U + j))
                pe.nop(nofuse=True)
                turn(j, n3, 5 + j % 2).then_inc(ring_n3T, 1)

            def gate(i, j):
                pe.wait_ge(ring_n3T_sb, ready(i * U + j))
                pe.nop(nofuse=True)
                for k in range(KC):
                    last = pe.matmul(bank[7][:, j * NE:(j + 1) * NE], n3T[:, j % 2, k * P:(k + 1) * P], gw[:, k, :],
                                     start=(k == 0), stop=(k == KC - 1))
                if j == U - 1:
                    last.then_inc(ring_gate, 1)

            def dense(i, before):
                for j in range(U):
                    query(i, j)
                if before is not None:
                    pe.wait_ge(logits_made, before + 1)
                for step, j in ((turn_nbr, 0), (turn_nbr, 1), (project_nbr, 0), (turn_nbr, 2), (project_nbr, 1), (turn_nbr, 3),
                                (project_nbr, 2), (turn_nbr, 4), (project_nbr, 3), (project_nbr, 4)):
                    step(i, j)
                for j in range(U):
                    attend(i, j)
                for j in range(U + 1):
                    if j < U:
                        turn_msg(i, j)
                    if j >= 1:
                        merge(i, j - 1)
                turn_n1(i, 0)
                for j in range(U):
                    if j + 1 < U:
                        turn_n1(i, j + 1)
                    hidden(i, j)
                    if before is not None:
                        for step, t in ((), ((turn_n3, 0), (turn_n3, 1)), ((gate, 0), (gate, 1), (turn_n3, 2), (turn_n3, 3)),
                                        ((gate, 2), (gate, 3), (turn_n3, 4)), ((gate, 4),))[j]:
                            step(before, t)
                for j in range(U):
                    hidden_down(i, j)

            dense(0, None)
            with pe.Fori(1, TURNS) as i:
                dense(i, i - 1)
            for step, j in ((turn_n3, 0), (turn_n3, 1), (gate, 0), (turn_n3, 2), (gate, 1), (turn_n3, 3), (gate, 2),
                            (turn_n3, 4), (gate, 3), (gate, 4)):
                step(TURNS - 1, j)

            pe.wait_ge(choice_counts, 1)
            pe.matmul(bank[7][:, 0:NE], before[:, :], tiny[:, 0, 0:NE], start=True, stop=True)
            pe.matmul(bank[7][:, 32:32 + NE], ones[:, :], tiny[:, 0, 0:NE], start=True, stop=True).then_inc(choice_prefix, 1)

            def e_turn(n, q, s):
                h = s % 2
                pe.wait_ge(e_rows[s], 16 * q + 16)
                pe.wait_ge(e_feat, n + 1)
                pe.nop(nofuse=True)
                for k in range(KC):
                    last = pe.transpose(bank[4 + h][:, k * P:(k + 1) * P], e_x[:, s, k * P:(k + 1) * P], ident[:, :])
                last.then_inc(e_turned, 1)

            def e_up(n, q, s):
                h = s % 2
                pe.wait_ge(e_feat, n + 3)
                pe.wait_ge(e_weights[s], 48 * q + 48)
                pe.wait_ge(e_hidden, n + 1)
                pe.nop(nofuse=True)
                for b, w, done in ((h, e_w1, e_h1), (2 + h, e_w2, e_h2)):
                    for m in range(EHC):
                        for k in range(KC):
                            last = pe.matmul(bank[b][:, m * P:(m + 1) * P], w[s][:, k * EH + m * P:k * EH + (m + 1) * P],
                                             e_xT[:, h, k * P:(k + 1) * P], start=(k == 0), stop=(k == KC - 1))
                    last.then_inc(done, 1)

            def e_down(n, s):
                h = s % 2
                pe.wait_ge(e_hidden, n + 3)
                pe.wait_ge(e_out_sb, n + 1)
                pe.nop(nofuse=True)
                for k in range(EHC):
                    last = pe.matmul(bank[6 + h][:, 0:C], e_hid[:, h, k * P:(k + 1) * P], e_w3[s][:, k * C:(k + 1) * C],
                                     start=(k == 0), stop=(k == EHC - 1))
                last.then_inc(e_out, 1)

            e_turn(0, 0, 0)
            e_up(0, 0, 0)
            e_turn(1, 0, 1)
            with pe.Fori(0, ETILES // WS - 1) as q:
                for s in range(WS):
                    e_up(q * WS + s + 1, q + (s + 1) // WS, (s + 1) % WS)
                    e_turn(q * WS + s + 2, q + (s + 2) // WS, (s + 2) % WS)
                    e_down(q * WS + s, s)
            q = ETILES // WS - 1
            for s in range(WS):
                if s + 1 < WS:
                    e_up(q * WS + s + 1, q, s + 1)
                if s + 2 < WS:
                    e_turn(q * WS + s + 2, q, s + 2)
                e_down(q * WS + s, s)

        @block.vector
        def _(dve):
            for s in (ring_feat, ring_kneg, ring_k, ring_qneg, ring_qelu, ring_msg, ring_n1, ring_h2_read, ring_x1, ring_n3, *ring_var):
                dve.sem_inc(s, U)
            for s in (kv_added, logits_made):
                dve.sem_inc(s, 1)
            dve.sem_inc(y_summed, DT)
            dve.sem_inc(flushed, BANKS)
            for s in (e_feat, e_hidden, e_out_sb):
                dve.sem_inc(s, 2)

            dve.wait_ge(x_loaded, 32)
            dve.tensor_reduce(tiny[:, 0, 0:NT], xn[:, :, :], AX, ALU.add)
            dve.drain()
            dve.tensor_scalar(tiny[:, 3, 0:NT], tiny[:, 0, 0:NT], -1.0 / C, None, ALU.mult)
            dve.drain()
            dve.tensor_tensor(xn[:, :, :], xn[:, :, :], tiny[:, 3, 0:NT].unsqueeze(2).to_broadcast([P, NT, C]), ALU.add)
            dve.drain()
            dve.tensor_tensor(squares, xn[:, :, :], xn[:, :, :], ALU.mult)
            dve.drain()
            dve.tensor_reduce(tiny[:, 1, 0:NT], squares, AX, ALU.add).then_inc(var_ready, 1)
            dve.wait_ge(std_ready, 1)
            dve.reciprocal(tiny[:, 3, 0:NT], tiny[:, 2, 0:NT])
            dve.drain()
            dve.tensor_tensor(xn[:, :, :], xn[:, :, :], tiny[:, 3, 0:NT].unsqueeze(2).to_broadcast([P, NT, C]), ALU.mult)\
                .then_inc(xn_ready, 1)

            dve.wait_ge(edges_loaded, 48)
            for n, a, op, by, plus in ((None, src_i, ALU.arith_shift_right, 7, 0.0), (0, src_i, ALU.bitwise_and, P - 1, 1.0),
                                       (1, dst_i, ALU.arith_shift_right, 7, 0.0), (2, dst_i, ALU.bitwise_and, P - 1, 0.0)):
                dve.tensor_scalar(part_i, a, by, None, op)
                dve.drain()
                dve.tensor_scalar(bin_f[:, :] if n is None else piece[:, n, :], part_i, plus, None, ALU.add)
                dve.drain()
            for n in range(3, PIECES):
                dve.drain()
                dve.tensor_copy(piece[:, n, :], wgt[:, :])
                if n < PIECES - 1:
                    dve.drain()
                    dve.tensor_tensor(wgt[:, :], wgt[:, :], piece[:, n, :], ALU.subtract)
            dve.wait_ge(consts_ready, 1)

            with dve.Fori(0, TURNS) as i:
                for j in range(U):
                    t = i * U + j
                    dve.wait_ge(ring_turned, ready(t))
                    dve.wait_ge(ring_kv, free(t))
                    dve.wait_ge(ring_kept, free(t))
                    dve.nop(nofuse=True)
                    dve.tensor_copy(feat[:, j, :], bank[j][:, 0:C]).then_inc(ring_feat, 1)
                for j in range(U):
                    dve.wait_ge(ring_kv_sb, ready(i * U + j))
                    dve.nop(nofuse=True)
                    dve.tensor_scalar(neg[:, j, :], wide[:, j, 0:C], 0.0, None, ALU.min).then_inc(ring_kneg, 1)
                for j in range(U):
                    dve.wait_ge(ring_kexp, ready(i * U + j))
                    dve.nop(nofuse=True)
                    dve.scalar_tensor_tensor(wide[:, j, 0:C], wide[:, j, 0:C], 0.0, neg[:, j, :], ALU.max, ALU.add).then_inc(ring_k, 1)
                dve.wait_ge(kv_part, i + 2)
                dve.nop(nofuse=True)
                for m in range(KC):
                    last = dve.tensor_tensor(KV[:, m, :], bank[5 + m][:, 0:P + 1], KV[:, m, :], ALU.add)
                last.then_inc(kv_added, 1)
            dve.drain()
            dve.tensor_scalar(KV[:, :, 0:P], KV[:, :, 0:P], 1.0 / N, None, ALU.mult)
            dve.drain()
            for a in range(HPC):
                own = slice(a * HD, (a + 1) * HD)
                dve.tensor_copy(KVd[own, :, a * HD:(a + 1) * HD], KV[own, :, a * HD:(a + 1) * HD])
                dve.tensor_copy(KVd[own, :, P + a:P + a + 1], KV[own, :, P:P + 1])
            dve.drain().then_inc(kvd_ready, 1)

            def count_bins(g):
                dve.tensor_tensor(in_bin[:, :, :], edges_of(bin_f[:, :], g).unsqueeze(1).to_broadcast([EP, BINS, GE]),
                                  iota[0:EP, 0:BINS].unsqueeze(2).to_broadcast([EP, BINS, GE]), ALU.is_equal)
                dve.drain()
                flat = in_bin[:, :, :].rearrange("p b c -> p (b c)")
                dve.tensor_tensor_scan(count[:, 1:1 + BINS * GE], flat, flat, 0.0, ALU.add, ALU.max).then_inc(counts_ready, 1)

            def find_places(g):
                dve.wait_ge(prefix_ready, g + 1)
                dve.nop(nofuse=True)
                places = count[:, 1:1 + BINS * GE].rearrange("p (b c) -> p b c", c=GE)
                dve.scalar_tensor_tensor(places, bank[7][0:EP, 0:BINS].unsqueeze(2).to_broadcast([EP, BINS, GE]), -1.0, places,
                                         ALU.add, ALU.add)
                dve.tensor_copy(ends[:, :], bank[7][0:BINS, 32:33])
                dve.drain()
                dve.tensor_tensor(places, places, in_bin[:, :, :], ALU.mult)
                dve.tensor_scalar(meets[:, :], boundary[:, :], ends[:, 0:1], None, ALU.is_gt)
                dve.drain()
                with nc.allow_low_precision(reason="each sum is one whole number and zeros"):
                    dve.tensor_reduce(place_i[:, 0, :], places.rearrange("p b c -> p c b"), AX, ALU.add)
                dve.drain()
                dve.tensor_scalar(place_i[:, 1, :], place_i[:, 0, :], 7, None, ALU.arith_shift_right)
                dve.tensor_scalar(place_i[:, 2, :], place_i[:, 0, :], P - 1, None, ALU.bitwise_and)
                dve.drain()
                dve.tensor_scalar(place_f[:, 0, :], place_i[:, 2, :], -1.0, None, ALU.mult).then_inc(places_ready, 1)
                dve.tensor_tensor(place_f[:, 1, :], place_i[:, 1, :], edges_of(bin_f[:, :], g), ALU.add)
                dve.tensor_tensor(in_tile[:, :, :], place_i[:, 1, :].unsqueeze(2).to_broadcast([EP, GE, GT]),
                                  iota[0:EP, 0:GT].unsqueeze(1).to_broadcast([EP, GE, GT]), ALU.is_equal)

            def make_records(g):
                dve.drain()
                dve.tensor_tensor(in_step[:, :, :], place_f[:, 1, :].unsqueeze(2).to_broadcast([EP, GE, STEPS]),
                                  iota[0:EP, 0:STEPS].unsqueeze(1).to_broadcast([EP, GE, STEPS]), ALU.is_equal)
                for n in range(1, PIECES):
                    dve.tensor_tensor(record[:, :, STEPS + (n - 1) * GT:STEPS + n * GT], in_tile[:, :, :],
                                      edges_of(piece[:, n, :], g).unsqueeze(2).to_broadcast([EP, GE, GT]), ALU.mult)
                dve.drain()
                dve.tensor_tensor(record[:, :, 0:STEPS], in_step[:, :, :],
                                  edges_of(piece[:, 0, :], g).unsqueeze(2).to_broadcast([EP, GE, STEPS]), ALU.mult)\
                    .then_inc(record_ready, 1)

            def make_list(g, h):
                in_order = bank[7][:, 64 + STEPS:64 + REC].rearrange("p (a b) -> p a b", b=GT)
                bins = bank[7][0:1, 64 + REC:64 + REC + STEPS]
                dve.wait_ge(ordered_ready, g + 1)
                dve.nop(nofuse=True)
                dve.tensor_tensor(pair_f[:, :], iota[0:1, 0:STEPS], bins, ALU.subtract)
                dve.tensor_scalar(pairs[h][:, 1, :], bins, float(BINS - 1), float(P), ALU.min, ALU.mult)
                dve.tensor_copy(ordered[:, :, :], in_order)
                dve.tensor_copy(node[h][:, :], bank[7][:, 64:64 + STEPS])
                dve.drain()
                dve.tensor_tensor(weight[h][:, :], ordered[:, 4, :], ordered[:, 3, :], ALU.add)
                dve.scalar_tensor_tensor(gather_i[h][:, :], ordered[:, 0, :], float(P), ordered[:, 1, :], ALU.mult, ALU.add)
                dve.tensor_scalar(pairs[h][:, 0, :], pair_f[:, :], float(GT - 1), float(C), ALU.min, ALU.mult)
                dve.drain()
                dve.tensor_tensor(weight[h][:, :], weight[h][:, :], ordered[:, 2, :], ALU.add)
                dve.drain().then_inc(list_ready, 1)

            def make_hot(h):
                for s in range(STEPS // SU):
                    own = slice(s * SU, (s + 1) * SU)
                    dve.tensor_tensor(hot[:, own, :], iota1[:, :].unsqueeze(1).to_broadcast([P, SU, P]),
                                      node[h][:, own].unsqueeze(2).to_broadcast([P, SU, P]), ALU.is_equal).then_inc(hot_ready, 1)

            def flush(g, c):
                for b in range(BANKS):
                    own = slice(b * BPB, min((b + 1) * BPB, BINS))
                    dve.wait_ge(met, (g * KC + c) * STEPS + min((b + 1) * BPB + GT - 1, STEPS))
                    dve.nop(nofuse=True)
                    dve.tensor_tensor(agg[:, own, c * P:(c + 1) * P], sums[:, own, :], agg[:, own, c * P:(c + 1) * P], ALU.add)\
                        .then_inc(flushed, 1)

            def add_up(g, h, ordering, more=True):
                if ordering:
                    count_bins(g + 2)
                    find_places(g + 2)
                for c in range(KC):
                    if ordering and c == KC - 1:
                        make_records(g + 2)
                    flush(g, c)
                dve.drain().then_inc(group_added, 1)
                if more:
                    make_hot(1 - h)
                if ordering:
                    make_list(g + 2, h)

            dve.wait_ge(slots_zeroed, 16)
            dve.wait_ge(xn_stored, 32)
            for g in range(2):
                count_bins(g)
                find_places(g)
                make_records(g)
                make_list(g, g)
            make_hot(0)
            with dve.Fori(0, (NG - 3) // 2) as i:
                for h in range(2):
                    add_up(2 * i + h, h, True)
            add_up(NG - 3, 0, True)
            add_up(NG - 2, 1, False)
            add_up(NG - 1, 0, False, more=False)

            def queries(i):
                for j in range(U + 2):
                    if j < U:
                        dve.wait_ge(ring_q, ready(i * U + j))
                        dve.nop(nofuse=True)
                        dve.tensor_scalar(neg[:, j, :], bank[j][:, 0:C], 0.0, None, ALU.min).then_inc(ring_qneg, 1)
                    if j >= 2:
                        t = j - 2
                        dve.wait_ge(ring_qexp, ready(i * U + t))
                        dve.nop(nofuse=True)
                        dve.scalar_tensor_tensor(wide[:, t, 0:C], bank[t][:, 0:C], 0.0, neg[:, t, :], ALU.max, ALU.add).then_inc(ring_qelu, 1)

            def messages(i):
                for j in range(U + 2):
                    if j >= 2:
                        t = j - 2
                        both = bank[t][:, 0:KC * (P + HPC)].rearrange("p (m c) -> p m c", m=KC)
                        for m in range(KC):
                            last = dve.scalar_tensor_tensor(
                                tok[:, t, m * P:(m + 1) * P].rearrange("p (a d) -> p a d", a=HPC),
                                both[:, m, 0:P].rearrange("p (a d) -> p a d", a=HPC), float(N),
                                tiny[:, 1, (t % 2) * KC * HPC + m * HPC:(t % 2) * KC * HPC + (m + 1) * HPC].unsqueeze(2)
                                .to_broadcast([P, HPC, HD]), ALU.mult, ALU.mult)
                        last.then_inc(ring_msg, 1)
                    if 1 <= j < U + 1:
                        t = j - 1
                        zs = slice((t % 2) * KC * HPC, (t % 2 + 1) * KC * HPC)
                        dve.reciprocal(tiny[:, 1, zs], tiny[:, 0, zs])
                    if j < U:
                        dve.wait_ge(ring_att, ready(i * U + j))
                        dve.nop(nofuse=True)
                        both = bank[j][:, 0:KC * (P + HPC)].rearrange("p (m c) -> p m c", m=KC)
                        z = tiny[:, 0, (j % 2) * KC * HPC:(j % 2 + 1) * KC * HPC].rearrange("p (m a) -> p m a", m=KC)
                        dve.tensor_scalar(z, both[:, :, P:P + HPC], ATT_EPS, None, ALU.add)
                    dve.drain()

            def layer_norm(n, i, produced, source, result):
                for j in range(U + 2):
                    if j < U:
                        if produced is not None:
                            dve.wait_ge(produced, ready(i * U + j))
                            dve.nop(nofuse=True)
                        dve.bn_stats(stat[:, n, j, 0:6], source(j))
                    if 1 <= j < U + 1:
                        dve.wait_ge(ring_std[n], ready(i * U + j - 1))
                        dve.nop(nofuse=True)
                        dve.reciprocal(stat[:, n, j - 1, 9:10], stat[:, n, j - 1, 8:9])
                    if j == U + 1 and n != 1:
                        break
                    dve.drain()
                    if j < U:
                        dve.bn_aggr(stat[:, n, j, 6:8], stat[:, n, j, 0:6]).then_inc(ring_var[n], 1)
                    result(j)

            def plain(n, source, to, done, wait=None):
                def result(j):
                    t = j - 1
                    if 0 <= t < U:
                        if wait is not None:
                            wait(t)
                        dve.tensor_scalar(to[:, t, :], source(t), stat[:, n, t, 6:7], stat[:, n, t, 9:10], ALU.subtract, ALU.mult)\
                            .then_inc(done, 1)
                return result

            def residual(i):
                def result(j):
                    if 1 <= j < U + 1:
                        t = j - 1
                        dve.scalar_tensor_tensor(tok[:, t, :], bank[t][:, 0:C], stat[:, 1, t, 6:7], g2r[:, :], ALU.subtract, ALU.mult)\
                            .then_inc(ring_h2_read, 1)
                    if j >= 2:
                        t = j - 2
                        dve.wait_ge(x_base, i * U + t + 1)
                        dve.nop(nofuse=True)
                        dve.scalar_tensor_tensor(tile_of(xn, i, t), tok[:, t, :], stat[:, 1, t, 9:10], x_again[:, t, :], ALU.mult, ALU.add)\
                            .then_inc(ring_x1, 1)
                return result

            def last_norm_and_gate(i):
                def kept(t):
                    dve.wait_ge(ring_n3_kept, free(i * U + t))
                    dve.nop(nofuse=True)

                x1 = lambda j: tile_of(xn, i, j)
                layer_norm(2, i, None, x1, plain(2, x1, n3, ring_n3, kept))
                dve.wait_ge(ring_gate, i + 1)
                dve.nop(nofuse=True)
                dve.tensor_tensor(logits[:, :, :].rearrange("p (a b) e -> p a b e", b=U)[:, bass.ds(i, 1), :, :]
                                  .rearrange("p a b e -> p (a b) e"),
                                  bank[7][:, 0:U * NE].rearrange("p (b e) -> p b e", b=U),
                                  gate_row[:, :].unsqueeze(1).to_broadcast([P, U, NE]), ALU.add).then_inc(logits_made, 1)

            def dense(i, before):
                in_bank = lambda j: bank[j][:, 0:C]
                queries(i)
                messages(i)
                layer_norm(0, i, ring_mm, in_bank, plain(0, in_bank, tok, ring_n1))
                if before is not None:
                    last_norm_and_gate(before)
                layer_norm(1, i, ring_h2, in_bank, residual(i))

            dense(0, None)
            with dve.Fori(1, TURNS) as i:
                dense(i, i - 1)
            dve.drain()
            last_norm_and_gate(TURNS - 1)

            dve.drain()
            top = routing(NT)
            hot1, hot2 = routing(NT, NE), routing(NT, NE)
            cand = routing(NT, NE)
            pick, first, total = routing(NT), routing(NT), routing(NT)
            iota_e = iota[:, 0:NE].unsqueeze(1).to_broadcast([P, NT, NE])

            def wide_of(a):
                return a.unsqueeze(2).to_broadcast([P, NT, NE])

            dve.tensor_reduce(top, logits[:, :, :], AX, ALU.max)
            dve.drain()
            dve.tensor_tensor(logits[:, :, :], logits[:, :, :], wide_of(top), ALU.subtract).then_inc(logits_neg, 1)
            dve.wait_ge(exp_ready, 1)
            dve.tensor_reduce(total, logits[:, :, :], AX, ALU.add)
            dve.drain()
            dve.reciprocal(total, total)
            dve.drain()
            dve.tensor_tensor(logits[:, :, :], logits[:, :, :], wide_of(total), ALU.mult)
            dve.drain()
            for c, chosen in ((0, hot1), (1, hot2)):
                dve.tensor_reduce(gates[:, c, :], logits[:, :, :], AX, ALU.max)
                dve.drain()
                dve.tensor_tensor(cand, logits[:, :, :], wide_of(gates[:, c, :]), ALU.not_equal)
                dve.drain()
                dve.scalar_tensor_tensor(cand, cand, float(NE), iota_e, ALU.mult, ALU.add)
                dve.drain()
                dve.tensor_reduce(pick, cand, AX, ALU.min)
                dve.drain()
                dve.tensor_tensor(chosen, iota_e, wide_of(pick), ALU.is_equal)
                dve.drain()
                if c == 0:
                    dve.scalar_tensor_tensor(logits[:, :, :], hot1, -2.0, logits[:, :, :], ALU.mult, ALU.add)
                    dve.drain()
            dve.tensor_tensor(total, gates[:, 0, :], gates[:, 1, :], ALU.add)
            dve.drain()
            dve.reciprocal(total, total)
            dve.drain()
            for c in range(2):
                dve.tensor_tensor(gates[:, c, :], gates[:, c, :], total, ALU.mult)
            taken = routing(NE, NT)
            run = routing(1 + NE * NT)
            by_expert = "p t e -> p e t"
            dve.tensor_tensor(cand, hot1, hot2, ALU.add)
            dve.drain()
            dve.tensor_tensor(taken, cand.rearrange(by_expert), valid[:, :].unsqueeze(1).to_broadcast([P, NE, NT]), ALU.mult)
            dve.memset(run[:, 0:1], 0.0)
            dve.drain()
            flat = taken.rearrange("p e t -> p (e t)")
            dve.tensor_tensor_scan(run[:, 1:1 + NE * NT], flat, flat, 0.0, ALU.add, ALU.max)
            dve.drain()
            begin = run[:, 0:NE * NT].rearrange("p (e t) -> p e t", t=NT)[:, :, 0]
            end = run[:, 1:1 + NE * NT].rearrange("p (e t) -> p e t", t=NT)[:, :, NT - 1]
            dve.tensor_tensor(tiny[:, 0, 0:NE], end, begin, ALU.subtract).then_inc(choice_counts, 1)
            dve.wait_ge(choice_prefix, 1)
            tiles_i = routing(NE, dt=I32)
            dve.tensor_scalar(tiles_i, bank[7][:, 32:32 + NE], float(P - 1), None, ALU.add)
            dve.drain()
            dve.tensor_scalar(tiles_i, tiles_i, 7, None, ALU.arith_shift_right)
            dve.drain()
            dve.tensor_copy(tiny[:, 1, 0:NE], tiles_i)
            dve.drain()
            dve.tensor_tensor_scan(tiny[:, 2, 0:NE], tiny[:, 1, 0:NE], tiny[:, 1, 0:NE], 0.0, ALU.add, ALU.max)
            dve.drain()
            dve.tensor_tensor(tiny[:, 3, 0:NE], tiny[:, 2, 0:NE], tiny[:, 1, 0:NE], ALU.subtract)
            dve.drain()
            dve.scalar_tensor_tensor(tiny[:, 3, 0:NE], tiny[:, 3, 0:NE], float(P), begin, ALU.mult, ALU.subtract)
            dve.drain()
            dve.tensor_tensor(tiny[:, 3, 0:NE], bank[7][:, 0:NE], tiny[:, 3, 0:NE], ALU.add)
            dve.drain()
            spot = run[:, 0:NE * NT].rearrange("p (e t) -> p e t", t=NT)
            dve.tensor_tensor(spot, spot, tiny[:, 3, 0:NE].unsqueeze(2).to_broadcast([P, NE, NT]), ALU.add)
            dve.drain()
            for c, chosen in ((0, hot1), (1, hot2)):
                dve.tensor_tensor(taken, spot, chosen.rearrange(by_expert), ALU.mult)
                dve.drain()
                dve.tensor_reduce(first, taken.rearrange("p e t -> p t e"), AX, ALU.add)
                dve.drain()
                dve.tensor_copy(slots[:, c, :], first)
                dve.drain()
            over = routing(ETILES, NE)
            dve.tensor_tensor(over[0:1], tiny[0:1, 2, 0:NE].unsqueeze(1).to_broadcast([1, ETILES, NE]),
                              iota[0:1, 0:ETILES].unsqueeze(2).to_broadcast([1, ETILES, NE]), ALU.is_le)
            dve.drain()
            last_of = routing(ETILES)
            dve.tensor_reduce(last_of[0:1], over[0:1], AX, ALU.add)
            dve.drain()
            dve.tensor_scalar(last_of[0:1], last_of[0:1], float(NE - 1), None, ALU.min)
            dve.drain()
            dve.tensor_copy(owner[:, :], last_of[0:1])
            dve.drain().then_inc(slots_ready, 1)

            def slot_of(i, n):
                return slots[:, :, 0:NT - 1].rearrange("p c (a b) -> p c a b", b=DT)[:, :, bass.ds(i, 1), n].rearrange("p c a -> p (c a)")

            def dense_of(a, i, n):
                return a[:, 0:NT - 1, :].rearrange("p (a b) c -> p a b c", b=DT)[:, bass.ds(i, 1), n, :].rearrange("p a c -> p (a c)")

            dve.wait_ge(ring_n3_kept, ready(NT - 1))
            for n in range(DT):
                dve.tensor_copy(s_x[:, n, :], agg[:, n, :])
                dve.tensor_copy(s_at[:, n, :], slots[:, :, n])
                dve.drain().then_inc(s_copied, 1)
            with dve.Fori(1, (NT - 1) // DT) as i:
                for n in range(DT):
                    dve.wait_ge(scattered[n], 32 * i)
                    dve.nop(nofuse=True)
                    dve.tensor_copy(s_x[:, n, :], dense_of(agg, i, n))
                    dve.tensor_copy(s_at[:, n, :], slot_of(i, n))
                    dve.drain().then_inc(s_copied, 1)
            dve.wait_ge(scattered[0], 32 * (NT - 1) // DT)
            dve.tensor_copy(s_x[:, 0, :], agg[:, NT - 1, :])
            dve.tensor_copy(s_at[:, 0, :], slots[:, :, NT - 1])
            dve.drain().then_inc(s_copied, 1)

            def e_feature(n, h):
                dve.wait_ge(e_turned, n + 3)
                dve.wait_ge(e_h2, n + 1)
                dve.nop(nofuse=True)
                dve.tensor_copy(e_xT[:, h, :], bank[4 + h][:, 0:C]).then_inc(e_feat, 1)

            def e_gated(n, h):
                dve.wait_ge(e_silu, n + 3)
                dve.wait_ge(e_h2, n + 3)
                dve.wait_ge(e_out, n + 1)
                dve.nop(nofuse=True)
                dve.tensor_tensor(e_hid[:, h, :], bank[2 + h][:, :], e_act[:, h, :], ALU.mult).then_inc(e_hidden, 1)

            def e_result(n, n_half, h):
                dve.wait_ge(e_out, n + 3)
                if n_half is not None:
                    dve.wait_ge(e_stored[h], 16 * n_half)
                dve.nop(nofuse=True)
                dve.tensor_copy(e_y[:, h, :], bank[6 + h][:, 0:C]).then_inc(e_out_sb, 1)

            e_feature(0, 0)
            e_gated(0, 0)
            e_feature(1, 1)
            for h in range(2):
                e_gated(h + 1, 1 - h)
                e_feature(h + 2, h)
                e_result(h, None, h)
            with dve.Fori(1, ETILES // 2 - 1) as i:
                for h in range(2):
                    e_gated(2 * i + h + 1, 1 - h)
                    e_feature(2 * i + h + 2, h)
                    e_result(2 * i + h, i, h)
            e_gated(ETILES - 1, 1)
            e_result(ETILES - 2, ETILES // 2 - 1, 0)
            e_result(ETILES - 1, ETILES // 2 - 1, 1)

            def combine(n, rows_n, x1, g_1, g_2):
                dve.scalar_tensor_tensor(c_out[0:rows_n, n, :], c_y1[0:rows_n, n, :], g_1, x1, ALU.mult, ALU.add)
                dve.drain()
                dve.scalar_tensor_tensor(c_out[0:rows_n, n, :], c_y2[0:rows_n, n, :], g_2, c_out[0:rows_n, n, :], ALU.mult, ALU.add)\
                    .then_inc(y_summed, 1)

            def gate_of(c, i, n):
                return gates[:, c, 0:NT - 1].rearrange("p (a b) -> p a b", b=DT)[:, bass.ds(i, 1), n]

            with dve.Fori(0, (NT - 1) // DT) as i:
                for n in range(DT):
                    dve.wait_ge(y_gathered[n], 32 * i + 32)
                    dve.wait_ge(y_stored[n], 16 * i + 16)
                    dve.nop(nofuse=True)
                    combine(n, P, dense_of(xn, i, n), gate_of(0, i, n), gate_of(1, i, n))
            dve.wait_ge(y_gathered[0], 32 * ((NT - 1) // DT) + 32)
            dve.wait_ge(y_stored[0], 16 * (NT - 1) // DT + 16)
            combine(0, LAST, xn[0:LAST, NT - 1, :], gates[0:LAST, 0, NT - 1:NT], gates[0:LAST, 1, NT - 1:NT])


_INS = ['x', 'src', 'dst', 'edge_weight', 'L0_gnn_W', 'L0_gnn_b', 'L0_mix_Wq', 'L0_mix_Wk', 'L0_mix_Wv', 'L0_mix_Wm',
        'L0_mix_W1', 'L0_mix_W2', 'L0_mix_g1', 'L0_mix_b1', 'L0_mix_g2', 'L0_mix_b2', 'L0_ffn_gate_w', 'L0_ffn_gate_b',
        'L0_ffn_w1', 'L0_ffn_w2', 'L0_ffn_w3']
_OUTS = [((3125, 256), 'float32')]


def kernel(**inputs):
    import numpy as _np
    import concourse.bacc as _bacc
    from concourse import mybir as _mybir
    from concourse.bass_utils import run_bass_kernel_spmd as _run

    nc = _bacc.Bacc("TRN2", target_bir_lowering=False, num_devices=1)
    arrays, args = {}, []
    for name in _INS:
        a = _np.ascontiguousarray(inputs[name])
        arrays[f"in_{name}_dram"] = a
        args.append(nc.dram_tensor(f"in_{name}_dram", a.shape, _mybir.dt.from_np(a.dtype), kind="ExternalInput").ap())
    for i, (shape, dtype) in enumerate(_OUTS):
        dt = _mybir.dt.from_np(_np.dtype(dtype))
        args.append(nc.dram_tensor(f"out_{i}_dram", shape, dt, kind="ExternalOutput").ap())
    gps_layer(nc, *args)
    r = _run(nc, [arrays], core_ids=[0])
    return r.results[0]["out_0_dram"]
```

```python
from contextlib import ExitStack

import concourse.bass as bass
from concourse import mybir

ALU = mybir.AluOpType
ACT = mybir.ActivationFunctionType
F32 = mybir.dt.float32
BF16 = mybir.dt.bfloat16
I32 = mybir.dt.int32
AX = mybir.AxisListType.X
DVE = (mybir.EngineType.DVE,)
PE = (mybir.EngineType.PE,)
SP = (mybir.EngineType.SP,)

P = 128
U = 5
LN_EPS = 1e-5
ATT_EPS = 1e-6
HEADS = 8


def gps_layer(nc, x, src, dst, edge_weight, gnn_W, gnn_b, Wq, Wk, Wv, Wm, W1, W2, g1, b1, g2, b2,
              gate_w, gate_b, ew1, ew2, ew3, out):
    N, C = x.shape
    KC = C // P
    NT = -(-N // P)
    LAST = N - (NT - 1) * P
    TURNS = NT // U
    E = src.shape[0]
    GE = 25
    EP = N // GE
    NG = E // (EP * GE)
    GT = -(-(EP * GE) // P)
    BINS = NT
    STEPS = GT + BINS - 1
    SU = 7
    PIECES = 6
    REC = STEPS + (PIECES - 1) * GT
    GC = 5
    HID = W1.shape[1]
    HC = HID // P
    NE = gate_w.shape[1]
    EH = ew1.shape[2]
    EHC = EH // P
    ETILES = (2 * N + NE * (P - 1)) // P
    HD = C // HEADS
    HPC = P // HD
    WS = 4
    DT = 6
    assert NT == U * TURNS and EP * GE * NG == E and STEPS % SU == 0 and ETILES % WS == 0
    assert NG % 2 == 1 and (NT - 1) % DT == 0

    xn_rows = nc.dram_tensor("xn_rows", [N, C], F32).ap()
    n3_rows = nc.dram_tensor("n3_rows", [N, C], F32).ap()
    expert_rows = nc.dram_tensor("expert_rows", [ETILES * P, C], F32).ap()

    with ExitStack() as ctx:
        def sb(name, shape, dt=F32):
            return ctx.enter_context(nc.sbuf_tensor(name, shape, dt))

        def sem(name):
            return ctx.enter_context(nc.semaphore(name))

        xn = sb("xn", [P, NT, C])
        xnT = sb("xnT", [P, KC, NT * P])
        agg = sb("agg", [P, NT, C])
        arena = sb("arena", [P, 2 * NT * C])
        rows = [arena[:, h * NT * C:h * NT * C + GT * C].rearrange("p (t c) -> p t c", c=C) for h in range(2)]
        ident = sb("ident", [P, P])
        iota = sb("iota", [P, P])
        iota1 = sb("iota1", [P, P])
        before = sb("before", [P, P])
        after = sb("after", [P, P])
        ones = sb("ones", [P, P])
        valid = sb("valid", [P, NT])
        wq = sb("wq", [P, KC, C])
        wkv = sb("wkv", [P, KC, 2 * C])
        wm = sb("wm", [P, KC, C])
        gnn_raw = xnT[:, 0, 0:KC * C].rearrange("p (k c) -> p k c", k=KC)
        gnnT = sb("gnnT", [P, KC, C])
        w1 = sb("w1", [P, 2 * KC, HID])
        w2 = sb("w2", [P, HC, C])
        gw = sb("gw", [P, KC, NE])
        g1c = sb("g1c", [P, KC])
        b1c = sb("b1c", [P, KC])
        g2r = sb("g2r", [P, C])
        bias_row = sb("bias_row", [P, 2, C])
        gate_row = sb("gate_row", [P, NE])
        values = sb("values", [P, U, KC, P + 1])
        KV = sb("KV", [P, KC, P + 1])
        KVd = sb("KVd", [P, KC, P + HPC])
        logits = sb("logits", [P, NT, NE])
        slots = sb("slots", [P, 2, NT], I32)
        slot_parts = sb("slot_parts", [P, 2, 2, NT], I32)
        token = sb("token", [P, NT, 2])
        token_tile = sb("token_tile", [P, ETILES])
        token_of = sb("token_of", [P, ETILES], I32)
        e_at = sb("e_at", [P, WS], I32)
        gates = sb("gates", [P, 2, NT])
        owner = sb("owner", [1, ETILES], I32)
        tiny = sb("tiny", [P, 8, 32])
        epsc = sb("epsc", [P, 1])
        x_stat = sb("x_stat", [P, NT, 8])
        x_root = sb("x_root", [P, 2, NT])
        stat = sb("stat", [P, 3, U, 10])
        s_at = sb("s_at", [P, DT, 2], I32)
        edge_i = sb("edge_i", [EP, 3, NG * GE], I32)
        src_i, dst_i, part_i = edge_i[:, 0, :], edge_i[:, 1, :], edge_i[:, 2, :]
        wgt = sb("wgt", [EP, NG * GE])
        bin_f = sb("bin_f", [EP, NG * GE])
        piece = sb("piece", [EP, PIECES, NG * GE], BF16)
        in_bin = sb("in_bin", [EP, BINS, GE])
        count = sb("count", [EP, 1 + BINS * GE])
        in_tile = sb("in_tile", [EP, GE, GT], BF16)
        in_slot = sb("in_slot", [EP, GE, P], BF16)
        in_step = sb("in_step", [EP, GE, STEPS], BF16)
        record = sb("record", [EP, GE, REC], BF16)
        ordered = sb("ordered", [P, PIECES - 1, GT])
        place_i = sb("place_i", [EP, 3, GE], I32)
        place_f = sb("place_f", [EP, 2, GE])
        ends = sb("ends", [BINS, 1])
        boundary = sb("boundary", [BINS, STEPS])
        meets = sb("meets", [BINS, STEPS])
        pair_f = sb("pair_f", [1, STEPS])
        pairs = [sb(f"pairs{h}", [1, 2, STEPS], I32) for h in range(2)]
        gather_i = [sb(f"gather_i{h}", [P, GT], I32) for h in range(2)]
        node = [sb(f"node{h}", [P, STEPS]) for h in range(2)]
        weight = [sb(f"weight{h}", [P, GT]) for h in range(2)]
        zero = sb("zero", [P, P])
        hot = xn[:, :, :].rearrange("p t c -> p (t c)")[:, 0:STEPS * P].rearrange("p (k c) -> p k c", c=P)

        at = [NT * C]

        def ring(width, slots_=U, start=None):
            if start is not None:
                at[0] = start
            a = arena[:, at[0]:at[0] + slots_ * width].rearrange("p (s c) -> p s c", c=width)
            at[0] += slots_ * width
            return a

        tok = ring(C)
        feat = ring(C)
        neg = ring(C)
        wide = ring(2 * C)
        assert at[0] <= 2 * NT * C
        e_xT = ring(C, 2, 0)
        e_act = ring(EH, 2)
        e_hid = ring(EH, 2)
        e_y = ring(C, 2)
        e_space = xnT[:, :, :].rearrange("p k n -> p (k n)")
        slot_size = 2 * KC * EH + EHC * C
        e_slots = [arena[:, at[0] + s * slot_size:at[0] + (s + 1) * slot_size] for s in range(WS - 1)] + [e_space[:, 0:slot_size]]
        e_w1, e_w2, e_w3 = ([a[:, b:b + n] for a in e_slots]
                            for b, n in ((0, KC * EH), (KC * EH, KC * EH), (2 * KC * EH, EHC * C)))
        assert at[0] + (WS - 1) * slot_size <= 2 * NT * C
        e_x = e_space[:, slot_size:slot_size + WS * C].rearrange("p (s c) -> p s c", c=C)
        in_place = agg[:, :, :].rearrange("p t c -> p (t c)")[:, 0:NT * P].bitcast(BF16).rearrange("p (a t s) -> p a t s", a=2, s=P)
        in_etile = e_space[:, 0:NT * ETILES].bitcast(BF16).rearrange("p (a t n) -> p a t n", a=2, n=ETILES)
        numbered = e_space[:, NT * ETILES:3 * NT * ETILES].bitcast(BF16).rearrange("p (a t b n) -> p a t b n", a=2, b=2, n=ETILES)
        x_again = ring(C, U, 0)
        nbr = ring(C)
        xn_again = ring(C)
        n3 = ring(C)
        nbrT = ring(C, 2)
        n3T = ring(C, 2)
        assert at[0] <= NT * C
        c_y1 = ring(C, DT, 0)
        c_y2 = ring(C, DT)
        c_out = ring(C, DT)
        r_at = [0]

        def routing(*shape, dt=F32):
            n = 1
            for s in shape:
                n *= s
            a = arena[:, r_at[0]:r_at[0] + n]
            r_at[0] += n
            if len(shape) == 2:
                a = a.rearrange("p (a b) -> p a b", b=shape[1])
            return a if dt == F32 else a.bitcast(dt)

        psum = ctx.enter_context(nc.psum_tensor("psum", [P, 8 * 512], F32))
        bank = [psum[:, i * 512:(i + 1) * 512] for i in range(8)]
        sums = psum[:, 0:BINS * P].rearrange("p (b c) -> p b c", c=P)
        BPB = 512 // P
        BANKS = -(-BINS // BPB)
        ROWS_BY = {0: 2, 2 * GC: 4, 4 * GC: 5}
        HOTS_BY = {0: 1, SU: 3, 3 * SU: STEPS // SU}
        HANDOVER = {0: (0, 1), 2 * BPB: (2, 3), 4 * BPB: tuple(range(4, BANKS))}

        edges_loaded, weights_loaded, first_weights, zero_pad = sem("edges_loaded"), sem("weights_loaded"), sem("first_weights"), sem("zero_pad")
        consts_ready, var_ready, std_ready, xn_ready, xn_stored = sem("consts_ready"), sem("var_ready"), sem("std_ready"), sem("xn_ready"), sem("xn_stored")
        x_loaded = [sem(f"x_loaded{i}") for i in range(TURNS)]
        gnn_turned, gnnT_ready = sem("gnn_turned"), sem("gnnT_ready")
        ring_tok, ring_turned, ring_feat, ring_kept = sem("ring_tok"), sem("ring_turned"), sem("ring_feat"), sem("ring_kept")
        ring_kv, ring_v, ring_kexp, ring_k = sem("ring_kv"), sem("ring_v"), sem("ring_kexp"), sem("ring_k")
        kv_summed, kvd_ready = sem("kv_summed"), sem("kvd_ready")
        counts_ready, prefix_ready, record_ready, ordered_ready, list_ready = sem("counts_ready"), sem("prefix_ready"), sem("record_ready"), sem("ordered_ready"), sem("list_ready")
        hot_ready, met, flushed, group_added = sem("hot_ready"), sem("met"), sem("flushed"), sem("group_added")
        gathered = [[sem(f"gathered{h}_{q}") for q in range(GT // GC)] for h in range(2)]
        scaled, places_ready, slot_hot_ready = sem("scaled"), sem("places_ready"), sem("slot_hot_ready")
        x_back, x_base = sem("x_back"), sem("x_base")
        ring_q, ring_qneg, ring_qexp, ring_qelu = sem("ring_q"), sem("ring_qneg"), sem("ring_qexp"), sem("ring_qelu")
        ring_att, ring_msg, ring_msgT, ring_msgT_sb = sem("ring_att"), sem("ring_msg"), sem("ring_msgT"), sem("ring_msgT_sb")
        ring_mm, ring_n1, ring_n1T, ring_n1T_sb = sem("ring_mm"), sem("ring_n1"), sem("ring_n1T"), sem("ring_n1T_sb")
        ring_h, ring_h_sb, ring_h2, ring_h2_read = sem("ring_h"), sem("ring_h_sb"), sem("ring_h2"), sem("ring_h2_read")
        ring_nbr, ring_nbrT, ring_nbrT_sb, ring_gnn, ring_gnn_sb, ring_x1 = sem("ring_nbr"), sem("ring_nbrT"), sem("ring_nbrT_sb"), sem("ring_gnn"), sem("ring_gnn_sb"), sem("ring_x1")
        ring_n3, n3_stored, ring_n3T, ring_n3T_sb, ring_gate, logits_made = sem("ring_n3"), sem("n3_stored"), sem("ring_n3T"), sem("ring_n3T_sb"), sem("ring_gate"), sem("logits_made")
        ring_var = [sem(f"ring_var{n}") for n in range(3)]
        ring_std = [sem(f"ring_std{n}") for n in range(3)]
        logits_neg, exp_ready, choice_counts, choice_prefix, slots_ready = sem("logits_neg"), sem("exp_ready"), sem("choice_counts"), sem("choice_prefix"), sem("slots_ready")
        etiles_made, row_numbers, tile_numbers = sem("etiles_made"), sem("row_numbers"), sem("tile_numbers")
        places_made, tokens_summed, tokens_ready = sem("places_made"), sem("tokens_summed"), sem("tokens_ready")
        s_copied = sem("s_copied")
        e_weights = [sem(f"e_weights{s}") for s in range(WS)]
        e_rows = [sem(f"e_rows{s}") for s in range(WS)]
        e_turned, e_feat, e_h1, e_h2, e_silu, e_hidden, e_out, e_out_sb = (
            sem("e_turned"), sem("e_feat"), sem("e_h1"), sem("e_h2"), sem("e_silu"), sem("e_hidden"), sem("e_out"), sem("e_out_sb"))
        e_stored = [sem("e_stored0"), sem("e_stored1")]
        y_gathered, y_summed, y_stored = [sem(f"y_gathered{n}") for n in range(DT)], sem("y_summed"), [sem(f"y_stored{n}") for n in range(DT)]

        def ready(t):
            return t + 1 + U

        def free(t):
            return t + 1

        def tile_of(a, i, j):
            return a[:].rearrange("p (a b) c -> p a b c", b=U)[:, bass.ds(i, 1), j, :].rearrange("p a c -> p (a c)")

        def xnT_of(k, i, j):
            return xnT[:, k, :].rearrange("p (a b c) -> p a b c", b=U, c=P)[:, bass.ds(i, 1), j, :].rearrange("p a c -> p (a c)")

        def edges_of(a, g):
            return a.rearrange("p (g c) -> p g c", c=GE)[:, bass.ds(g, 1), :].rearrange("p g c -> p (g c)")

        count_begin = count[:, 0:BINS * GE].rearrange("p (b c) -> p b c", c=GE)[:, :, 0]
        count_end = count[:, 1:1 + BINS * GE].rearrange("p (b c) -> p b c", c=GE)[:, :, GE - 1]
        x_tiles = x[0:(NT - 1) * P, :].rearrange("(t p) c -> p t c", p=P)
        block = ctx.enter_context(nc.Block())

        @block.sync
        def _(sp):
            sp.sem_inc(n3_stored, 16)
            for i in range(TURNS - 1):
                sp.dma_start(xn[:, i * U:(i + 1) * U, :], x_tiles[:, i * U:(i + 1) * U, :]).then_inc(x_loaded[i], 16)
            sp.dma_start(xn[:, NT - U:NT - 1, :], x_tiles[:, NT - U:NT - 1, :]).then_inc(x_loaded[TURNS - 1], 16)
            sp.wait_ge(zero_pad, 1)
            sp.dma_start(xn[0:LAST, NT - 1, :], x[(NT - 1) * P:N, :]).then_inc(x_loaded[TURNS - 1], 16)
            chunks = "(k p) n -> p k n"
            for a, b in ((gnn_raw[:, :, :], gnn_W), (wkv[:, :, 0:C], Wk), (wkv[:, :, C:2 * C], Wv)):
                sp.dma_start(a, b.rearrange(chunks, p=P)).then_inc(first_weights, 16)
            for a, b in ((src_i, src), (dst_i, dst), (wgt[:, :], edge_weight)):
                sp.dma_start(a, b.rearrange("(p c) -> p c", p=EP)).then_inc(edges_loaded, 16)
            loads = [(wq[:, :, :], Wq.rearrange(chunks, p=P)), (wm[:, :, :], Wm.rearrange(chunks, p=P)),
                     (w1[:, :, :], W1.rearrange(chunks, p=P)),
                     (w2[:, :, :], W2.rearrange(chunks, p=P)), (gw[:, :, :], gate_w.rearrange(chunks, p=P)),
                     (g2r[:, :], g2.rearrange("(a c) -> a c", a=1).to_broadcast([P, C])),
                     (bias_row[:, 0, :], b2.rearrange("(a c) -> a c", a=1).to_broadcast([P, C])),
                     (bias_row[:, 1, :], gnn_b.rearrange("(a c) -> a c", a=1).to_broadcast([P, C])),
                     (gate_row[:, :], gate_b.rearrange("(a c) -> a c", a=1).to_broadcast([P, NE]))]
            for a, b in loads:
                sp.dma_start(a, b).then_inc(weights_loaded, 16)
            with nc.allow_non_contiguous_dma(reason="two short columns"):
                for k in range(KC):
                    sp.dma_start(g1c[:, k:k + 1], g1[k * P:(k + 1) * P].rearrange("(p a) -> p a", a=1)).then_inc(weights_loaded, 16)
                    sp.dma_start(b1c[:, k:k + 1], b1[k * P:(k + 1) * P].rearrange("(p a) -> p a", a=1)).then_inc(weights_loaded, 16)
            sp.wait_ge(xn_ready, TURNS)
            sp.dma_start(xn_rows[0:(NT - 1) * P, :].rearrange("(t p) c -> p t c", p=P), xn[:, 0:NT - 1, :]).then_inc(xn_stored, 16)
            sp.dma_start(xn_rows[(NT - 1) * P:N, :], xn[0:LAST, NT - 1, :]).then_inc(xn_stored, 16)
            def store_n3(i):
                sp.wait_ge(ring_n3, ready(i * U + U - 1))
                if i < TURNS - 1:
                    sp.dma_start(n3_tiles[:, i * U:(i + 1) * U, :], n3[:, :, :]).then_inc(n3_stored, 16)
                else:
                    sp.dma_start(n3_tiles[:, i * U:NT - 1, :], n3[:, 0:U - 1, :]).then_inc(n3_stored, 16)
                    sp.dma_start(n3_rows[(NT - 1) * P:N, :], n3[0:LAST, U - 1, :]).then_inc(n3_stored, 16)

            sp.wait_ge(group_added, NG)
            xn_tiles, n3_tiles = (a[0:(NT - 1) * P, :].rearrange("(t p) c -> p t c", p=P) for a in (xn_rows, n3_rows))
            for i in range(TURNS):
                if i >= 1:
                    sp.wait_ge(ring_x1, ready(i * U - 1))
                for a, tiles, rest in ((x_again, x_tiles, x), (xn_again, xn_tiles, xn_rows)):
                    sp.dma_start(a[:, 0:U - 1, :], tiles[:, i * U:i * U + U - 1, :]).then_inc(x_back, 16)
                    if i < TURNS - 1:
                        sp.dma_start(a[:, U - 1, :], tiles[:, i * U + U - 1, :]).then_inc(x_back, 16)
                    else:
                        sp.dma_start(a[0:LAST, U - 1, :], rest[(NT - 1) * P:N, :]).then_inc(x_back, 16)
                if i >= 1:
                    store_n3(i - 1)
            store_n3(TURNS - 1)
            def e_owner(q, s):
                return nc.values_load(owner[0:1, :].rearrange("p (a b) -> p a b", b=WS)[:, bass.ds(q, 1), s], engines=SP,
                                   min_val=0, max_val=NE - 1,
                                   skip_runtime_bounds_check_because="it is a minimum with NE - 1 of a count")

            def e_load_weights(e, s, kinds):
                for w, b, k in kinds:
                    sp.dma_start(w[s].rearrange("p (k n) -> p k n", k=k),
                                 b.rearrange("e (k p) n -> e p k n", p=P)[bass.ds(e, 1), :, :, :].rearrange("e p k n -> (e p) k n"))\
                        .then_inc(e_weights[s], 16)

            up, down = ((e_w1, ew1, KC), (e_w2, ew2, KC)), ((e_w3, ew3, EHC),)
            sp.wait_ge(slots_ready, 1)
            sp.wait_ge(n3_stored, 16 + 16 * TURNS + 16)
            for s in range(WS):
                if s == WS - 1:
                    sp.wait_ge(tokens_ready, 1)
                e_load_weights(e_owner(0, s), s, up + down)
            with sp.Fori(1, ETILES // WS) as q:
                for s in range(WS):
                    n = q * WS + s
                    e = e_owner(q, s)
                    sp.wait_ge(e_h2, n - WS + 3)
                    sp.nop(nofuse=True)
                    e_load_weights(e, s, up)
                    sp.wait_ge(e_out, n - WS + 3)
                    sp.nop(nofuse=True)
                    e_load_weights(e, s, down)
            with sp.Fori(0, (NT - 1) // DT) as i:
                for n in range(DT):
                    sp.wait_ge(y_summed, i * DT + n + 1 + DT)
                    sp.nop(nofuse=True)
                    sp.dma_start(out[0:(NT - 1) * P, :].rearrange("(a b p) c -> a b p c", b=DT, p=P)[bass.ds(i, 1), n, :, :]
                                 .rearrange("a p c -> (a p) c"), c_out[:, n, :]).then_inc(y_stored[n], 16)
            sp.wait_ge(y_summed, NT + DT)
            sp.dma_start(out[(NT - 1) * P:N, :], c_out[0:LAST, 0, :]).then_inc(y_stored[0], 16)
            for n in range(DT):
                sp.wait_ge(y_stored[n], 16 + 16 * (NT - 1) // DT + (16 if n == 0 else 0))

        @block.scalar
        def _(act):
            for s in (ring_tok, ring_feat, ring_v, ring_kexp, ring_qexp, ring_msgT_sb, ring_n1T_sb,
                      ring_h_sb, ring_nbrT_sb, ring_gnn_sb, ring_n3T_sb, *ring_std):
                act.sem_inc(s, U)
            act.sem_inc(e_silu, 2)
            for n in range(DT):
                act.sem_inc(y_stored[n], 16)
            act.wait_ge(consts_ready, 1)
            def x_roots(i):
                own = slice(i * U, (i + 1) * U)
                act.wait_ge(var_ready, i + 1)
                act.activation(x_root[:, 0, own], x_stat[:, own, 7], ACT.Sqrt, bias=epsc[:, 0:1]).then_inc(std_ready, 1)

            def slot_hot(g, part=0, parts=1):
                own = slice(part * GE // parts, (part + 1) * GE // parts)
                if part == 0:
                    act.wait_ge(places_ready, g + 1)
                    act.nop(nofuse=True)
                for c in range(own.start, own.stop):
                    act.activation(in_slot[:, c, :], iota[0:EP, :], ACT.Abs, bias=place_f[:, 0, c:c + 1])
                act.drain()
                last = act.activation(in_slot[:, own, :], in_slot[:, own, :], ACT.Relu, scale=-1.0, bias=1.0)
                if part == parts - 1:
                    last.then_inc(slot_hot_ready, 1)

            def kv_rows(i):
                act.wait_ge(xn_ready, i + 1)
                for j in range(U):
                    act.wait_ge(ring_turned, free(i * U + j))
                    act.activation(tok[:, j, :], xn[:, i * U + j, :], ACT.Copy).then_inc(ring_tok, 1)

            def kv_features(i):
                for j in range(U):
                    t = i * U + j
                    act.wait_ge(ring_turned, ready(t))
                    act.wait_ge(ring_kept, free(t))
                    act.activation(feat[:, j, :], bank[j][:, 0:C], ACT.Copy).then_inc(ring_feat, 1)

            x_roots(0)
            x_roots(1)
            kv_rows(0)
            x_roots(2)
            kv_features(0)
            x_roots(3)
            x_roots(4)
            act.wait_ge(gnn_turned, 1)
            act.activation(gnnT[:, :, :], bank[5][:, :].rearrange("p (k n) -> p k n", k=KC), ACT.Copy).then_inc(gnnT_ready, 1)
            for i in range(TURNS):
                if i + 1 < TURNS:
                    kv_rows(i + 1)
                for j in range(U):
                    act.wait_ge(ring_kv, ready(i * U + j))
                    if i > 0:
                        act.wait_ge(kv_summed, i)
                    act.activation(neg[:, j, :], bank[j][:, 0:C], ACT.Relu, scale=-1.0)
                    act.activation(values[:, j, :, 0:P], bank[j][:, C:2 * C].rearrange("p (m c) -> p m c", m=KC), ACT.Copy).then_inc(ring_v, 1)
                    act.drain()
                    act.activation(neg[:, j, :], neg[:, j, :], ACT.Exp, scale=-1.0).then_inc(ring_kexp, 1)
                    if i in (2, 3):
                        slot_hot(i - 2, j, U)
                if i + 1 < TURNS:
                    kv_features(i + 1)

            def scale_rows(g_half, h, chunks):
                for q in chunks:
                    act.wait_ge(gathered[h][q], 16 * GC * (g_half + 1))
                    act.nop(nofuse=True)
                    for t in range(q * GC, (q + 1) * GC):
                        last = act.activation(rows[h][:, t, :], rows[h][:, t, :], ACT.Copy, scale=weight[h][:, t:t + 1])
                    last.then_inc(scaled, 1)

            early, late = range(0, 1), range(1, GT // GC)
            scale_rows(0, 0, early)
            scale_rows(0, 0, late)
            with act.Fori(0, (NG - 3) // 2) as i:
                scale_rows(i, 1, early)
                slot_hot(2 * i + 2)
                scale_rows(i, 1, late)
                scale_rows(i + 1, 0, early)
                slot_hot(2 * i + 3)
                scale_rows(i + 1, 0, late)
            scale_rows((NG - 3) // 2, 1, early)
            slot_hot(NG - 1)
            scale_rows((NG - 3) // 2, 1, late)
            scale_rows((NG - 1) // 2, 0, range(GT // GC))

            act.wait_ge(weights_loaded, 16 * 13)
            act.wait_ge(group_added, NG)
            def q_exp(i, j):
                act.wait_ge(ring_qneg, ready(i * U + j))
                act.nop(nofuse=True)
                act.activation(neg[:, j, :], neg[:, j, :], ACT.Exp).then_inc(ring_qexp, 1)

            def copy_out(i, j, produced, b, to, done):
                act.wait_ge(produced, ready(i * U + j))
                act.nop(nofuse=True)
                act.activation(to, bank[b][:, 0:C], ACT.Copy).then_inc(done, 1)

            def nbr_turned(i, j):
                copy_out(i, j, ring_nbrT, 5 + j % 2, nbrT[:, j % 2, :], ring_nbrT_sb)

            def nbr_projected(i, j):
                copy_out(i, j, ring_gnn, 7, nbr[:, j, :], ring_gnn_sb)

            def n3_turned(i, j):
                copy_out(i, j, ring_n3T, 5 + j % 2, n3T[:, j % 2, :], ring_n3T_sb)

            def std(n, i, j):
                act.wait_ge(ring_var[n], ready(i * U + j))
                act.nop(nofuse=True)
                act.activation(stat[:, n, j, 8:9], stat[:, n, j, 7:8], ACT.Sqrt, bias=epsc[:, 0:1]).then_inc(ring_std[n], 1)

            def n1_turned(i, j):
                act.wait_ge(ring_n1T, ready(i * U + j))
                act.nop(nofuse=True)
                for k in range(KC):
                    last = act.activation(feat[:, j, k * P:(k + 1) * P], bank[j][:, k * P:(k + 1) * P], ACT.Identity,
                                          scale=g1c[:, k:k + 1], bias=b1c[:, k:k + 1])
                last.then_inc(ring_n1T_sb, 1)

            def hidden(i, j):
                act.wait_ge(ring_h, ready(i * U + j))
                act.nop(nofuse=True)
                act.activation(wide[:, j, :], bank[j][:, :], ACT.Relu).then_inc(ring_h_sb, 1)

            def dense(i, past):
                act.preload_act_table(ACT.Exp)
                for step, j in ((q_exp, 0), (nbr_turned, 0), (q_exp, 1), (nbr_turned, 1), (q_exp, 2), (nbr_projected, 0),
                                (nbr_turned, 2), (q_exp, 3), (nbr_projected, 1), (nbr_turned, 3), (q_exp, 4),
                                (nbr_projected, 2), (nbr_turned, 4), (nbr_projected, 3), (nbr_projected, 4)):
                    step(i, j)
                act.preload_act_table(ACT.Sqrt)
                for j in range(U):
                    copy_out(i, j, ring_msgT, j, feat[:, j, :], ring_msgT_sb)
                for j in range(U):
                    std(0, i, j)
                    if 1 <= j < 3:
                        n1_turned(i, j - 1)
                for j in range(U):
                    hidden(i, j)
                    if j + 2 < U:
                        n1_turned(i, j + 2)
                    if past is not None:
                        for t in ((0, 1, 2), (3, 4), (), (), ())[j]:
                            std(2, past, t)
                        for t in ((), (0, 1), (2, 3), (4,), ())[j]:
                            n3_turned(past, t)
                for j in range(U):
                    std(1, i, j)

            dense(0, None)
            with act.Fori(1, TURNS) as i:
                dense(i, i - 1)
            for j in range(U + 1):
                if j < U:
                    std(2, TURNS - 1, j)
                if j >= 1:
                    n3_turned(TURNS - 1, j - 1)

            act.wait_ge(logits_neg, 1)
            act.activation(logits[:, :, :], logits[:, :, :], ACT.Exp).then_inc(exp_ready, 1)

            for c in range(2):
                act.wait_ge(etiles_made, c + 1)
                act.activation(numbered[:, c, :, 0, :], in_etile[:, c, :, :], ACT.Copy, scale=token[:, 0, 0:1]).then_inc(row_numbers, 1)
            act.preload_act_table(ACT.Silu)

            with act.Fori(0, ETILES // 2) as i:
                for h in range(2):
                    n = 2 * i + h
                    act.wait_ge(e_h1, n + 3)
                    act.wait_ge(e_hidden, n + 1)
                    act.nop(nofuse=True)
                    act.activation(e_act[:, h, :], bank[h][:, :], ACT.Silu).then_inc(e_silu, 1)

            def at_slots(n, tile):
                act.activation(s_at[:, n, :], tile, ACT.Copy).then_inc(s_copied, 1)

            for n in range(DT):
                at_slots(n, slots[:, :, n])
            with act.Fori(1, (NT - 1) // DT) as i:
                for n in range(DT):
                    act.wait_ge(y_gathered[n], 32 * i)
                    act.nop(nofuse=True)
                    at_slots(n, slots[:, :, 0:NT - 1].rearrange("p c (a b) -> p c a b", b=DT)[:, :, bass.ds(i, 1), n].rearrange("p c a -> p (c a)"))
            act.wait_ge(y_gathered[0], 32 * (NT - 1) // DT)
            at_slots(0, slots[:, :, NT - 1])

        @block.gpsimd
        def _(pool):
            for s in (ring_kept, ring_nbr):
                pool.sem_inc(s, U)
            pool.memset(xn[:, NT - 1, :], 0.0)
            pool.drain().then_inc(zero_pad, 1)
            pool.memset(epsc[:, :], LN_EPS)
            pool.memset(ones[:, :], 1.0)
            pool.memset(zero[:, :], 0.0)
            pool.memset(ident[:, :], 0.0)
            pool.memset(before[:, :], 1.0)
            pool.memset(after[:, :], 1.0)
            pool.memset(valid[:, :], 1.0)
            pool.memset(values[:, :, :, :], 1.0)
            pool.memset(KVd[:, :, :], 0.0)
            pool.memset(agg[:, :, :], 0.0)
            pool.memset(count[:, 0:1], 0.0)
            pool.drain()
            pool.affine_select(out=ident[:, :], in_=ident[:, :], compare_op=ALU.not_equal, fill=1.0, base=0,
                               pattern=[[-1, P]], channel_multiplier=1)
            pool.affine_select(out=before[:, :], in_=before[:, :], compare_op=ALU.is_gt, fill=0.0, base=0,
                               pattern=[[1, P]], channel_multiplier=-1)
            pool.affine_select(out=after[:, :], in_=after[:, :], compare_op=ALU.is_gt, fill=0.0, base=0,
                               pattern=[[-1, P]], channel_multiplier=1)
            pool.affine_select(out=valid[:, NT - 1:NT], in_=valid[:, NT - 1:NT], compare_op=ALU.is_gt, fill=0.0, base=LAST,
                               pattern=[[0, 1]], channel_multiplier=-1)
            pool.iota(iota1[:, :], [[1, P]], base=1, channel_multiplier=0, allow_small_or_imprecise_dtypes=True)
            pool.iota(iota[:, :], [[1, P]], base=0, channel_multiplier=0, allow_small_or_imprecise_dtypes=True)
            pool.iota(token[:, :, 0], [[0, NT]], base=0, channel_multiplier=1, allow_small_or_imprecise_dtypes=True)
            pool.iota(token[:, :, 1], [[1, NT]], base=0, channel_multiplier=0, allow_small_or_imprecise_dtypes=True)
            pool.iota(boundary[:, :], [[P, STEPS]], base=0, channel_multiplier=-P, allow_small_or_imprecise_dtypes=True)
            pool.drain().then_inc(consts_ready, 1)

            def gather(g, h, first):
                pool.wait_ge(list_ready, g + 1)
                if not first:
                    pool.wait_ge(group_added, g - 1)
                pool.nop(nofuse=True)
                for t in range(GT):
                    pool.indirect_dma_start(rows[h][:, t, :], None, xn_rows,
                                            bass.IndirectOffsetOnAxis(ap=gather_i[h][:, t:t + 1], axis=0)).then_inc(gathered[h][t // GC], 16)

            def keep_features(i):
                for j in range(U):
                    pool.wait_ge(ring_feat, ready(i * U + j))
                    pool.nop(nofuse=True)
                    for k in range(KC):
                        last = pool.tensor_copy(xnT_of(k, i, j), feat[:, j, k * P:(k + 1) * P])
                    last.then_inc(ring_kept, 1)

            pool.wait_ge(gnn_turned, 1)
            with pool.Fori(0, TURNS - 1) as i:
                keep_features(i)
            pool.wait_ge(xn_stored, 32)
            pool.drain()
            gather(0, 0, True)
            keep_features(TURNS - 1)
            pool.drain()
            pool.wait_ge(kvd_ready, 1)
            gather(1, 1, True)
            with pool.Fori(0, (NG - 3) // 2) as i:
                for h in range(2):
                    gather(2 * i + h + 2, h, False)
            gather(NG - 1, 0, False)

            pool.wait_ge(weights_loaded, 16 * 13)
            pool.tensor_tensor(bias_row[:, 0, :], bias_row[:, 0, :], bias_row[:, 1, :], ALU.add)
            pool.drain()
            def base(i):
                for j in range(U):
                    pool.tensor_copy(nbr[:, j, :], tile_of(agg, i, j)).then_inc(ring_nbr, 1)
                pool.wait_ge(x_back, 64 * i + 64)
                pool.nop(nofuse=True)
                for j in range(U):
                    pool.tensor_tensor(x_again[:, j, :], x_again[:, j, :], bias_row[:, 0, :], ALU.add)
                pool.drain()
                for j in range(U):
                    pool.tensor_tensor(x_again[:, j, :], x_again[:, j, :], xn_again[:, j, :], ALU.add)
                pool.drain()
                for j in range(U):
                    pool.wait_ge(ring_gnn_sb, ready(i * U + j))
                    pool.nop(nofuse=True)
                    pool.tensor_tensor(x_again[:, j, :], x_again[:, j, :], nbr[:, j, :], ALU.add).then_inc(x_base, 1)
                pool.drain()

            pool.wait_ge(group_added, NG)
            with pool.Fori(0, TURNS) as i:
                base(i)

            for c in range(2):
                pool.wait_ge(etiles_made, c + 1)
                pool.tensor_tensor(numbered[:, c, :, 1, :], in_etile[:, c, :, :],
                                   token[:, :, 1].unsqueeze(2).to_broadcast([P, NT, ETILES]), ALU.mult).then_inc(tile_numbers, 1)

            def e_gather(s):
                pool.indirect_dma_start(e_x[:, s, :], None, n3_rows, bass.IndirectOffsetOnAxis(ap=e_at[:, s:s + 1], axis=0))\
                    .then_inc(e_rows[s], 16)

            pool.wait_ge(tokens_ready, 1)
            pool.wait_ge(n3_stored, 16 + 16 * TURNS + 16)
            pool.tensor_copy(e_at[:, :], token_of[:, 0:WS])
            pool.drain()
            for s in range(WS):
                e_gather(s)

            def e_store(q, s):
                h = s % 2
                pool.wait_ge(e_out_sb, q * WS + s + 3)
                pool.nop(nofuse=True)
                pool.dma_start(expert_rows.rearrange("(a b p) c -> a b p c", b=WS, p=P)[bass.ds(q, 1), s, :, :]
                               .rearrange("a p c -> (a p) c"), e_y[:, h, :]).then_inc(e_stored[h], 16)

            with pool.Fori(0, ETILES // WS - 1) as q:
                for s in range(WS):
                    pool.wait_ge(e_turned, q * WS + s + 3)
                    pool.nop(nofuse=True)
                    pool.tensor_copy(e_at[:, s:s + 1], token_of[:, :].rearrange("p (a b) -> p a b", b=WS)[:, bass.ds(q + 1, 1), s])
                    pool.drain()
                    e_gather(s)
                    e_store(q, s)
            for s in range(WS):
                e_store(ETILES // WS - 1, s)

            def collect(n, rows_n):
                for c, y in ((0, c_y1), (1, c_y2)):
                    pool.indirect_dma_start(y[0:rows_n, n, :], None, expert_rows,
                                            bass.IndirectOffsetOnAxis(ap=s_at[0:rows_n, n, c:c + 1], axis=0)).then_inc(y_gathered[n], 16)

            for h in range(2):
                pool.wait_ge(e_stored[h], 16 * ETILES // 2)
            with pool.Fori(0, (NT - 1) // DT) as i:
                for n in range(DT):
                    pool.wait_ge(s_copied, i * DT + n + 1)
                    pool.wait_ge(y_summed, i * DT + n + 1)
                    pool.nop(nofuse=True)
                    collect(n, P)
            pool.wait_ge(s_copied, NT)
            pool.wait_ge(y_summed, NT)
            collect(0, LAST)

        @block.tensor
        def _(pe):
            for s in (ring_turned, ring_kv, ring_q, ring_att, ring_msgT, ring_mm, ring_n1T, ring_h, ring_h2,
                      ring_nbrT, ring_gnn, ring_n3T):
                pe.sem_inc(s, U)
            for s in (e_turned, e_h1, e_h2, e_out):
                pe.sem_inc(s, 2)

            def turn(j, a, b=None):
                for k in range(KC):
                    last = pe.transpose(bank[j if b is None else b][:, k * P:(k + 1) * P], a[:, j, k * P:(k + 1) * P], ident[:, :])
                return last

            def project(j, w, n):
                for k in range(KC):
                    last = pe.matmul(bank[j][:, 0:n], feat[:, j, k * P:(k + 1) * P], w[:, k, 0:n],
                                     start=(k == 0), stop=(k == KC - 1))
                return last

            pe.wait_ge(consts_ready, 1)
            def prefix(g):
                pe.wait_ge(counts_ready, g + 1)
                pe.nop(nofuse=True)
                pe.matmul(bank[7][0:EP, 0:BINS], before[0:EP, 0:EP], count_end, start=True, stop=False)
                pe.matmul(bank[7][0:EP, 0:BINS], after[0:EP, 0:EP], count_begin, start=False, stop=True)
                pe.matmul(bank[7][0:BINS, 32:33], count_end, ones[0:EP, 0:1], start=True, stop=True).then_inc(prefix_ready, 1)

            def reorder(g):
                pe.wait_ge(record_ready, g + 1)
                pe.wait_ge(slot_hot_ready, g + 1)
                pe.nop(nofuse=True)
                pe.matmul(bank[7][0:1, 64 + REC:64 + REC + STEPS], ones[0:BINS, 0:1], meets[:, :], start=True, stop=True)
                for c in range(GE):
                    last = pe.matmul(bank[7][:, 64:64 + REC], in_slot[:, c, :], record[:, c, :],
                                     start=(c == 0), stop=(c == GE - 1))
                last.then_inc(ordered_ready, 1)

            def kv_turn(i):
                for j in range(U):
                    pe.wait_ge(ring_tok, ready(i * U + j))
                    pe.wait_ge(ring_v, free(i * U + j))
                    pe.wait_ge(ring_k, free(i * U + j))
                    turn(j, tok).then_inc(ring_turned, 1)

            kv_turn(0)
            pe.wait_ge(first_weights, 48)
            for i in range(TURNS):
                if i == 0:
                    for m in range(KC):
                        for k in range(KC):
                            last = pe.transpose(bank[5][:, k * C + m * P:k * C + (m + 1) * P], gnn_raw[:, m, k * P:(k + 1) * P], ident[:, :])
                    last.then_inc(gnn_turned, 1)
                if i == 3:
                    prefix(1)
                for j in range(U):
                    pe.wait_ge(ring_feat, ready(i * U + j))
                    project(j, wkv, 2 * C).then_inc(ring_kv, 1)
                if i == 1:
                    prefix(0)
                if i + 1 < TURNS:
                    kv_turn(i + 1)
                if i == 0:
                    pe.wait_ge(gnnT_ready, 1)
                if i in (2, 4):
                    reorder(i // 2 - 1)
                for j in range(U):
                    t = i * U + j
                    pe.wait_ge(ring_k, ready(t))
                    tokens = P if t < NT - 1 else LAST
                    for m in range(KC):
                        last = pe.matmul(bank[5 + m][:, 0:P + 1], wide[0:tokens, j, m * P:(m + 1) * P], values[0:tokens, j, m, :],
                                         start=(t == 0), stop=(t == NT - 1), skip_group_check=True)
                last.then_inc(kv_summed, 1)

            def add_up(g, h, ordering):
                pe.wait_ge(list_ready, g + 1)
                pe.nop(nofuse=True)
                for c in range(KC):
                    for s in range(STEPS // SU):
                        (_, row_at), (_, sum_at) = (
                            nc.values_load_multi_w_load_instructions(
                                pairs[h][0:1, a, s * SU:(s + 1) * SU], engines=PE, min_val=0, max_val=most,
                                skip_runtime_bounds_check_because="bins and tiles are clipped when the list is made")
                            for a, most in ((0, (GT - 1) * C), (1, (BINS - 1) * P)))
                        for k in range(SU):
                            n = s * SU + k
                            if n in HANDOVER:
                                banks = HANDOVER[n]
                                pe.wait_ge(flushed, (g * KC + c) * BANKS + banks[-1] + 1)
                                pe.nop(nofuse=True)
                                for b in banks:
                                    pe.matmul(bank[b][:, 0:2], zero[:, :], ident[:, 0:2], start=True, stop=True)
                            if c == 0 and n in ROWS_BY:
                                pe.wait_ge(scaled, g * (GT // GC) + ROWS_BY[n])
                                pe.nop(nofuse=True)
                            if c == 0 and n in HOTS_BY:
                                pe.wait_ge(hot_ready, g * (STEPS // SU) + HOTS_BY[n])
                                pe.nop(nofuse=True)
                            pe.matmul(psum[:, bass.ds(sum_at[k], P)], hot[:, n, :],
                                      rows[h][:, :, :].rearrange("p t c -> p (t c)")[:, c * P:][:, bass.ds(row_at[k], P)],
                                      start=False, stop=True, skip_group_check=True).then_inc(met, 1)
                            if ordering and c == 0 and n == 4 * SU:
                                prefix(g + 2)
                if ordering:
                    reorder(g + 2)

            with pe.Fori(0, (NG - 3) // 2) as i:
                for h in range(2):
                    add_up(2 * i + h, h, True)
            add_up(NG - 3, 0, True)
            add_up(NG - 2, 1, False)
            add_up(NG - 1, 0, False)

            pe.wait_ge(weights_loaded, 16 * 13)
            pe.wait_ge(group_added, NG)
            def query(i, j):
                pe.wait_ge(ring_h2_read, free(i * U + j))
                pe.wait_ge(ring_kept, ready(i * U + j))
                pe.nop(nofuse=True)
                for m in range(KC):
                    for k in range(KC):
                        last = pe.matmul(bank[j][:, m * P:(m + 1) * P], wq[:, k, m * P:(m + 1) * P], xnT_of(k, i, j),
                                         start=(k == 0), stop=(k == KC - 1))
                last.then_inc(ring_q, 1)

            def turn_nbr(i, j):
                pe.wait_ge(ring_nbr, ready(i * U + j))
                pe.nop(nofuse=True)
                turn(j, nbr, 5 + j % 2).then_inc(ring_nbrT, 1)

            def project_nbr(i, j):
                pe.wait_ge(ring_nbrT_sb, ready(i * U + j))
                pe.wait_ge(ring_gnn_sb, i * U + j + U)
                pe.nop(nofuse=True)
                for k in range(KC):
                    last = pe.matmul(bank[7][:, 0:C], nbrT[:, j % 2, k * P:(k + 1) * P], gnnT[:, k, :],
                                     start=(k == 0), stop=(k == KC - 1))
                last.then_inc(ring_gnn, 1)

            def attend(i, j):
                pe.wait_ge(ring_qelu, ready(i * U + j))
                pe.nop(nofuse=True)
                for m in range(KC):
                    last = pe.matmul(bank[j][:, m * (P + HPC):(m + 1) * (P + HPC)], wide[:, j, m * P:(m + 1) * P], KVd[:, m, :],
                                     start=True, stop=True)
                last.then_inc(ring_att, 1)

            def turn_msg(i, j):
                pe.wait_ge(ring_msg, ready(i * U + j))
                pe.nop(nofuse=True)
                turn(j, tok).then_inc(ring_msgT, 1)

            def merge(i, j):
                pe.wait_ge(ring_msgT_sb, ready(i * U + j))
                pe.nop(nofuse=True)
                project(j, wm, C).then_inc(ring_mm, 1)

            def turn_n1(i, j):
                pe.wait_ge(ring_n1, ready(i * U + j))
                pe.nop(nofuse=True)
                turn(j, tok).then_inc(ring_n1T, 1)

            def hidden(i, j):
                pe.wait_ge(ring_n1T_sb, ready(i * U + j))
                pe.nop(nofuse=True)
                for m in range(HC):
                    for k in range(2 * KC):
                        operand = xnT_of(k, i, j) if k < KC else feat[:, j, (k - KC) * P:(k - KC + 1) * P]
                        last = pe.matmul(bank[j][:, m * P:(m + 1) * P], w1[:, k, m * P:(m + 1) * P], operand,
                                         start=(k == 0), stop=(k == 2 * KC - 1))
                last.then_inc(ring_h, 1)

            def hidden_down(i, j):
                pe.wait_ge(ring_h_sb, ready(i * U + j))
                pe.nop(nofuse=True)
                for k in range(HC):
                    last = pe.matmul(bank[j][:, 0:C], wide[:, j, k * P:(k + 1) * P], w2[:, k, :],
                                     start=(k == 0), stop=(k == HC - 1))
                last.then_inc(ring_h2, 1)

            def turn_n3(i, j):
                pe.wait_ge(ring_n3, ready(i * U + j))
                pe.nop(nofuse=True)
                turn(j, n3, 5 + j % 2).then_inc(ring_n3T, 1)

            def gate(i, j):
                pe.wait_ge(ring_n3T_sb, ready(i * U + j))
                pe.nop(nofuse=True)
                for k in range(KC):
                    last = pe.matmul(bank[7][:, j * NE:(j + 1) * NE], n3T[:, j % 2, k * P:(k + 1) * P], gw[:, k, :],
                                     start=(k == 0), stop=(k == KC - 1))
                if j == U - 1:
                    last.then_inc(ring_gate, 1)

            def dense(i, past):
                for j in range(U):
                    query(i, j)
                if past is not None:
                    pe.wait_ge(logits_made, past + 1)
                for step, j in ((turn_nbr, 0), (turn_nbr, 1), (project_nbr, 0), (turn_nbr, 2), (project_nbr, 1), (turn_nbr, 3),
                                (project_nbr, 2), (turn_nbr, 4), (project_nbr, 3), (project_nbr, 4)):
                    step(i, j)
                for j in range(U):
                    attend(i, j)
                for j in range(U + 1):
                    if j < U:
                        turn_msg(i, j)
                    if j >= 1:
                        merge(i, j - 1)
                turn_n1(i, 0)
                for j in range(U):
                    if j + 1 < U:
                        turn_n1(i, j + 1)
                    hidden(i, j)
                    if past is not None:
                        for step, t in ((), ((turn_n3, 0), (turn_n3, 1)), ((gate, 0), (gate, 1), (turn_n3, 2), (turn_n3, 3)),
                                        ((gate, 2), (gate, 3), (turn_n3, 4)), ((gate, 4),))[j]:
                            step(past, t)
                for j in range(U):
                    hidden_down(i, j)

            dense(0, None)
            with pe.Fori(1, TURNS) as i:
                dense(i, i - 1)
            for step, j in ((turn_n3, 0), (turn_n3, 1), (gate, 0), (turn_n3, 2), (gate, 1), (turn_n3, 3), (gate, 2),
                            (turn_n3, 4), (gate, 3), (gate, 4)):
                step(TURNS - 1, j)

            pe.wait_ge(choice_counts, 1)
            pe.matmul(bank[7][:, 0:NE], before[:, :], tiny[:, 0, 0:NE], start=True, stop=True)
            pe.matmul(bank[7][:, 32:32 + NE], ones[:, :], tiny[:, 0, 0:NE], start=True, stop=True).then_inc(choice_prefix, 1)

            for c in range(2):
                for s in (places_made, row_numbers, tile_numbers):
                    pe.wait_ge(s, c + 1)
                for t in range(NT):
                    tokens = P if t < NT - 1 else LAST
                    last = pe.matmul(bank[6][:, 0:2 * ETILES], in_place[0:tokens, c, t, :],
                                     numbered[0:tokens, c, t, :, :].rearrange("p b n -> p (b n)"),
                                     start=(c == 0 and t == 0), stop=(c == 1 and t == NT - 1))
            last.then_inc(tokens_summed, 1)

            def e_turn(n, q, s):
                h = s % 2
                pe.wait_ge(e_rows[s], 16 * q + 16)
                pe.wait_ge(e_feat, n + 1)
                pe.nop(nofuse=True)
                for k in range(KC):
                    last = pe.transpose(bank[4 + h][:, k * P:(k + 1) * P], e_x[:, s, k * P:(k + 1) * P], ident[:, :])
                last.then_inc(e_turned, 1)

            def e_up(n, q, s):
                h = s % 2
                pe.wait_ge(e_feat, n + 3)
                pe.wait_ge(e_weights[s], 48 * q + 48)
                pe.wait_ge(e_hidden, n + 1)
                pe.nop(nofuse=True)
                for b, w, done in ((h, e_w1, e_h1), (2 + h, e_w2, e_h2)):
                    for m in range(EHC):
                        for k in range(KC):
                            last = pe.matmul(bank[b][:, m * P:(m + 1) * P], w[s][:, k * EH + m * P:k * EH + (m + 1) * P],
                                             e_xT[:, h, k * P:(k + 1) * P], start=(k == 0), stop=(k == KC - 1))
                    last.then_inc(done, 1)

            def e_down(n, s):
                h = s % 2
                pe.wait_ge(e_hidden, n + 3)
                pe.wait_ge(e_out_sb, n + 1)
                pe.nop(nofuse=True)
                for k in range(EHC):
                    last = pe.matmul(bank[6 + h][:, 0:C], e_hid[:, h, k * P:(k + 1) * P], e_w3[s][:, k * C:(k + 1) * C],
                                     start=(k == 0), stop=(k == EHC - 1))
                last.then_inc(e_out, 1)

            e_turn(0, 0, 0)
            e_up(0, 0, 0)
            e_turn(1, 0, 1)
            with pe.Fori(0, ETILES // WS - 1) as q:
                for s in range(WS):
                    e_up(q * WS + s + 1, q + (s + 1) // WS, (s + 1) % WS)
                    e_turn(q * WS + s + 2, q + (s + 2) // WS, (s + 2) % WS)
                    e_down(q * WS + s, s)
            q = ETILES // WS - 1
            for s in range(WS):
                if s + 1 < WS:
                    e_up(q * WS + s + 1, q, s + 1)
                if s + 2 < WS:
                    e_turn(q * WS + s + 2, q, s + 2)
                e_down(q * WS + s, s)

        @block.vector
        def _(dve):
            for s in (ring_k, ring_qneg, ring_qelu, ring_msg, ring_n1, ring_h2_read, ring_x1, ring_n3, *ring_var):
                dve.sem_inc(s, U)
            dve.sem_inc(logits_made, 1)
            dve.sem_inc(y_summed, DT)
            dve.sem_inc(flushed, BANKS)
            for s in (e_feat, e_hidden, e_out_sb):
                dve.sem_inc(s, 2)

            for i in range(TURNS + 1):
                if i < TURNS:
                    dve.wait_ge(x_loaded[i], 16 if i < TURNS - 1 else 32)
                    for t in range(i * U, (i + 1) * U):
                        dve.bn_stats(x_stat[:, t, 0:6], xn[:, t, :])
                    dve.drain()
                    for t in range(i * U, (i + 1) * U):
                        last = dve.bn_aggr(x_stat[:, t, 6:8], x_stat[:, t, 0:6])
                    last.then_inc(var_ready, 1)
                if i >= 1:
                    dve.wait_ge(std_ready, i)
                    own = slice((i - 1) * U, i * U)
                    dve.reciprocal(x_root[:, 1, own], x_root[:, 0, own])
                    dve.drain()
                    for t in range((i - 1) * U, i * U):
                        last = dve.tensor_scalar(xn[:, t, :], xn[:, t, :], x_stat[:, t, 6:7], x_root[:, 1, t:t + 1],
                                                 ALU.subtract, ALU.mult)
                    last.then_inc(xn_ready, 1)

            def count_bins(g):
                dve.tensor_tensor(in_bin[:, :, :], edges_of(bin_f[:, :], g).unsqueeze(1).to_broadcast([EP, BINS, GE]),
                                  iota[0:EP, 0:BINS].unsqueeze(2).to_broadcast([EP, BINS, GE]), ALU.is_equal)
                dve.drain()
                flat = in_bin[:, :, :].rearrange("p b c -> p (b c)")
                dve.tensor_tensor_scan(count[:, 1:1 + BINS * GE], flat, flat, 0.0, ALU.add, ALU.max).then_inc(counts_ready, 1)

            def find_places(g):
                dve.wait_ge(prefix_ready, g + 1)
                dve.nop(nofuse=True)
                places = count[:, 1:1 + BINS * GE].rearrange("p (b c) -> p b c", c=GE)
                dve.scalar_tensor_tensor(places, bank[7][0:EP, 0:BINS].unsqueeze(2).to_broadcast([EP, BINS, GE]), -1.0, places,
                                         ALU.add, ALU.add)
                dve.tensor_copy(ends[:, :], bank[7][0:BINS, 32:33])
                dve.drain()
                dve.tensor_tensor(places, places, in_bin[:, :, :], ALU.mult)
                dve.tensor_scalar(meets[:, :], boundary[:, :], ends[:, 0:1], None, ALU.is_gt)
                dve.drain()
                with nc.allow_low_precision(reason="each sum is one whole number and zeros"):
                    dve.tensor_reduce(place_i[:, 0, :], places.rearrange("p b c -> p c b"), AX, ALU.add)
                dve.drain()
                dve.tensor_scalar(place_i[:, 1, :], place_i[:, 0, :], 7, None, ALU.arith_shift_right)
                dve.tensor_scalar(place_i[:, 2, :], place_i[:, 0, :], P - 1, None, ALU.bitwise_and)
                dve.drain()
                dve.tensor_scalar(place_f[:, 0, :], place_i[:, 2, :], -1.0, None, ALU.mult).then_inc(places_ready, 1)
                dve.tensor_tensor(place_f[:, 1, :], place_i[:, 1, :], edges_of(bin_f[:, :], g), ALU.add)
                dve.tensor_tensor(in_tile[:, :, :], place_i[:, 1, :].unsqueeze(2).to_broadcast([EP, GE, GT]),
                                  iota[0:EP, 0:GT].unsqueeze(1).to_broadcast([EP, GE, GT]), ALU.is_equal)

            def make_records(g):
                dve.drain()
                dve.tensor_tensor(in_step[:, :, :], place_f[:, 1, :].unsqueeze(2).to_broadcast([EP, GE, STEPS]),
                                  iota[0:EP, 0:STEPS].unsqueeze(1).to_broadcast([EP, GE, STEPS]), ALU.is_equal)
                for n in range(1, PIECES):
                    dve.tensor_tensor(record[:, :, STEPS + (n - 1) * GT:STEPS + n * GT], in_tile[:, :, :],
                                      edges_of(piece[:, n, :], g).unsqueeze(2).to_broadcast([EP, GE, GT]), ALU.mult)
                dve.drain()
                dve.tensor_tensor(record[:, :, 0:STEPS], in_step[:, :, :],
                                  edges_of(piece[:, 0, :], g).unsqueeze(2).to_broadcast([EP, GE, STEPS]), ALU.mult)\
                    .then_inc(record_ready, 1)

            def make_list(g, h):
                in_order = bank[7][:, 64 + STEPS:64 + REC].rearrange("p (a b) -> p a b", b=GT)
                bins = bank[7][0:1, 64 + REC:64 + REC + STEPS]
                dve.wait_ge(ordered_ready, g + 1)
                dve.nop(nofuse=True)
                dve.tensor_tensor(pair_f[:, :], iota[0:1, 0:STEPS], bins, ALU.subtract)
                dve.tensor_scalar(pairs[h][:, 1, :], bins, float(BINS - 1), float(P), ALU.min, ALU.mult)
                dve.tensor_copy(ordered[:, :, :], in_order)
                dve.tensor_copy(node[h][:, :], bank[7][:, 64:64 + STEPS])
                dve.drain()
                dve.tensor_tensor(weight[h][:, :], ordered[:, 4, :], ordered[:, 3, :], ALU.add)
                dve.scalar_tensor_tensor(gather_i[h][:, :], ordered[:, 0, :], float(P), ordered[:, 1, :], ALU.mult, ALU.add)
                dve.tensor_scalar(pairs[h][:, 0, :], pair_f[:, :], float(GT - 1), float(C), ALU.min, ALU.mult)
                dve.drain()
                dve.tensor_tensor(weight[h][:, :], weight[h][:, :], ordered[:, 2, :], ALU.add)
                dve.drain().then_inc(list_ready, 1)

            def make_hot(h):
                for s in range(STEPS // SU):
                    own = slice(s * SU, (s + 1) * SU)
                    dve.tensor_tensor(hot[:, own, :], iota1[:, :].unsqueeze(1).to_broadcast([P, SU, P]),
                                      node[h][:, own].unsqueeze(2).to_broadcast([P, SU, P]), ALU.is_equal).then_inc(hot_ready, 1)

            def flush(g, c):
                for b in range(BANKS):
                    own = slice(b * BPB, min((b + 1) * BPB, BINS))
                    dve.wait_ge(met, (g * KC + c) * STEPS + min((b + 1) * BPB + GT - 1, STEPS))
                    dve.nop(nofuse=True)
                    dve.tensor_tensor(agg[:, own, c * P:(c + 1) * P], sums[:, own, :], agg[:, own, c * P:(c + 1) * P], ALU.add)\
                        .then_inc(flushed, 1)

            def add_up(g, h, ordering, more=True):
                if ordering:
                    count_bins(g + 2)
                    find_places(g + 2)
                for c in range(KC):
                    if ordering and c == KC - 1:
                        make_records(g + 2)
                    flush(g, c)
                dve.drain().then_inc(group_added, 1)
                if more:
                    make_hot(1 - h)
                if ordering:
                    make_list(g + 2, h)

            def keys(i):
                for j in range(U):
                    dve.wait_ge(ring_kexp, ready(i * U + j))
                    dve.scalar_tensor_tensor(wide[:, j, 0:C], bank[j][:, 0:C], 0.0, neg[:, j, :], ALU.max, ALU.add).then_inc(ring_k, 1)

            keys(0)

            dve.wait_ge(edges_loaded, 48)
            for n, a, op, by, plus in ((None, src_i, ALU.arith_shift_right, 7, 0.0), (0, src_i, ALU.bitwise_and, P - 1, 1.0),
                                       (1, dst_i, ALU.arith_shift_right, 7, 0.0), (2, dst_i, ALU.bitwise_and, P - 1, 0.0)):
                dve.tensor_scalar(part_i, a, by, None, op)
                dve.drain()
                dve.tensor_scalar(bin_f[:, :] if n is None else piece[:, n, :], part_i, plus, None, ALU.add)
                dve.drain()
            for n in range(3, PIECES):
                dve.drain()
                dve.tensor_copy(piece[:, n, :], wgt[:, :])
                if n < PIECES - 1:
                    dve.drain()
                    dve.tensor_tensor(wgt[:, :], wgt[:, :], piece[:, n, :], ALU.subtract)
            dve.wait_ge(consts_ready, 1)

            count_bins(0)
            keys(1)
            find_places(0)
            make_records(0)
            keys(2)
            make_list(0, 0)
            count_bins(1)
            find_places(1)
            keys(3)
            make_records(1)
            keys(4)
            make_list(1, 1)
            dve.wait_ge(kv_summed, TURNS)
            for m in range(KC):
                dve.tensor_scalar(KV[:, m, 0:P], bank[5 + m][:, 0:P], 1.0 / N, None, ALU.mult)
                dve.tensor_copy(KV[:, m, P:P + 1], bank[5 + m][:, P:P + 1])
            dve.drain()
            for a in range(HPC):
                own = slice(a * HD, (a + 1) * HD)
                dve.tensor_copy(KVd[own, :, a * HD:(a + 1) * HD], KV[own, :, a * HD:(a + 1) * HD])
                dve.tensor_copy(KVd[own, :, P + a:P + a + 1], KV[own, :, P:P + 1])
            dve.drain().then_inc(kvd_ready, 1)

            dve.wait_ge(consts_ready, 1)
            dve.wait_ge(xn_stored, 32)
            dve.wait_ge(ring_tok, ready(NT - 1))
            make_hot(0)
            with dve.Fori(0, (NG - 3) // 2) as i:
                for h in range(2):
                    add_up(2 * i + h, h, True)
            add_up(NG - 3, 0, True)
            add_up(NG - 2, 1, False)
            add_up(NG - 1, 0, False, more=False)

            def queries(i):
                for j in range(U + 2):
                    if j < U:
                        dve.wait_ge(ring_q, ready(i * U + j))
                        dve.nop(nofuse=True)
                        dve.tensor_scalar(neg[:, j, :], bank[j][:, 0:C], 0.0, None, ALU.min).then_inc(ring_qneg, 1)
                    if j >= 2:
                        t = j - 2
                        dve.wait_ge(ring_qexp, ready(i * U + t))
                        dve.nop(nofuse=True)
                        dve.scalar_tensor_tensor(wide[:, t, 0:C], bank[t][:, 0:C], 0.0, neg[:, t, :], ALU.max, ALU.add).then_inc(ring_qelu, 1)

            def messages(i):
                for j in range(U + 2):
                    if j >= 2:
                        t = j - 2
                        both = bank[t][:, 0:KC * (P + HPC)].rearrange("p (m c) -> p m c", m=KC)
                        for m in range(KC):
                            last = dve.scalar_tensor_tensor(
                                tok[:, t, m * P:(m + 1) * P].rearrange("p (a d) -> p a d", a=HPC),
                                both[:, m, 0:P].rearrange("p (a d) -> p a d", a=HPC), float(N),
                                tiny[:, 1, (t % 2) * KC * HPC + m * HPC:(t % 2) * KC * HPC + (m + 1) * HPC].unsqueeze(2)
                                .to_broadcast([P, HPC, HD]), ALU.mult, ALU.mult)
                        last.then_inc(ring_msg, 1)
                    if 1 <= j < U + 1:
                        t = j - 1
                        zs = slice((t % 2) * KC * HPC, (t % 2 + 1) * KC * HPC)
                        dve.reciprocal(tiny[:, 1, zs], tiny[:, 0, zs])
                    if j < U:
                        dve.wait_ge(ring_att, ready(i * U + j))
                        dve.nop(nofuse=True)
                        both = bank[j][:, 0:KC * (P + HPC)].rearrange("p (m c) -> p m c", m=KC)
                        z = tiny[:, 0, (j % 2) * KC * HPC:(j % 2 + 1) * KC * HPC].rearrange("p (m a) -> p m a", m=KC)
                        dve.tensor_scalar(z, both[:, :, P:P + HPC], ATT_EPS, None, ALU.add)
                    dve.drain()

            def layer_norm(n, i, produced, source, result):
                for j in range(U + 2):
                    if j < U:
                        if produced is not None:
                            dve.wait_ge(produced, ready(i * U + j))
                            dve.nop(nofuse=True)
                        dve.bn_stats(stat[:, n, j, 0:6], source(j))
                    if 1 <= j < U + 1:
                        dve.wait_ge(ring_std[n], ready(i * U + j - 1))
                        dve.nop(nofuse=True)
                        dve.reciprocal(stat[:, n, j - 1, 9:10], stat[:, n, j - 1, 8:9])
                    if j == U + 1 and n != 1:
                        break
                    dve.drain()
                    if j < U:
                        dve.bn_aggr(stat[:, n, j, 6:8], stat[:, n, j, 0:6]).then_inc(ring_var[n], 1)
                    result(j)

            def plain(n, source, to, done, wait=None):
                def result(j):
                    t = j - 1
                    if 0 <= t < U:
                        if wait is not None:
                            wait(t)
                        dve.tensor_scalar(to[:, t, :], source(t), stat[:, n, t, 6:7], stat[:, n, t, 9:10], ALU.subtract, ALU.mult)\
                            .then_inc(done, 1)
                return result

            def residual(i):
                def result(j):
                    if 1 <= j < U + 1:
                        t = j - 1
                        dve.scalar_tensor_tensor(tok[:, t, :], bank[t][:, 0:C], stat[:, 1, t, 6:7], g2r[:, :], ALU.subtract, ALU.mult)\
                            .then_inc(ring_h2_read, 1)
                    if j >= 2:
                        t = j - 2
                        dve.wait_ge(x_base, i * U + t + 1)
                        dve.nop(nofuse=True)
                        dve.scalar_tensor_tensor(tile_of(xn, i, t), tok[:, t, :], stat[:, 1, t, 9:10], x_again[:, t, :], ALU.mult, ALU.add)\
                            .then_inc(ring_x1, 1)
                return result

            def last_norm_and_gate(i):
                def kept(t):
                    if t == 0:
                        dve.wait_ge(n3_stored, 16 * i + 16)
                        dve.nop(nofuse=True)

                x1 = lambda j: tile_of(xn, i, j)
                layer_norm(2, i, None, x1, plain(2, x1, n3, ring_n3, kept))
                dve.wait_ge(ring_gate, i + 1)
                dve.nop(nofuse=True)
                dve.tensor_tensor(logits[:, :, :].rearrange("p (a b) e -> p a b e", b=U)[:, bass.ds(i, 1), :, :]
                                  .rearrange("p a b e -> p (a b) e"),
                                  bank[7][:, 0:U * NE].rearrange("p (b e) -> p b e", b=U),
                                  gate_row[:, :].unsqueeze(1).to_broadcast([P, U, NE]), ALU.add).then_inc(logits_made, 1)

            def dense(i, past):
                in_bank = lambda j: bank[j][:, 0:C]
                queries(i)
                messages(i)
                layer_norm(0, i, ring_mm, in_bank, plain(0, in_bank, tok, ring_n1))
                if past is not None:
                    last_norm_and_gate(past)
                layer_norm(1, i, ring_h2, in_bank, residual(i))

            dense(0, None)
            with dve.Fori(1, TURNS) as i:
                dense(i, i - 1)
            dve.drain()
            last_norm_and_gate(TURNS - 1)

            dve.drain()
            top = routing(NT)
            hot1, hot2 = routing(NT, NE), routing(NT, NE)
            cand = routing(NT, NE)
            pick, first, total = routing(NT), routing(NT), routing(NT)
            iota_e = iota[:, 0:NE].unsqueeze(1).to_broadcast([P, NT, NE])

            def wide_of(a):
                return a.unsqueeze(2).to_broadcast([P, NT, NE])

            dve.tensor_reduce(top, logits[:, :, :], AX, ALU.max)
            dve.drain()
            dve.tensor_tensor(logits[:, :, :], logits[:, :, :], wide_of(top), ALU.subtract).then_inc(logits_neg, 1)
            dve.wait_ge(exp_ready, 1)
            dve.tensor_reduce(total, logits[:, :, :], AX, ALU.add)
            dve.drain()
            dve.reciprocal(total, total)
            dve.drain()
            dve.tensor_tensor(logits[:, :, :], logits[:, :, :], wide_of(total), ALU.mult)
            dve.drain()
            for c, chosen in ((0, hot1), (1, hot2)):
                dve.tensor_reduce(gates[:, c, :], logits[:, :, :], AX, ALU.max)
                dve.drain()
                dve.tensor_tensor(cand, logits[:, :, :], wide_of(gates[:, c, :]), ALU.not_equal)
                dve.drain()
                dve.scalar_tensor_tensor(cand, cand, float(NE), iota_e, ALU.mult, ALU.add)
                dve.drain()
                dve.tensor_reduce(pick, cand, AX, ALU.min)
                dve.drain()
                dve.tensor_tensor(chosen, iota_e, wide_of(pick), ALU.is_equal)
                dve.drain()
                if c == 0:
                    dve.scalar_tensor_tensor(logits[:, :, :], hot1, -2.0, logits[:, :, :], ALU.mult, ALU.add)
                    dve.drain()
            dve.tensor_tensor(total, gates[:, 0, :], gates[:, 1, :], ALU.add)
            dve.drain()
            dve.reciprocal(total, total)
            dve.drain()
            for c in range(2):
                dve.tensor_tensor(gates[:, c, :], gates[:, c, :], total, ALU.mult)
            taken = routing(NE, NT)
            run = routing(1 + NE * NT)
            by_expert = "p t e -> p e t"
            dve.tensor_tensor(cand, hot1, hot2, ALU.add)
            dve.drain()
            dve.tensor_tensor(taken, cand.rearrange(by_expert), valid[:, :].unsqueeze(1).to_broadcast([P, NE, NT]), ALU.mult)
            dve.memset(run[:, 0:1], 0.0)
            dve.drain()
            flat = taken.rearrange("p e t -> p (e t)")
            dve.tensor_tensor_scan(run[:, 1:1 + NE * NT], flat, flat, 0.0, ALU.add, ALU.max)
            dve.drain()
            begin = run[:, 0:NE * NT].rearrange("p (e t) -> p e t", t=NT)[:, :, 0]
            end = run[:, 1:1 + NE * NT].rearrange("p (e t) -> p e t", t=NT)[:, :, NT - 1]
            dve.tensor_tensor(tiny[:, 0, 0:NE], end, begin, ALU.subtract).then_inc(choice_counts, 1)
            dve.wait_ge(choice_prefix, 1)
            tiles_i = routing(NE, dt=I32)
            dve.tensor_scalar(tiles_i, bank[7][:, 32:32 + NE], float(P - 1), None, ALU.add)
            dve.drain()
            dve.tensor_scalar(tiles_i, tiles_i, 7, None, ALU.arith_shift_right)
            dve.drain()
            dve.tensor_copy(tiny[:, 1, 0:NE], tiles_i)
            dve.drain()
            dve.tensor_tensor_scan(tiny[:, 2, 0:NE], tiny[:, 1, 0:NE], tiny[:, 1, 0:NE], 0.0, ALU.add, ALU.max)
            dve.drain()
            dve.tensor_tensor(tiny[:, 3, 0:NE], tiny[:, 2, 0:NE], tiny[:, 1, 0:NE], ALU.subtract)
            dve.drain()
            dve.scalar_tensor_tensor(tiny[:, 3, 0:NE], tiny[:, 3, 0:NE], float(P), begin, ALU.mult, ALU.subtract)
            dve.drain()
            dve.tensor_tensor(tiny[:, 3, 0:NE], bank[7][:, 0:NE], tiny[:, 3, 0:NE], ALU.add)
            dve.drain()
            spot = run[:, 0:NE * NT].rearrange("p (e t) -> p e t", t=NT)
            dve.tensor_tensor(spot, spot, tiny[:, 3, 0:NE].unsqueeze(2).to_broadcast([P, NE, NT]), ALU.add)
            dve.drain()
            for c, chosen in ((0, hot1), (1, hot2)):
                dve.tensor_tensor(taken, spot, chosen.rearrange(by_expert), ALU.mult)
                dve.drain()
                dve.tensor_reduce(first, taken.rearrange("p e t -> p t e"), AX, ALU.add)
                dve.drain()
                dve.tensor_copy(slots[:, c, :], first)
                dve.drain()
            over = routing(ETILES, NE)
            dve.tensor_tensor(over[0:1], tiny[0:1, 2, 0:NE].unsqueeze(1).to_broadcast([1, ETILES, NE]),
                              iota[0:1, 0:ETILES].unsqueeze(2).to_broadcast([1, ETILES, NE]), ALU.is_le)
            dve.drain()
            last_of = routing(ETILES)
            dve.tensor_reduce(last_of[0:1], over[0:1], AX, ALU.add)
            dve.drain()
            dve.tensor_scalar(last_of[0:1], last_of[0:1], float(NE - 1), None, ALU.min)
            dve.drain()
            dve.tensor_copy(owner[:, :], last_of[0:1])
            dve.drain().then_inc(slots_ready, 1)

            dve.tensor_scalar(slot_parts[:, 0, :, :], slots[:, :, :], P - 1, None, ALU.bitwise_and)
            dve.tensor_scalar(slot_parts[:, 1, :, :], slots[:, :, :], 7, None, ALU.arith_shift_right)
            dve.drain()
            for part, to, n, done in ((1, in_etile, ETILES, etiles_made), (0, in_place, P, places_made)):
                for c in range(2):
                    dve.tensor_tensor(to[:, c, :, :], slot_parts[:, part, c, :].unsqueeze(2).to_broadcast([P, NT, n]),
                                      iota[:, 0:n].unsqueeze(1).to_broadcast([P, NT, n]), ALU.is_equal).then_inc(done, 1)
            dve.wait_ge(tokens_summed, 1)
            dve.tensor_copy(token_tile[:, :], bank[6][:, ETILES:2 * ETILES])
            dve.drain()
            dve.scalar_tensor_tensor(token_of[:, :], token_tile[:, :], float(P), bank[6][:, 0:ETILES], ALU.mult, ALU.add)
            dve.drain().then_inc(tokens_ready, 1)

            def dense_of(a, i, n):
                return a[:, 0:NT - 1, :].rearrange("p (a b) c -> p a b c", b=DT)[:, bass.ds(i, 1), n, :].rearrange("p a c -> p (a c)")

            def e_feature(n, h):
                dve.wait_ge(e_turned, n + 3)
                dve.wait_ge(e_h2, n + 1)
                dve.nop(nofuse=True)
                dve.tensor_copy(e_xT[:, h, :], bank[4 + h][:, 0:C]).then_inc(e_feat, 1)

            def e_gated(n, h):
                dve.wait_ge(e_silu, n + 3)
                dve.wait_ge(e_h2, n + 3)
                dve.wait_ge(e_out, n + 1)
                dve.nop(nofuse=True)
                dve.tensor_tensor(e_hid[:, h, :], bank[2 + h][:, :], e_act[:, h, :], ALU.mult).then_inc(e_hidden, 1)

            def e_result(n, n_half, h):
                dve.wait_ge(e_out, n + 3)
                if n_half is not None:
                    dve.wait_ge(e_stored[h], 16 * n_half)
                dve.nop(nofuse=True)
                dve.tensor_copy(e_y[:, h, :], bank[6 + h][:, 0:C]).then_inc(e_out_sb, 1)

            e_feature(0, 0)
            e_gated(0, 0)
            e_feature(1, 1)
            for h in range(2):
                e_gated(h + 1, 1 - h)
                e_feature(h + 2, h)
                e_result(h, None, h)
            with dve.Fori(1, ETILES // 2 - 1) as i:
                for h in range(2):
                    e_gated(2 * i + h + 1, 1 - h)
                    e_feature(2 * i + h + 2, h)
                    e_result(2 * i + h, i, h)
            e_gated(ETILES - 1, 1)
            e_result(ETILES - 2, ETILES // 2 - 1, 0)
            e_result(ETILES - 1, ETILES // 2 - 1, 1)

            def combine(n, rows_n, x1, g_1, g_2):
                dve.scalar_tensor_tensor(c_out[0:rows_n, n, :], c_y1[0:rows_n, n, :], g_1, x1, ALU.mult, ALU.add)
                dve.drain()
                dve.scalar_tensor_tensor(c_out[0:rows_n, n, :], c_y2[0:rows_n, n, :], g_2, c_out[0:rows_n, n, :], ALU.mult, ALU.add)\
                    .then_inc(y_summed, 1)

            def gate_of(c, i, n):
                return gates[:, c, 0:NT - 1].rearrange("p (a b) -> p a b", b=DT)[:, bass.ds(i, 1), n]

            with dve.Fori(0, (NT - 1) // DT) as i:
                for n in range(DT):
                    dve.wait_ge(y_gathered[n], 32 * i + 32)
                    dve.wait_ge(y_stored[n], 16 * i + 16)
                    dve.nop(nofuse=True)
                    combine(n, P, dense_of(xn, i, n), gate_of(0, i, n), gate_of(1, i, n))
            dve.wait_ge(y_gathered[0], 32 * ((NT - 1) // DT) + 32)
            dve.wait_ge(y_stored[0], 16 * (NT - 1) // DT + 16)
            combine(0, LAST, xn[0:LAST, NT - 1, :], gates[0:LAST, 0, NT - 1:NT], gates[0:LAST, 1, NT - 1:NT])


_INS = ['x', 'src', 'dst', 'edge_weight', 'L0_gnn_W', 'L0_gnn_b', 'L0_mix_Wq', 'L0_mix_Wk', 'L0_mix_Wv', 'L0_mix_Wm',
        'L0_mix_W1', 'L0_mix_W2', 'L0_mix_g1', 'L0_mix_b1', 'L0_mix_g2', 'L0_mix_b2', 'L0_ffn_gate_w', 'L0_ffn_gate_b',
        'L0_ffn_w1', 'L0_ffn_w2', 'L0_ffn_w3']
_OUTS = [((3125, 256), 'float32')]


def kernel(**inputs):
    import numpy as _np
    import concourse.bacc as _bacc
    from concourse import mybir as _mybir
    from concourse.bass_utils import run_bass_kernel_spmd as _run

    nc = _bacc.Bacc("TRN2", target_bir_lowering=False, num_devices=1)
    arrays, args = {}, []
    for name in _INS:
        a = _np.ascontiguousarray(inputs[name])
        arrays[f"in_{name}_dram"] = a
        args.append(nc.dram_tensor(f"in_{name}_dram", a.shape, _mybir.dt.from_np(a.dtype), kind="ExternalInput").ap())
    for i, (shape, dtype) in enumerate(_OUTS):
        dt = _mybir.dt.from_np(_np.dtype(dtype))
        args.append(nc.dram_tensor(f"out_{i}_dram", shape, dt, kind="ExternalOutput").ap())
    gps_layer(nc, *args)
    r = _run(nc, [arrays], core_ids=[0])
    return r.results[0]["out_0_dram"]
```
